# Optimizing a Trainium2 kernel written in Bass

```python
import numpy as np
import jax
import jax.numpy as jnp

def _softmax(x, axis=-1):
    return jax.nn.softmax(x, axis=axis)

def _gelu(x):
    return jax.nn.gelu(x, approximate=True)

def _silu(x):
    return jax.nn.silu(x)

def _sigmoid(x):
    return jax.nn.sigmoid(x)

def _layernorm(x, axis=-1, eps=1e-05):
    m = jnp.mean(x, axis=axis, keepdims=True)
    v = jnp.var(x, axis=axis, keepdims=True)
    return (x - m) / jnp.sqrt(v + eps)

def _scatter_add(tgt, idx, src, axis=0):
    return tgt.at[idx].add(src)

def _segment_sum(src, seg, n):
    return jax.ops.segment_sum(src, seg, n)
kernel_name = 'mk_macaron_d2_jaxref_r8_26ffb4'

def setup_inputs(seed: int=0):
    np.random.seed(seed)
    _w = jnp.asarray

    def _L0_attn_setup():
        import jax, jax.numpy as jnp
        import numpy as np
        D = 128

        def _layernorm(x, gamma, beta, eps=1e-05):
            mu = jnp.mean(x, axis=-1, keepdims=True)
            var = jnp.var(x, axis=-1, keepdims=True)
            return (x - mu) * jax.lax.rsqrt(var + eps) * gamma + beta
        key = jax.random.key(seed)
        ks = jax.random.split(key, 8)
        B, S = (4, 512)
        hidden_states = jax.random.normal(ks[0], (B, S, D), dtype=jnp.float32)
        attention_mask = jnp.ones((B, S), dtype=jnp.int32)
        scale = 0.02
        Wq = jax.random.normal(ks[1], (D, D), jnp.float32) * scale
        bq = jnp.zeros((D,), jnp.float32)
        Wk = jax.random.normal(ks[2], (D, D), jnp.float32) * scale
        bk = jnp.zeros((D,), jnp.float32)
        Wv = jax.random.normal(ks[3], (D, D), jnp.float32) * scale
        bv = jnp.zeros((D,), jnp.float32)
        Wqa = jnp.zeros((D, D), jnp.float32)
        bqa = jnp.ones((D,), jnp.float32)
        Wka = jnp.zeros((D, D), jnp.float32)
        bka = jnp.ones((D,), jnp.float32)
        gamma = jnp.ones((D,), jnp.float32)
        beta = jnp.zeros((D,), jnp.float32)
        return {'hidden_states': hidden_states, 'attention_mask': attention_mask, 'Wq': Wq, 'bq': bq, 'Wqa': Wqa, 'bqa': bqa, 'Wk': Wk, 'bk': bk, 'Wka': Wka, 'bka': bka, 'Wv': Wv, 'bv': bv, 'gamma': gamma, 'beta': beta}
    _L0_attn_in = _L0_attn_setup()

    def _L0_ffn_setup():
        import jax, jax.numpy as jnp
        import numpy as np
        HIDDEN = 128
        MOE_FF = 64
        SHARED_FF = 352
        NUM_EXPERTS = 16
        TOP_K = 2
        NORM_TOPK = True
        key = jax.random.key(seed)
        ks = jax.random.split(key, 8)
        s = 0.02
        return {'layer_input': jax.random.normal(ks[0], (1, 256, HIDDEN), dtype=jnp.float32), 'gate_w': jax.random.normal(ks[1], (NUM_EXPERTS, HIDDEN), dtype=jnp.float32) * s, 'w_gate_up': jax.random.normal(ks[2], (NUM_EXPERTS, HIDDEN, 2 * MOE_FF), dtype=jnp.float32) * s, 'w_down': jax.random.normal(ks[3], (NUM_EXPERTS, MOE_FF, HIDDEN), dtype=jnp.float32) * s, 'shared_w_gate': jax.random.normal(ks[4], (SHARED_FF, HIDDEN), dtype=jnp.float32) * s, 'shared_w_up': jax.random.normal(ks[5], (SHARED_FF, HIDDEN), dtype=jnp.float32) * s, 'shared_w_down': jax.random.normal(ks[6], (HIDDEN, SHARED_FF), dtype=jnp.float32) * s, 'shared_gate_w': jax.random.normal(ks[7], (1, HIDDEN), dtype=jnp.float32) * s}
    _L0_ffn_in = _L0_ffn_setup()

    def _L1_attn_setup():
        import jax, jax.numpy as jnp
        import numpy as np
        D_MODEL = 128
        B, S = (4, 256)
        key = jax.random.key(seed)
        k1, k2, k3 = jax.random.split(key, 3)
        scale = 1.0 / np.sqrt(D_MODEL)
        x = jax.random.normal(k1, (B, S, D_MODEL), dtype=jnp.float32)
        Wq = jax.random.normal(k2, (D_MODEL, D_MODEL), dtype=jnp.float32) * scale
        bq = jnp.zeros((D_MODEL,), dtype=jnp.float32)
        Wk = jax.random.normal(k3, (D_MODEL, D_MODEL), dtype=jnp.float32) * scale
        bk = jnp.zeros((D_MODEL,), dtype=jnp.float32)
        return {'x': x, 'Wq': Wq, 'bq': bq, 'Wk': Wk, 'bk': bk}
    _L1_attn_in = _L1_attn_setup()

    def _L1_ffn_setup():
        import jax, jax.numpy as jnp
        import numpy as np
        NUM_EXPERTS = 8
        TOP_K = 2
        key = jax.random.key(seed)
        ks = jax.random.split(key, 9)
        B, S, D, H, R, E = (4, 256, 128, 512, 64, NUM_EXPERTS)
        s = lambda fan_in: 1.0 / np.sqrt(fan_in)
        return {'x': jax.random.normal(ks[0], (B, S, D), dtype=jnp.float32), 'Wr1': jax.random.normal(ks[1], (R, D), dtype=jnp.float32) * s(D), 'br1': jax.random.normal(ks[2], (R,), dtype=jnp.float32) * s(D), 'Wr2': jax.random.normal(ks[3], (E, R), dtype=jnp.float32) * s(R), 'br2': jax.random.normal(ks[4], (E,), dtype=jnp.float32) * s(R), 'W1': jax.random.normal(ks[5], (E, H, D), dtype=jnp.float32) * s(D), 'b1': jax.random.normal(ks[6], (E, H), dtype=jnp.float32) * s(D), 'W2': jax.random.normal(ks[7], (E, D, H), dtype=jnp.float32) * s(H), 'b2': jax.random.normal(ks[8], (E, D), dtype=jnp.float32) * s(H)}
    _L1_ffn_in = _L1_ffn_setup()
    _d = {'L0_attn_hidden_states': _L0_attn_in['hidden_states'], 'L0_attn_attention_mask': _L0_attn_in['attention_mask'], 'L0_attn_Wq': _L0_attn_in['Wq'], 'L0_attn_bq': _L0_attn_in['bq'], 'L0_attn_Wqa': _L0_attn_in['Wqa'], 'L0_attn_bqa': _L0_attn_in['bqa'], 'L0_attn_Wk': _L0_attn_in['Wk'], 'L0_attn_bk': _L0_attn_in['bk'], 'L0_attn_Wka': _L0_attn_in['Wka'], 'L0_attn_bka': _L0_attn_in['bka'], 'L0_attn_Wv': _L0_attn_in['Wv'], 'L0_attn_bv': _L0_attn_in['bv'], 'L0_attn_gamma': _L0_attn_in['gamma'], 'L0_attn_beta': _L0_attn_in['beta'], 'L0_ffn_gate_w': _L0_ffn_in['gate_w'], 'L0_ffn_w_gate_up': _L0_ffn_in['w_gate_up'], 'L0_ffn_w_down': _L0_ffn_in['w_down'], 'L0_ffn_shared_w_gate': _L0_ffn_in['shared_w_gate'], 'L0_ffn_shared_w_up': _L0_ffn_in['shared_w_up'], 'L0_ffn_shared_w_down': _L0_ffn_in['shared_w_down'], 'L0_ffn_shared_gate_w': _L0_ffn_in['shared_gate_w'], 'L1_attn_Wq': _L1_attn_in['Wq'], 'L1_attn_bq': _L1_attn_in['bq'], 'L1_attn_Wk': _L1_attn_in['Wk'], 'L1_attn_bk': _L1_attn_in['bk'], 'L1_ffn_Wr1': _L1_ffn_in['Wr1'], 'L1_ffn_br1': _L1_ffn_in['br1'], 'L1_ffn_Wr2': _L1_ffn_in['Wr2'], 'L1_ffn_br2': _L1_ffn_in['br2'], 'L1_ffn_W1': _L1_ffn_in['W1'], 'L1_ffn_b1': _L1_ffn_in['b1'], 'L1_ffn_W2': _L1_ffn_in['W2'], 'L1_ffn_b2': _L1_ffn_in['b2']}
    _x0 = _d['L0_attn_hidden_states']
    _d['L0_attn_hidden_states'] = jax.random.normal(jax.random.fold_in(jax.random.key(seed), 1), (16, 256, 128), dtype=_x0.dtype)
    del _x0
    return _d

def reference(L0_attn_hidden_states, L0_attn_attention_mask, L0_attn_Wq, L0_attn_bq, L0_attn_Wqa, L0_attn_bqa, L0_attn_Wk, L0_attn_bk, L0_attn_Wka, L0_attn_bka, L0_attn_Wv, L0_attn_bv, L0_attn_gamma, L0_attn_beta, L0_ffn_gate_w, L0_ffn_w_gate_up, L0_ffn_w_down, L0_ffn_shared_w_gate, L0_ffn_shared_w_up, L0_ffn_shared_w_down, L0_ffn_shared_gate_w, L1_attn_Wq, L1_attn_bq, L1_attn_Wk, L1_attn_bk, L1_ffn_Wr1, L1_ffn_br1, L1_ffn_Wr2, L1_ffn_br2, L1_ffn_W1, L1_ffn_b1, L1_ffn_W2, L1_ffn_b2):

    def _L0_attn_ref(hidden_states, attention_mask, Wq, bq, Wqa, bqa, Wk, bk, Wka, bka, Wv, bv, gamma, beta):
        import jax, jax.numpy as jnp
        import numpy as np
        D = 128

        def _layernorm(x, gamma, beta, eps=1e-05):
            mu = jnp.mean(x, axis=-1, keepdims=True)
            var = jnp.var(x, axis=-1, keepdims=True)
            return (x - mu) * jax.lax.rsqrt(var + eps) * gamma + beta
        h = _layernorm(hidden_states, gamma, beta)
        B, S, d_model = h.shape
        inv_sqrt_d = 1.0 / jnp.sqrt(jnp.float32(d_model))
        query = h @ Wq + bq
        keys = h @ Wk + bk
        values = h @ Wv + bv
        scaling = jnp.arange(1, S + 1, dtype=h.dtype).reshape(1, S, 1)
        query_weight = jax.nn.softmax((query @ Wqa + bqa) * inv_sqrt_d, axis=-1)
        pooled_query = jnp.cumsum(query_weight * query, axis=1) / scaling
        mixed_keys = pooled_query * keys
        keys_weight = jax.nn.softmax((mixed_keys @ Wka + bka) * inv_sqrt_d, axis=-1)
        pooled_keys = jnp.cumsum(keys_weight * mixed_keys, axis=1) / scaling
        return pooled_keys * values

    def _L0_ffn_ref(layer_input, gate_w, w_gate_up, w_down, shared_w_gate, shared_w_up, shared_w_down, shared_gate_w):
        import jax, jax.numpy as jnp
        import numpy as np
        HIDDEN = 128
        MOE_FF = 64
        SHARED_FF = 352
        NUM_EXPERTS = 16
        TOP_K = 2
        NORM_TOPK = True
        B, S, D = layer_input.shape
        x = layer_input.reshape(-1, D)
        N = x.shape[0]
        shared = jax.nn.silu(x @ shared_w_gate.T) * (x @ shared_w_up.T) @ shared_w_down.T
        shared = shared * jax.nn.sigmoid(x @ shared_gate_w.T)
        logits = x @ gate_w.T
        probs = jax.nn.softmax(logits.astype(jnp.float32), axis=-1)
        rw, sel = jax.lax.top_k(probs, TOP_K)
        if NORM_TOPK:
            rw = rw / rw.sum(axis=-1, keepdims=True)
        rw = rw.astype(x.dtype)
        combine = jnp.zeros((N, NUM_EXPERTS), x.dtype).at[jnp.arange(N)[:, None], sel].set(rw)
        gu = jnp.einsum('nd,edf->nef', x, w_gate_up)
        g, h = jnp.split(gu, 2, axis=-1)
        h = jax.nn.silu(g) * h
        expert_out = jnp.einsum('nef,efd,ne->nd', h, w_down, combine)
        out = expert_out + shared
        return out.reshape(B, S, D)

    def _L1_attn_ref(x, Wq, bq, Wk, bk):
        import jax, jax.numpy as jnp
        import numpy as np
        D_MODEL = 128
        B, S = (4, 256)
        gamma_1 = 1.0
        gamma_2 = 1.0
        d_model = x.shape[-1]
        q = jnp.einsum('bsd,ed->bse', x, Wq) + bq
        k = jnp.einsum('bsd,ed->bse', x, Wk) + bk
        attn = jnp.einsum('bse,bte->bst', q, k) / np.sqrt(d_model)
        attn = jax.nn.softmax(attn, axis=-1)
        S_len = x.shape[1]
        eye = jnp.eye(S_len, dtype=x.dtype)
        attn = gamma_1 * eye[None, :, :] + attn
        mean = jnp.mean(attn, axis=-1, keepdims=True)
        attn = attn - gamma_2 * mean
        return jnp.einsum('bst,btd->bsd', attn, x)

    def _L1_ffn_ref(x, Wr1, br1, Wr2, br2, W1, b1, W2, b2):
        import jax, jax.numpy as jnp
        import numpy as np
        NUM_EXPERTS = 8
        TOP_K = 2
        B, S, D = x.shape
        E = Wr2.shape[0]
        xf = x.reshape(-1, D)
        h = jax.nn.gelu(xf @ Wr1.T + br1, approximate=False)
        probs = jax.nn.softmax(h @ Wr2.T + br2, axis=-1)
        w, idx = jax.lax.top_k(probs, TOP_K)
        comb = jnp.sum(jax.nn.one_hot(idx, E, dtype=xf.dtype) * w[..., None], axis=1)
        out = jnp.zeros_like(xf)
        for e in range(E):
            he = jax.nn.gelu(xf @ W1[e].T + b1[e], approximate=False)
            ye = he @ W2[e].T + b2[e]
            out = out + comb[:, e:e + 1] * ye
        return out.reshape(B, S, D)
    x = L0_attn_hidden_states
    x = x + 0.5 * _L0_ffn_ref(_layernorm(x, axis=-1), L0_ffn_gate_w, L0_ffn_w_gate_up, L0_ffn_w_down, L0_ffn_shared_w_gate, L0_ffn_shared_w_up, L0_ffn_shared_w_down, L0_ffn_shared_gate_w)
    x = x + _L0_attn_ref(_layernorm(x, axis=-1), L0_attn_attention_mask, L0_attn_Wq, L0_attn_bq, L0_attn_Wqa, L0_attn_bqa, L0_attn_Wk, L0_attn_bk, L0_attn_Wka, L0_attn_bka, L0_attn_Wv, L0_attn_bv, L0_attn_gamma, L0_attn_beta)
    x = x + 0.5 * _L0_ffn_ref(_layernorm(x, axis=-1), L0_ffn_gate_w, L0_ffn_w_gate_up, L0_ffn_w_down, L0_ffn_shared_w_gate, L0_ffn_shared_w_up, L0_ffn_shared_w_down, L0_ffn_shared_gate_w)
    x = x + 0.5 * _L1_ffn_ref(_layernorm(x, axis=-1), L1_ffn_Wr1, L1_ffn_br1, L1_ffn_Wr2, L1_ffn_br2, L1_ffn_W1, L1_ffn_b1, L1_ffn_W2, L1_ffn_b2)
    x = x + _L1_attn_ref(_layernorm(x, axis=-1), L1_attn_Wq, L1_attn_bq, L1_attn_Wk, L1_attn_bk)
    x = x + 0.5 * _L1_ffn_ref(_layernorm(x, axis=-1), L1_ffn_Wr1, L1_ffn_br1, L1_ffn_Wr2, L1_ffn_br2, L1_ffn_W1, L1_ffn_b1, L1_ffn_W2, L1_ffn_b2)
    return x

_drawn_inputs = setup_inputs


def setup_inputs(seed=0):
    import zlib

    import numpy as np

    out = dict(_drawn_inputs(seed))
    spreads = {'L0_attn_bq': (0.0, 2.0),
     'L0_attn_Wqa': (0.0, 2.0),
     'L0_attn_bqa': (1.0, 0.6),
     'L0_attn_bk': (0.0, 2.0),
     'L0_attn_Wka': (0.0, 2.0),
     'L0_attn_bka': (1.0, 0.6),
     'L0_attn_bv': (0.0, 2.0),
     'L0_attn_gamma': (1.0, 0.6),
     'L0_attn_beta': (0.0, 2.0),
     'L1_attn_bq': (0.0, 2.0),
     'L1_attn_bk': (0.0, 2.0)}
    factors = {'L0_attn_Wq': 64.0,
     'L0_attn_Wk': 64.0,
     'L0_attn_Wv': 64.0,
     'L0_ffn_gate_w': 8.0,
     'L0_ffn_w_gate_up': 8.0,
     'L0_ffn_w_down': 8.0,
     'L0_ffn_shared_w_gate': 7.542,
     'L0_ffn_shared_w_up': 6.702,
     'L0_ffn_shared_w_down': 7.345,
     'L0_ffn_shared_gate_w': 8.0,
     'L1_ffn_b1': 19.354,
     'L1_ffn_b2': 28.564,
     'L1_ffn_br1': 14.288,
     'L1_ffn_br2': 4.94}
    for name, (base, spread) in spreads.items():
        noise = np.random.default_rng([zlib.crc32(name.encode()), seed]).standard_normal(out[name].shape)
        drawn = base * np.exp(spread * noise) if base else spread * noise
        out[name] = jnp.asarray(drawn.astype(out[name].dtype))
    for name, factor in factors.items():
        out[name] = (out[name] * factor).astype(out[name].dtype)
    return out
```

```python
from contextlib import ExitStack

import concourse.bass as bass
from concourse import mybir

ALU = mybir.AluOpType
ACT = mybir.ActivationFunctionType
F32 = mybir.dt.float32
F32R = mybir.dt.float32r
AX_X = mybir.AxisListType.X

P = 128
D = 128
TILES = 4
GTOK = TILES * P
SEQ = 256
GROUPS = 8
E0, F0 = 16, 64
PAIRS = E0 // 2
SHARED = 352
SH_ROWS = [128, 128, 96]
N0 = PAIRS + len(SH_ROWS)
E1, H1 = 8, 512
CH1 = H1 // P
N1 = E1 * CH1
RING = 4
LO = 32
HI_BY_ACT = (1, 3)
EPS = 1e-5
BIG = 1.0e30
INV = float(D) ** -0.5
C_G, C_H, C_D = 0, E0 * F0, 2 * E0 * F0
C_SG = C_D + PAIRS * D
C_SU, C_SD = C_SG + SHARED, C_SG + 2 * SHARED
W0_COLS = C_SD + len(SH_ROWS) * D
W1_COLS = E1 * H1

SMALL = [
    ("gate0", E0 + 1), ("wr1", 64), ("wr2", E1), ("b1", N1), ("b2", E1), ("br1", 1), ("gamma", 1), ("beta", 1),
    ("bq", 1), ("bk", 1), ("wq", D), ("wqa", D), ("wk", D), ("wka", D), ("wv", D), ("bq_row", D), ("bqa_row", D),
    ("bka_row", D), ("bv_row", D), ("wq1", D), ("wk1", D), ("bq1", 1), ("bk1", 1), ("ident", P), ("tri0", SEQ),
    ("tri1", P), ("tie", TILES * E0), ("sel0", (PAIRS + 1) * P), ("sel1", E1 * P),
]
SMALL_AT = {}
SMALL_COLS = 0
for _n, _w in SMALL:
    SMALL_AT[_n] = (SMALL_COLS, _w)
    SMALL_COLS += _w


def program(nc, x_in, small_in, w0_in, w1_in, w2_in, out):
    x_dram = x_in.rearrange("a (b p) d -> p (a b) d", p=P)
    out_dram = out.rearrange("a (b p) d -> p (a b) d", p=P)
    with ExitStack() as ctx:
        def sb(name, shape, dt=F32):
            return ctx.enter_context(nc.sbuf_tensor(name, shape, dt))

        def sem(name):
            return ctx.enter_context(nc.semaphore(name))

        X = sb("x_sb", [P, GROUPS * TILES, D])
        small = sb("small_sb", [P, SMALL_COLS])
        w0h, w0l = sb("w0h", [P, W0_COLS], F32R), sb("w0l", [P, W0_COLS], F32R)
        w1h, w1l = sb("w1h", [P, W1_COLS], F32R), sb("w1l", [P, W1_COLS], F32R)
        w2h, w2l = sb("w2h", [P, W1_COLS], F32R), sb("w2l", [P, W1_COLS], F32R)
        work = sb("work", [P, 2, RING, GTOK])
        with nc.sbuf_tensor("attn", [P, 2, RING, GTOK], F32) as attn:
            pass
        hi = sb("hi", [P, RING, GTOK], F32R)
        lo = sb("lo", [P, RING, GTOK], F32R)
        sel0r = sb("sel0r", [P, PAIRS + 1, P], F32R)
        sel1r = sb("sel1r", [P, E1, P], F32R)
        xn = sb("xn", [P, 2, TILES, D])
        xT = sb("xT", [P, 2, GTOK])
        xh, xl = sb("xh", [P, 2, GTOK], F32R), sb("xl", [P, 2, GTOK], F32R)
        combT = sb("combT", [64, 2, GTOK], F32R)
        comb_bc = sb("comb_bc", [P, 2, GTOK])
        term = sb("term", [P, 2, GTOK])
        yT = sb("yT", [P, GTOK])
        hr = sb("hr", [65, GTOK])
        st = sb("st", [P, 2, TILES, 6])
        mv = sb("mv", [P, 2, TILES, 2])
        ve = sb("ve", [P, 2, TILES])
        rstd = sb("rstd", [P, 2, TILES])
        mhalf = sb("mhalf", [P, TILES])
        cm = sb("cm", [P, TILES, P], F32R)
        hold = sb("hold", [P, 1])
        rt = sb("rt", [P, 8, TILES * (E0 + 1)])
        mx = sb("mx", [P, 8, TILES])
        rsum = sb("rsum", [P, 2, TILES])
        rinv = sb("rinv", [P, 2, TILES])

        bank = [ctx.enter_context(nc.psum_tensor(f"bank{i}", [P, GTOK], F32)) for i in range(8)]
        GATE, UP = bank[0:2], bank[2:4]
        RINGB = [bank[0], bank[1], bank[2]]
        YB = [bank[3], bank[4]]
        Y0, CB, TB, RB = bank[4], bank[5], bank[6], bank[7]

        def cst(name, rows=P):
            a, w = SMALL_AT[name]
            return small[0:rows, a:a + w]

        ident = cst("ident")

        s_small, s_x0, s_raw = sem("s_small"), sem("s_x_loaded"), sem("s_raw_loaded")
        s_wh, s_wl = sem("s_weights_high"), sem("s_weights_low")
        s_mhalf, s_sel, s_hr1 = sem("s_minus_half"), sem("s_selectors"), sem("s_hr_ones")
        s_out = sem("s_out")
        s_ve, s_rstd, s_xn = sem("s_var_eps"), sem("s_rstd"), sem("s_xn")
        s_T, s_xh, s_xl = sem("s_xn_transposed"), sem("s_xT_high"), sem("s_xT_low")
        s_ct = sem("s_comb_transposed_copied")
        s_yT, s_xo = sem("s_yT"), sem("s_x_updated_by_ffn")
        s_oT = sem("s_out_transposed")
        r0 = {n: sem("s0_" + n) for n in ("chain", "logits", "d", "exp", "comb", "combT")}
        s_up, s_silu, s_t, s_u, s_uh, s_ul, s_dn = (sem("s0_" + n) for n in ("up", "silu", "gated", "scaled", "high", "low", "down"))
        r1 = {n: sem("s1_" + n) for n in ("chain", "hid", "gelu", "logits", "d", "exp", "comb", "combT")}
        s1_up, s1_he, s1_hiA, s1_hiD, s1_lo, s1_Y = (sem("s1_" + n) for n in ("up", "gelu_f", "high_act", "high_dve", "low", "down"))
        s1_cbp, s1_cb, s1_term, s1_acc = (sem("s1_" + n) for n in ("comb_bc_psum", "comb_bc", "term", "acc"))
        A0N = ("chain", "ve1", "rstd1", "ve2", "rstd2", "xn", "T", "hT", "q", "k", "qt", "v", "qT", "kT", "l1", "d1",
               "e1", "wq", "pool", "mixed", "l2", "mixt", "mtok", "d2", "e2", "w2", "pk", "x")
        a0 = {n: sem("a0_" + n) for n in A0N}
        A1N = ("chain", "ve1", "rstd1", "xn", "T", "xT", "q", "k", "qT", "kT", "s", "nmax", "e", "a", "aT", "aTc", "o", "x")
        a1 = {n: sem("a1_" + n) for n in A1N}

        block = ctx.enter_context(nc.Block())

        def tile_of(g, j):
            return X[:, bass.ds(g * TILES + j, 1), :]

        def group_of(g):
            return X[:, bass.ts(g, TILES), :]

        def t4(ap):
            return ap.rearrange("p (j d) -> p j d", j=TILES)

        def over(col, n):
            return col.unsqueeze(2).broadcast_to([P, TILES, n])

        def down_w(w, k):
            if k < PAIRS:
                return w[:, C_D + k * D:C_D + (k + 1) * D]
            s = k - PAIRS
            return w[0:SH_ROWS[s], C_SD + s * D:C_SD + (s + 1) * D]

        def up_w(w, k, gate):
            if k < PAIRS:
                a = (C_G if gate else C_H) + k * P
                return w[:, a:a + P]
            s = k - PAIRS
            a = (C_SG if gate else C_SU) + s * P
            return w[:, a:a + SH_ROWS[s]]

        def rows(k):
            return P if k < PAIRS else SH_ROWS[k - PAIRS]

        class Chain:

            def __init__(self, eng, s, base):
                self.eng, self.s, self.base, self.n = eng, s, base, 0

            def link(self, ins):
                self.n += 1
                ins.then_inc(self.s, 1)
                self.eng.wait_ge(self.s, self.base + self.n)

        def ffn_groups(eng, f, occ, front, back, finish):
            front(8 * f, 8 * occ, 0, 0)
            back(8 * f, 8 * occ, 0, 0, True)
            with eng.Fori(0, GROUPS // 2 - 1) as i:
                for p in (1, 0):
                    g = i * 2 + (2 - p)
                    back(g + 8 * f, g + 8 * occ, g, p, True)
            back(8 * f + GROUPS - 1, 8 * occ + GROUPS - 1, GROUPS - 1, (GROUPS - 1) % 2, False)
            finish(8 * f + GROUPS - 1, 8 * occ + GROUPS - 1, GROUPS - 1)

        @block.sync
        def _(sp):
            sp.dma_start(small[:], small_in).then_inc(s_small, 16)
            sp.dma_start(X[:], x_dram).then_inc(s_x0, 16)
            stage = work[:].rearrange("p a r n -> p (a r n)")
            sp.dma_start(stage[:, 0:4096], w0_in[:, 0:4096]).then_inc(s_raw, 16)
            sp.wait_ge(s_wl, 1)
            sp.dma_start(stage[:, 0:W0_COLS - 4096], w0_in[:, 4096:W0_COLS]).then_inc(s_raw, 16)
            sp.wait_ge(s_wl, 2)
            sp.dma_start(stage[:, 0:W1_COLS], w1_in).then_inc(s_raw, 16)
            sp.wait_ge(s_wl, 3)
            sp.dma_start(stage[:, 0:W1_COLS], w2_in).then_inc(s_raw, 16)
            with sp.Fori(0, GROUPS) as g:
                sp.wait_ge(s_xo, g + 3 * GROUPS + 2)
                sp.dma_start(out_dram[:, bass.ts(g, TILES), :], group_of(g)).then_inc(s_out, 16)
            sp.wait_ge(s_out, 16 * GROUPS)

        WEIGHTS = [(w0h, w0l, 0, 4096), (w0h, w0l, 4096, W0_COLS), (w1h, w1l, 0, W1_COLS), (w2h, w2l, 0, W1_COLS)]

        @block.gpsimd
        def _(pool):
            nc.gpsimd.memset(mhalf[:], -0.5).then_inc(s_mhalf, 1)
            pool.wait_ge(s_mhalf, 1)

            def power(s_in, s_done, n, p):
                pool.wait_ge(s_in, n + 1)
                nc.gpsimd.tensor_tensor(rstd[:, p, :], ve[:, p, :], mhalf[:], ALU.pow).then_inc(s_done, 1)

            def ffn0(m, r, g, p, more):
                for k in range(N0):
                    if k == 1 and more:
                        power(s_ve, s_rstd, m + 1, 1 - p)
                    M = rows(k)
                    pool.wait_ge(s_uh, r * N0 + k + 1)
                    nc.gpsimd.tensor_tensor(lo[0:M, k % RING, :], work[0:M, 1, k % RING, :],
                                            hi[0:M, k % RING, :].bitcast(F32), ALU.subtract).then_inc(s_ul, 1)

            def ffn1(m, r, g, p, more):
                for e in range(E1):
                    if e == 1 and more:
                        power(s_ve, s_rstd, m + 1, 1 - p)
                    if e:
                        pool.wait_ge(s1_term, r * E1 + e + 1)
                        if e > 1:
                            pool.wait_ge(s1_acc, r * (E1 - 1) + e - 1)
                        nc.gpsimd.tensor_tensor(yT[:], yT[:], term[:, e % 2, :], ALU.add).then_inc(s1_acc, 1)

            def front(m, r, g, p):
                power(s_ve, s_rstd, m, p)

            none = lambda *a: None

            def attn(names, s):
                with pool.Fori(0, GROUPS // 2) as i:
                    for a, b in names:
                        for p in (0, 1):
                            power(s[a], s[b], i * 2 + p, p)

            ffn_groups(pool, 0, 0, front, ffn0, none)
            attn([("ve1", "rstd1"), ("ve2", "rstd2")], a0)
            ffn_groups(pool, 1, 1, front, ffn0, none)
            ffn_groups(pool, 2, 0, front, ffn1, none)
            attn([("ve1", "rstd1")], a1)
            ffn_groups(pool, 3, 1, front, ffn1, none)

        @block.scalar
        def _(act):
            A = nc.scalar.activation

            act.wait_ge(s_small, 16)
            A(sel0r[:].rearrange("p a b -> p (a b)"), cst("sel0"), ACT.Copy).then_inc(s_sel, 1)
            A(sel1r[:].rearrange("p a b -> p (a b)"), cst("sel1"), ACT.Copy).then_inc(s_sel, 1)
            stage = work[:].rearrange("p a r n -> p (a r n)")
            for n, (wh, _, a, b) in enumerate(WEIGHTS):
                act.wait_ge(s_raw, 16 * (n + 1))
                A(wh[:, a:b], stage[:, 0:b - a], ACT.Copy).then_inc(s_wh, 1)

            def take_xT(m, p):
                act.wait_ge(s_T, m + 1)
                A(xT[:, p, :], TB[:], ACT.Copy)
                A(xh[:, p, :], TB[:], ACT.Copy).then_inc(s_xh, 1)

            def route_exp(s, r, width):
                act.wait_ge(s["d"], r + 1)
                A(rt[:, 1, 0:TILES * width], rt[:, 0, 0:TILES * width], ACT.Exp).then_inc(s["exp"], 1)

            def take_comb(s, r, p):
                act.wait_ge(s["combT"], r + 1)
                A(combT[:, p, :], RB[0:64, :], ACT.Copy).then_inc(s_ct, 1)

            def hidden(r):
                act.wait_ge(r1["hid"], r + 1)
                A(hr[0:64, :], RB[0:64, :], ACT.Gelu, bias=cst("br1", 64)).then_inc(r1["gelu"], 1)

            def front0(m, r, g, p):
                take_xT(m, p)
                route_exp(r0, r, E0 + 1)
                take_comb(r0, r, p)

            def back0(m, r, g, p, more):
                def high(k):
                    M = rows(k)
                    act.wait_ge(s_u, r * N0 + k + 1)
                    A(hi[0:M, k % RING, :], work[0:M, 1, k % RING, :], ACT.Copy).then_inc(s_uh, 1)

                for k in range(N0):
                    M = rows(k)
                    act.wait_ge(s_up, r * N0 + k + 1)
                    A(work[0:M, 0, k % RING, :], GATE[k % 2][0:M, :], ACT.Silu).then_inc(s_silu, 1)
                    if k:
                        high(k - 1)
                    if more and k == 3:
                        take_xT(m + 1, 1 - p)
                    if more and k == 6:
                        route_exp(r0, r + 1, E0 + 1)
                    if more and k == 9:
                        take_comb(r0, r + 1, 1 - p)
                high(N0 - 1)
                act.wait_ge(s_dn, (r + 1) * N0)
                A(yT[:], Y0[:], ACT.Copy).then_inc(s_yT, 1)

            def front1(m, r, g, p):
                take_xT(m, p)
                hidden(r)
                route_exp(r1, r, E1)
                take_comb(r1, r, p)

            def back1(m, r, g, p, more):
                for kk in range(N1):
                    e, c = divmod(kk, CH1)
                    act.wait_ge(s1_up, r * N1 + kk + 1)
                    b = small[:, SMALL_AT["b1"][0] + kk:SMALL_AT["b1"][0] + kk + 1]
                    A(work[:, 0, kk % RING, :], RINGB[kk % 3][:], ACT.Gelu, bias=b).then_inc(s1_he, 1)
                    if c in HI_BY_ACT:
                        A(hi[:, kk % RING, :], RINGB[kk % 3][:], ACT.Gelu, bias=b).then_inc(s1_hiA, 1)
                    if c == 1:
                        act.wait_ge(s1_cbp, r * E1 + e + 1)
                        A(comb_bc[:, e % 2, :], CB[:], ACT.Copy).then_inc(s1_cb, 1)
                    if more and kk == 10:
                        take_xT(m + 1, 1 - p)
                    if more and kk == 14:
                        hidden(r + 1)
                    if more and kk == 19:
                        route_exp(r1, r + 1, E1)
                    if more and kk == 26:
                        take_comb(r1, r + 1, 1 - p)

            none = lambda *a: None

            def attn0():
                def softmax_exp(n, d, e, p):
                    act.wait_ge(a0[d], n + 1)
                    A(work[:, p, 1, :], work[:, p, 0, :], ACT.Exp, scale=INV).then_inc(a0[e], 1)

                with act.Fori(0, GROUPS // 2) as i:
                    for p in (0, 1):
                        act.wait_ge(a0["T"], i * 2 + p + 1)
                        A(xT[:, p, :], bank[6 + p][:], ACT.Identity, bias=cst("beta"), scale=cst("gamma"))\
                            .then_inc(a0["hT"], 1)
                    for p in (0, 1):
                        act.wait_ge(a0["q"], i * 2 + p + 1)
                        A(attn[:, 0, p, :], bank[p][:], ACT.Identity, bias=cst("bq")).then_inc(a0["qT"], 1)
                        act.wait_ge(a0["k"], i * 2 + p + 1)
                        A(attn[:, 0, 2 + p, :], bank[2 + p][:], ACT.Identity, bias=cst("bk")).then_inc(a0["kT"], 1)
                    for p in (0, 1):
                        softmax_exp(i * 2 + p, "d1", "e1", p)
                    for p in (0, 1):
                        act.wait_ge(a0["mixt"], i * 2 + p + 1)
                        A(attn[:, 0, p, :], bank[4 + p][:], ACT.Copy).then_inc(a0["mtok"], 1)
                    for p in (0, 1):
                        softmax_exp(i * 2 + p, "d2", "e2", p)

            def attn1():
                with act.Fori(0, GROUPS // 2) as i:
                    for p in (0, 1):
                        act.wait_ge(a1["T"], i * 2 + p + 1)
                        A(xT[:, p, :], bank[6 + p][:], ACT.Copy).then_inc(a1["xT"], 1)
                    for p in (0, 1):
                        act.wait_ge(a1["q"], i * 2 + p + 1)
                        A(attn[:, 0, p, :], bank[p][:], ACT.Identity, bias=cst("bq1")).then_inc(a1["qT"], 1)
                        act.wait_ge(a1["k"], i * 2 + p + 1)
                        A(attn[:, 0, 2 + p, :], bank[2 + p][:], ACT.Identity, bias=cst("bk1")).then_inc(a1["kT"], 1)
                    for p in (0, 1):
                        act.wait_ge(a1["nmax"], i * 2 + p + 1)
                        for j in range(TILES):
                            ins = A(work[:, p, j // 2, (j % 2) * SEQ:(j % 2 + 1) * SEQ],
                                    bank[4 * (j // 2) + p][:, (j % 2) * SEQ:(j % 2 + 1) * SEQ], ACT.Exp,
                                    bias=mx[:, p, j:j + 1], scale=INV, accum_out=rsum[:, p, j:j + 1])
                        ins.then_inc(a1["e"], 1)
                    for p in (0, 1):
                        act.wait_ge(a1["aT"], i * 2 + p + 1)
                        A(attn[:, 1, 2 * p, :], bank[2 + p][:], ACT.Copy)
                        A(attn[:, 1, 2 * p + 1, :], bank[6 + p][:], ACT.Copy).then_inc(a1["aTc"], 1)

            act.wait_ge(s_hr1, 1)
            ffn_groups(act, 0, 0, front0, back0, none)
            attn0()
            ffn_groups(act, 1, 1, front0, back0, none)
            ffn_groups(act, 2, 0, front1, back1, none)
            attn1()
            ffn_groups(act, 3, 1, front1, back1, none)

        @block.tensor
        def _(pe):
            MM = nc.tensor.matmul

            def three(dst, w_hi, w_lo, x_hi, x_lo, start, stop):
                MM(dst, w_hi, x_hi, start=start, stop=False)
                MM(dst, w_hi, x_lo, start=False, stop=False)
                return MM(dst, w_lo, x_hi, start=False, stop=stop)

            def transpose4(dst, src, n=P):
                for j in range(TILES):
                    last = nc.tensor.transpose(dst[0:n, j * P:(j + 1) * P], src(j), ident)
                return last

            def front_T(m, p):
                pe.wait_ge(s_xn, m + 1)
                transpose4(TB, lambda j: xn[:, p, j, :]).then_inc(s_T, 1)

            def logits0(m, r, p):
                pe.wait_ge(s_xh, m + 1)
                for j in range(TILES):
                    last = MM(RB[:, j * 32:j * 32 + E0 + 1], xT[:, p, j * P:(j + 1) * P], cst("gate0"),
                              start=True, stop=True)
                last.then_inc(r0["logits"], 1)

            def comb_T(s, r):
                pe.wait_ge(s["comb"], r + 1)
                transpose4(RB, lambda j: cm[:, j, :].bitcast(F32)).then_inc(s["combT"], 1)

            def out_T(s, count):
                pe.wait_ge(s, count)
                transpose4(TB, lambda j: yT[:, j * P:(j + 1) * P]).then_inc(s_oT, 1)

            def hidden(m, r, p):
                pe.wait_ge(s_xh, m + 1)
                MM(RB[0:64, :], cst("wr1"), xT[:, p, :], start=True, stop=True).then_inc(r1["hid"], 1)

            def logits1(r):
                pe.wait_ge(r1["gelu"], r + 1)
                for j in range(TILES):
                    last = MM(RB[:, j * 32:j * 32 + E1], hr[0:65, j * P:(j + 1) * P], cst("wr2", 65),
                              start=True, stop=True)
                last.then_inc(r1["logits"], 1)

            def front0(m, r, g, p):
                front_T(m, p)
                logits0(m, r, p)
                comb_T(r0, r)

            def back0(m, r, g, p, more):
                def up(k):
                    M = rows(k)
                    if k >= 2:
                        pe.wait_ge(s_t, r * N0 + k - 1)
                    three(GATE[k % 2][0:M, :], up_w(w0h, k, True), up_w(w0l, k, True), xh[:, p, :], xl[:, p, :], True, True)
                    three(UP[k % 2][0:M, :], up_w(w0h, k, False), up_w(w0l, k, False), xh[:, p, :], xl[:, p, :], True, True)
                    if k:
                        pe.wait_ge(s_u, r * N0 + k)
                    MM(CB[0:M, :], sel0r[0:64, min(k, PAIRS), 0:M], combT[:, p, :], start=True, stop=True).then_inc(s_up, 1)

                def down(k):
                    M = rows(k)
                    pe.wait_ge(s_ul, r * N0 + k + 1)
                    three(Y0[:], down_w(w0h, k), down_w(w0l, k), hi[0:M, k % RING, :], lo[0:M, k % RING, :],
                          k == 0, k == N0 - 1).then_inc(s_dn, 1)

                pe.wait_ge(s_xl, m + 1)
                pe.wait_ge(s_ct, m + 1)
                up(0)
                up(1)
                if not isinstance(g, int) or g > 0:
                    out_prev(m, r, g)
                for k in range(N0):
                    if k + 2 < N0:
                        up(k + 2)
                    down(k)
                    if more and k == 1:
                        pe.wait_ge(s_xo, m + 1)
                        front_T(m + 1, 1 - p)
                    if more and k == 3:
                        logits0(m + 1, r + 1, 1 - p)
                    if more and k == 7:
                        comb_T(r0, r + 1)

            def out_prev(m, r, g):
                out_T(s_yT, r)

            def finish0(m, r, g):
                out_T(s_yT, r + 1)

            def front1(m, r, g, p):
                front_T(m, p)
                hidden(m, r, p)
                logits1(r)
                comb_T(r1, r)

            def back1(m, r, g, p, more):
                def up(kk):
                    ws = slice(kk * P, (kk + 1) * P)
                    three(RINGB[kk % 3][:], w1h[:, ws], w1l[:, ws], xh[:, p, :], xl[:, p, :], True, True).then_inc(s1_up, 1)

                def down(kk):
                    e, c = divmod(kk, CH1)
                    if c == 0:
                        if e >= 1:
                            pe.wait_ge(s1_cb, r * E1 + e)
                        if e >= 2:
                            pe.wait_ge(s1_term, r * E1 + e - 1)
                        MM(CB[:], sel1r[0:64, e, :], combT[:, p, :], start=True, stop=True).then_inc(s1_cbp, 1)
                    ws = slice(kk * P, (kk + 1) * P)
                    pe.wait_ge(s1_lo, r * N1 + kk + 1)
                    last = three(YB[e % 2][:], w2h[:, ws], w2l[:, ws], hi[:, kk % RING, :], lo[:, kk % RING, :],
                                 c == 0, c == CH1 - 1)
                    if c == CH1 - 1:
                        last.then_inc(s1_Y, 1)

                pe.wait_ge(s_xl, m + 1)
                pe.wait_ge(s_ct, m + 1)
                up(0)
                up(1)
                if not isinstance(g, int) or g > 0:
                    out_T(s1_acc, r * (E1 - 1))
                for kk in range(N1):
                    if kk + 2 < N1:
                        up(kk + 2)
                    down(kk)
                    if more and kk == 7:
                        pe.wait_ge(s_xo, m + 1)
                        front_T(m + 1, 1 - p)
                    if more and kk == 11:
                        hidden(m + 1, r + 1, 1 - p)
                    if more and kk == 15:
                        logits1(r + 1)
                    if more and kk == 23:
                        comb_T(r1, r + 1)

            def finish1(m, r, g):
                out_T(s1_acc, (r + 1) * (E1 - 1))

            def tok_major(dst, src, w):
                for j in range(TILES):
                    last = MM(dst[:, j * D:(j + 1) * D], src[:, j * P:(j + 1) * P], w, start=True, stop=True)
                return last

            def attn0():
                tri0, tri1 = cst("tri0"), cst("tri1")
                with pe.Fori(0, GROUPS // 2) as i:
                    for p in (0, 1):
                        n = i * 2 + p
                        pe.wait_ge(a0["xn"], n + 1)
                        transpose4(bank[6 + p], lambda j: xn[:, p, j, :]).then_inc(a0["T"], 1)
                    for p in (0, 1):
                        n = i * 2 + p
                        pe.wait_ge(a0["hT"], n + 1)
                        MM(bank[p][:], cst("wq"), xT[:, p, :], start=True, stop=True).then_inc(a0["q"], 1)
                        MM(bank[2 + p][:], cst("wk"), xT[:, p, :], start=True, stop=True).then_inc(a0["k"], 1)
                        tok_major(bank[4 + p], xT[:, p, :], cst("wq")).then_inc(a0["qt"], 1)
                        tok_major(bank[6 + p], xT[:, p, :], cst("wv")).then_inc(a0["v"], 1)
                    for p in (0, 1):
                        n = i * 2 + p
                        pe.wait_ge(a0["qT"], n + 1)
                        tok_major(bank[p], attn[:, 0, p, :], cst("wqa")).then_inc(a0["l1"], 1)
                    for p in (0, 1):
                        n = i * 2 + p
                        pe.wait_ge(a0["wq"], n + 1)
                        pe.wait_ge(a0["kT"], n + 1)
                        for b in (0, 1):
                            w = lambda j: work[:, p, 2, j * D:(j + 1) * D]
                            MM(bank[2 + p][:, b * SEQ:(b + 1) * SEQ], w(2 * b), tri0, start=True, stop=False)
                            last = MM(bank[2 + p][:, b * SEQ + P:(b + 1) * SEQ], w(2 * b + 1), tri1, start=False, stop=True)
                        last.then_inc(a0["pool"], 1)
                    for p in (0, 1):
                        n = i * 2 + p
                        pe.wait_ge(a0["mixed"], n + 1)
                        mixed = attn[:, 1, p, :]
                        tok_major(bank[p], mixed, cst("wka")).then_inc(a0["l2"], 1)
                        transpose4(bank[4 + p], lambda j: mixed[:, j * P:(j + 1) * P]).then_inc(a0["mixt"], 1)
                    for p in (0, 1):
                        n = i * 2 + p
                        pe.wait_ge(a0["w2"], n + 1)
                        w = lambda j: work[:, p, 2, j * D:(j + 1) * D]
                        dst = lambda j: bank[2 + p][:, j * D:(j + 1) * D]
                        for b in (0, 1):
                            MM(dst(2 * b), tri0[:, 0:P], w(2 * b), start=True, stop=True)
                            MM(dst(2 * b + 1), tri0[:, P:SEQ], w(2 * b), start=True, stop=False)
                            last = MM(dst(2 * b + 1), tri1, w(2 * b + 1), start=False, stop=True)
                        last.then_inc(a0["pk"], 1)

            def attn1():
                with pe.Fori(0, GROUPS // 2) as i:
                    for p in (0, 1):
                        pe.wait_ge(a1["xn"], i * 2 + p + 1)
                        transpose4(bank[6 + p], lambda j: xn[:, p, j, :]).then_inc(a1["T"], 1)
                    for p in (0, 1):
                        pe.wait_ge(a1["xT"], i * 2 + p + 1)
                        MM(bank[p][:], cst("wq1"), xT[:, p, :], start=True, stop=True).then_inc(a1["q"], 1)
                        MM(bank[2 + p][:], cst("wk1"), xT[:, p, :], start=True, stop=True).then_inc(a1["k"], 1)
                    for p in (0, 1):
                        pe.wait_ge(a1["qT"], i * 2 + p + 1)
                        pe.wait_ge(a1["kT"], i * 2 + p + 1)
                        for j in range(TILES):
                            b = j // 2
                            last = MM(bank[4 * b + p][:, (j % 2) * SEQ:(j % 2 + 1) * SEQ],
                                      attn[:, 0, p, j * P:(j + 1) * P],
                                      attn[:, 0, 2 + p, b * SEQ:(b + 1) * SEQ], start=True, stop=True)
                        last.then_inc(a1["s"], 1)
                    for p in (0, 1):
                        pe.wait_ge(a1["a"], i * 2 + p + 1)
                        for j in range(TILES):
                            for h in (0, 1):
                                last = nc.tensor.transpose(bank[2 + 4 * h + p][:, j * P:(j + 1) * P],
                                                           work[:, p, 2 + j // 2, (j % 2) * SEQ + h * P:(j % 2) * SEQ + (h + 1) * P], ident)
                        last.then_inc(a1["aT"], 1)
                    for p in (0, 1):
                        pe.wait_ge(a1["aTc"], i * 2 + p + 1)
                        for j in range(TILES):
                            b = j // 2
                            for h in (0, 1):
                                last = MM(bank[p][:, j * D:(j + 1) * D], attn[:, 1, 2 * p + h, j * P:(j + 1) * P],
                                          xn[:, p, 2 * b + h, :], start=(h == 0), stop=(h == 1))
                        last.then_inc(a1["o"], 1)

            pe.wait_ge(s_small, 16)
            pe.wait_ge(s_sel, 2)
            pe.wait_ge(s_wl, len(WEIGHTS))
            pe.wait_ge(s_hr1, 1)
            ffn_groups(pe, 0, 0, front0, back0, finish0)
            attn0()
            ffn_groups(pe, 1, 1, front0, back0, finish0)
            ffn_groups(pe, 2, 0, front1, back1, finish1)
            attn1()
            ffn_groups(pe, 3, 1, front1, back1, finish1)

        @block.vector
        def _(dve):
            V = nc.vector
            V.memset(hr[64:65, :], 1.0).then_inc(s_hr1, 1)
            V.memset(cm[:].bitcast(F32), 0.0).then_inc(s_xo, 1)
            stage = work[:].rearrange("p a r n -> p (a r n)")
            for n, (wh, wl, a, b) in enumerate(WEIGHTS):
                dve.wait_ge(s_wh, n + 1)
                V.tensor_tensor(wl[:, a:b], stage[:, 0:b - a], wh[:, a:b].bitcast(F32), ALU.subtract).then_inc(s_wl, 1)
            dve.wait_ge(s_small, 16)
            dve.wait_ge(s_x0, 16)
            dve.wait_ge(s_xo, 1)
            dve.wait_ge(s_wl, len(WEIGHTS))

            def variance(ch, src, p):
                for j in range(TILES):
                    last = V.bn_stats(st[:, p, j, :], src(j))
                ch.link(last)
                V.memset(hold[:], 0.0)
                for j in range(TILES):
                    last = V.bn_aggr(mv[:, p, j, :], st[:, p, j, :])
                ch.link(last)
                return V.tensor_scalar(ve[:, p, :], mv[:, p, :, 1], EPS, None, ALU.add)

            def normed(src, p):
                for j in range(TILES):
                    last = V.tensor_scalar(xn[:, p, j:j + 1, :], src(j), mv[:, p, j, 0:1], rstd[:, p, j:j + 1],
                                           ALU.subtract, ALU.mult)
                return last

            chains = {}

            def stats(s, K, m, r, g, p):
                ch = chains[p] = Chain(dve, s["chain"], r * K)
                variance(ch, lambda j: tile_of(g, j), p).then_inc(s_ve, 1)

            def norm(m, g, p):
                dve.wait_ge(s_rstd, m + 1)
                normed(lambda j: tile_of(g, j), p).then_inc(s_xn, 1)

            def split(m, p):
                dve.wait_ge(s_xh, m + 1)
                V.tensor_tensor(xl[:, p, :], TB[:], xh[:, p, :].bitcast(F32), ALU.subtract).then_inc(s_xl, 1)

            def tab(i, w):
                return rt[:, i, 0:TILES * w].rearrange("p (j e) -> p j e", j=TILES)

            def route_max(s, r, p, E, w):
                ch = chains[p]
                lg = RB[:, 0:TILES * 32].rearrange("p (j e) -> p j e", j=TILES)
                dve.wait_ge(s["logits"], r + 1)
                ch.link(V.tensor_reduce(mx[:, 0, :], lg[:, :, 0:E], AX_X, ALU.max))
                if w > E:
                    V.tensor_scalar(tab(0, w)[:, :, E:w], lg[:, :, E:w], -1.0, None, ALU.mult)
                V.tensor_tensor(tab(0, w)[:, :, 0:E], lg[:, :, 0:E], over(mx[:, 0, :], E), ALU.subtract).then_inc(s["d"], 1)

            def route_top2(s, r, p, E, w):
                ch = chains[p]
                dve.wait_ge(s["d"], r + 1)
                d = tab(0, w)[:, :, 0:E]
                tie = cst("tie").rearrange("p (j e) -> p j e", j=TILES)[:, :, 0:E]
                ch.link(V.scalar_tensor_tensor(tab(2, E), d, 0.0, tie, ALU.is_ge, ALU.mult))
                ch.link(V.tensor_reduce(mx[:, 1, :], tab(2, E), AX_X, ALU.max))
                ch.link(V.tensor_tensor(tab(3, E), tab(2, E), over(mx[:, 1, :], E), ALU.is_equal))
                ch.link(V.scalar_tensor_tensor(tab(4, E), tab(3, E), -BIG, d, ALU.mult, ALU.add))
                ch.link(V.tensor_reduce(mx[:, 2, :], tab(4, E), AX_X, ALU.max))
                ch.link(V.tensor_tensor(tab(5, E), tab(4, E), over(mx[:, 2, :], E), ALU.is_equal))
                ch.link(V.tensor_tensor(tab(5, E), tab(5, E), tie, ALU.mult))
                ch.link(V.tensor_reduce(mx[:, 3, :], tab(5, E), AX_X, ALU.max))
                ch.link(V.tensor_tensor(tab(6, E), tab(5, E), over(mx[:, 3, :], E), ALU.is_equal))
                ch.link(V.tensor_tensor(tab(3, E), tab(3, E), tab(6, E), ALU.add))

            def comb_parts(ch, s, src, w):
                ch.link(V.tensor_scalar(cm[:, :, 0:w], src, 0.5, None, ALU.mult))
                V.scalar_tensor_tensor(cm[:, :, LO:LO + w], src, 0.5, cm[:, :, 0:w].bitcast(F32), ALU.mult,
                                       ALU.subtract).then_inc(s["comb"], 1)

            def route_comb0(r, p):
                ch = chains[p]
                w = E0 + 1
                dve.wait_ge(r0["exp"], r + 1)
                ex = tab(1, w)
                V.tensor_scalar(mx[:, 4, :], ex[:, :, E0], 1.0, None, ALU.add)
                ch.link(V.tensor_tensor(tab(4, E0), ex[:, :, 0:E0], tab(3, E0), ALU.mult))
                V.tensor_reduce(mx[:, 5, :], tab(4, E0), AX_X, ALU.add)
                return ch

            def route_tail0(r, p):
                ch = route_comb0(r, p)
                w = E0 + 1
                ch.link(V.reciprocal(tab(7, w)[:, :, E0], mx[:, 4, :]))
                ch.link(V.reciprocal(mx[:, 6, :], mx[:, 5, :]))
                ch.link(V.tensor_tensor(tab(7, w)[:, :, 0:E0], tab(4, E0), over(mx[:, 6, :], E0), ALU.mult))
                comb_parts(ch, r0, tab(7, w), w)
                assert ch.n == K0C, ch.n

            def route_tail1(r, p):
                ch = chains[p]
                dve.wait_ge(r1["exp"], r + 1)
                ex = tab(1, E1)
                ch.link(V.tensor_reduce(mx[:, 5, :], ex, AX_X, ALU.add))
                ch.link(V.reciprocal(mx[:, 6, :], mx[:, 5, :]))
                ch.link(V.tensor_tensor(tab(4, E1), ex, tab(3, E1), ALU.mult))
                ch.link(V.tensor_tensor(tab(7, E1), tab(4, E1), over(mx[:, 6, :], E1), ALU.mult))
                comb_parts(ch, r1, tab(7, E1), E1)
                assert ch.n == K1C, ch.n

            def add_out(g, n):
                dve.wait_ge(s_oT, n)
                V.tensor_tensor(group_of(g), group_of(g), t4(TB[:]), ALU.add).then_inc(s_xo, 1)

            def front0(m, r, g, p):
                if m:
                    dve.wait_ge(s_xo, 1)
                stats(r0, K0C, m, r, g, p)
                norm(m, g, p)
                split(m, p)
                route_max(r0, r, p, E0, E0 + 1)
                route_top2(r0, r, p, E0, E0 + 1)
                route_tail0(r, p)

            def back0(m, r, g, p, more):
                for k in range(N0):
                    M = rows(k)
                    if k == 1 and (not isinstance(g, int) or g > 0):
                        add_out(g - 1, m)
                    S, U = work[0:M, 0, k % RING, :], work[0:M, 1, k % RING, :]
                    dve.wait_ge(s_silu, r * N0 + k + 1)
                    V.tensor_tensor(S, S, UP[k % 2][0:M, :], ALU.mult).then_inc(s_t, 1)
                    dve.wait_ge(s_t, r * N0 + k + 1)
                    V.tensor_tensor(U, S, CB[0:M, :], ALU.mult).then_inc(s_u, 1)
                    if more and k == 0:
                        stats(r0, K0C, m + 1, r + 1, g + 1, 1 - p)
                    if more and k == 1:
                        norm(m + 1, g + 1, 1 - p)
                    if more and k == 4:
                        split(m + 1, 1 - p)
                    if more and k == 5:
                        route_max(r0, r + 1, 1 - p, E0, E0 + 1)
                    if more and k == 6:
                        route_top2(r0, r + 1, 1 - p, E0, E0 + 1)
                    if more and k == 7:
                        route_tail0(r + 1, 1 - p)

            def finish(m, r, g):
                add_out(g, m + 1)

            def front1(m, r, g, p):
                stats(r1, K1C, m, r, g, p)
                norm(m, g, p)
                split(m, p)
                route_max(r1, r, p, E1, E1)
                route_top2(r1, r, p, E1, E1)
                route_tail1(r, p)

            def back1(m, r, g, p, more):
                NA = len(HI_BY_ACT)
                ND = CH1 - NA
                seen_a = seen_d = 0
                for kk in range(N1):
                    e, c = divmod(kk, CH1)
                    if kk == 1 and (not isinstance(g, int) or g > 0):
                        add_out(g - 1, m)
                    he, h, l = work[:, 0, kk % RING, :], hi[:, kk % RING, :], lo[:, kk % RING, :]
                    dve.wait_ge(s1_he, r * N1 + kk + 1)
                    if c in HI_BY_ACT:
                        seen_a += 1
                        dve.wait_ge(s1_hiA, r * (E1 * NA) + seen_a)
                    else:
                        seen_d += 1
                        V.tensor_scalar(h, he, 1.0, None, ALU.mult).then_inc(s1_hiD, 1)
                        dve.wait_ge(s1_hiD, r * (E1 * ND) + seen_d)
                    V.tensor_tensor(l, he, h.bitcast(F32), ALU.subtract).then_inc(s1_lo, 1)
                    if kk % CH1 == 2 and e:
                        weigh(r, e - 1)
                    if more and kk == 4:
                        stats(r1, K1C, m + 1, r + 1, g + 1, 1 - p)
                    if more and kk == 6:
                        norm(m + 1, g + 1, 1 - p)
                    if more and kk == 12:
                        split(m + 1, 1 - p)
                    if more and kk == 18:
                        route_max(r1, r + 1, 1 - p, E1, E1)
                    if more and kk == 20:
                        route_top2(r1, r + 1, 1 - p, E1, E1)
                    if more and kk == 22:
                        route_tail1(r + 1, 1 - p)
                weigh(r, E1 - 1)

            def weigh(r, e):
                dve.wait_ge(s1_Y, r * E1 + e + 1)
                dve.wait_ge(s1_cb, r * E1 + e + 1)
                if e >= 3:
                    dve.wait_ge(s1_acc, r * (E1 - 1) + e - 2)
                dst = term[:, e % 2, :] if e else yT[:]
                b = SMALL_AT["b2"][0] + e
                V.scalar_tensor_tensor(dst, YB[e % 2][:], small[:, b:b + 1], comb_bc[:, e % 2, :], ALU.add,
                                       ALU.mult).then_inc(s1_term, 1)

            def row(name):
                return cst(name).unsqueeze(1).broadcast_to([P, TILES, D])

            def attn0():
                s = a0
                with dve.Fori(0, GROUPS // 2) as i:
                    ch = Chain(dve, s["chain"], i * KA0)
                    for p in (0, 1):
                        variance(ch, lambda j: tile_of(i * 2 + p, j), p).then_inc(s["ve1"], 1)
                    for p in (0, 1):
                        dve.wait_ge(s["rstd1"], i * 2 + p + 1)
                        ch.link(normed(lambda j: tile_of(i * 2 + p, j), p))
                        variance(ch, lambda j: xn[:, p, j, :], p).then_inc(s["ve2"], 1)
                    for p in (0, 1):
                        dve.wait_ge(s["rstd2"], i * 2 + p + 1)
                        normed(lambda j: xn[:, p, j:j + 1, :], p).then_inc(s["xn"], 1)
                    for p in (0, 1):
                        dve.wait_ge(s["qt"], i * 2 + p + 1)
                        V.tensor_tensor(t4(attn[:, 1, 2 + p, :]), t4(bank[4 + p][:]), row("bq_row"), ALU.add)
                        dve.wait_ge(s["v"], i * 2 + p + 1)
                        V.tensor_tensor(t4(comb_bc[:, p, :]), t4(bank[6 + p][:]), row("bv_row"), ALU.add)

                    def logits(p, lsem, bias, dsem):
                        dve.wait_ge(s[lsem], i * 2 + p + 1)
                        L = t4(work[:, p, 0, :])
                        ch.link(V.tensor_tensor(L, t4(bank[p][:]), row(bias), ALU.add))
                        ch.link(V.tensor_reduce(mx[:, p, :], L, AX_X, ALU.max))
                        V.tensor_tensor(L, L, over(mx[:, p, :], D), ALU.subtract).then_inc(s[dsem], 1)

                    def weights(p, esem, by, bysem, wsem):
                        dve.wait_ge(s[esem], i * 2 + p + 1)
                        Ex = t4(work[:, p, 1, :])
                        ch.link(V.tensor_reduce(rsum[:, p, :], Ex, AX_X, ALU.add))
                        ch.link(V.reciprocal(rinv[:, p, :], rsum[:, p, :]))
                        ch.link(V.tensor_tensor(Ex, Ex, over(rinv[:, p, :], D), ALU.mult))
                        if bysem:
                            dve.wait_ge(s[bysem], i * 2 + p + 1)
                        V.tensor_tensor(t4(work[:, p, 2, :]), Ex, t4(by), ALU.mult).then_inc(s[wsem], 1)

                    for p in (0, 1):
                        logits(p, "l1", "bqa_row", "d1")
                    for p in (0, 1):
                        weights(p, "e1", attn[:, 1, 2 + p, :], None, "wq")
                    for p in (0, 1):
                        dve.wait_ge(s["pool"], i * 2 + p + 1)
                        dve.wait_ge(s["kT"], i * 2 + p + 1)
                        V.tensor_tensor(attn[:, 1, p, :], bank[2 + p][:], attn[:, 0, 2 + p, :], ALU.mult)\
                            .then_inc(s["mixed"], 1)
                    for p in (0, 1):
                        logits(p, "l2", "bka_row", "d2")
                    for p in (0, 1):
                        weights(p, "e2", attn[:, 0, p, :], "mtok", "w2")
                    for p in (0, 1):
                        dve.wait_ge(s["pk"], i * 2 + p + 1)
                        ch.link(V.tensor_tensor(term[:, p, :], bank[2 + p][:], comb_bc[:, p, :], ALU.mult))
                        ch.link(V.tensor_tensor(group_of(i * 2 + p), group_of(i * 2 + p), t4(term[:, p, :]), ALU.add))
                    assert ch.n == KA0, ch.n

            def attn1():
                s = a1
                with dve.Fori(0, GROUPS // 2) as i:
                    ch = Chain(dve, s["chain"], i * KA1)
                    for p in (0, 1):
                        variance(ch, lambda j: tile_of(i * 2 + p, j), p).then_inc(s["ve1"], 1)
                    for p in (0, 1):
                        dve.wait_ge(s["rstd1"], i * 2 + p + 1)
                        normed(lambda j: tile_of(i * 2 + p, j), p).then_inc(s["xn"], 1)
                    for p in (0, 1):
                        dve.wait_ge(s["s"], i * 2 + p + 1)
                        for b in (0, 1):
                            last = V.tensor_reduce(mx[:, 2 + p, 2 * b:2 * b + 2],
                                                   bank[4 * b + p][:].rearrange("q (j t) -> q j t", j=2), AX_X, ALU.max)
                        ch.link(last)
                        V.tensor_scalar(mx[:, p, :], mx[:, 2 + p, :], -INV, None, ALU.mult).then_inc(s["nmax"], 1)
                    for p in (0, 1):
                        dve.wait_ge(s["e"], i * 2 + p + 1)
                        ch.link(V.reciprocal(rinv[:, p, :], rsum[:, p, :]))
                        E = lambda b: work[:, p, b, :].rearrange("q (j t) -> q j t", j=2)
                        A_ = lambda b: work[:, p, 2 + b, :].rearrange("q (j t) -> q j t", j=2)
                        two = lambda col, b: col[:, 2 * b:2 * b + 2].unsqueeze(2).broadcast_to([P, 2, SEQ])
                        for b in (0, 1):
                            last = V.tensor_tensor(E(b), E(b), two(rinv[:, p, :], b), ALU.mult)
                        ch.link(last)
                        for b in (0, 1):
                            for h in (0, 1):
                                dia = E(b)[:, h, h * P:(h + 1) * P]
                                last = V.tensor_tensor(dia, dia, ident, ALU.add)
                        ch.link(last)
                        for b in (0, 1):
                            last = V.tensor_reduce(mx[:, 4 + p, 2 * b:2 * b + 2], E(b), AX_X, ALU.add)
                        ch.link(last)
                        ch.link(V.tensor_scalar(mx[:, 6 + p, :], mx[:, 4 + p, :], 1.0 / SEQ, None, ALU.mult))
                        for b in (0, 1):
                            last = V.tensor_tensor(A_(b), E(b), two(mx[:, 6 + p, :], b), ALU.subtract)
                        last.then_inc(s["a"], 1)
                    for p in (0, 1):
                        dve.wait_ge(s["o"], i * 2 + p + 1)
                        ch.link(V.tensor_tensor(group_of(i * 2 + p), group_of(i * 2 + p), t4(bank[p][:]), ALU.add))
                    assert ch.n == KA1, ch.n

            ffn_groups(dve, 0, 0, front0, back0, finish)
            dve.wait_ge(s_xo, 1 + GROUPS)
            attn0()
            ffn_groups(dve, 1, 1, front0, back0, finish)
            dve.wait_ge(s_xo, 1 + 2 * GROUPS)
            ffn_groups(dve, 2, 0, front1, back1, finish)
            dve.wait_ge(s_xo, 1 + 3 * GROUPS)
            attn1()
            ffn_groups(dve, 3, 1, front1, back1, finish)


K0C, K1C, KA0, KA1 = 18, 18, 34, 18


def kernel(**inputs):
    import numpy as np
    import concourse.bacc as bacc
    from concourse import mybir as mb
    from concourse.bass_utils import run_bass_kernel_spmd as run

    a = {k: np.asarray(v) for k, v in inputs.items()}

    def col(v):
        out = np.zeros((P, 1), np.float32)
        out[:v.shape[0], 0] = v
        return out

    def block_of(v, width):
        out = np.zeros((P, width), np.float32)
        out[:v.shape[0], :v.shape[1]] = v
        return out

    tok = np.arange(SEQ)
    mean_to = (tok[:, None] <= tok[None, :]) / (tok[None, :] + 1.0)
    tie = np.tile(np.arange(E0, 0, -1, dtype=np.float32), TILES)
    sel0 = np.zeros((P, PAIRS + 1, P), np.float32)
    sel1 = np.zeros((P, E1, P), np.float32)
    for base in (0, LO):
        for k in range(PAIRS):
            sel0[base + 2 * k, k, 0:F0] = 1
            sel0[base + 2 * k + 1, k, F0:P] = 1
        sel0[base + E0, PAIRS, :] = 1
        for e in range(E1):
            sel1[base + e, e, :] = 1

    wr2 = np.concatenate([a["L1_ffn_Wr2"].T, a["L1_ffn_br2"][None, :]], axis=0)
    parts = {
        "gate0": np.concatenate([a["L0_ffn_gate_w"].T, a["L0_ffn_shared_gate_w"].T], axis=1),
        "wr1": a["L1_ffn_Wr1"].T, "wr2": block_of(wr2, E1),
        "b1": a["L1_ffn_b1"].reshape(N1, P).T, "b2": a["L1_ffn_b2"].T, "br1": col(a["L1_ffn_br1"]),
        "gamma": col(a["L0_attn_gamma"]), "beta": col(a["L0_attn_beta"]),
        "bq": col(a["L0_attn_bq"]), "bk": col(a["L0_attn_bk"]),
        "wq": a["L0_attn_Wq"], "wqa": a["L0_attn_Wqa"], "wk": a["L0_attn_Wk"], "wka": a["L0_attn_Wka"],
        "wv": a["L0_attn_Wv"],
        "bq_row": np.broadcast_to(a["L0_attn_bq"], (P, D)), "bqa_row": np.broadcast_to(a["L0_attn_bqa"], (P, D)),
        "bka_row": np.broadcast_to(a["L0_attn_bka"], (P, D)), "bv_row": np.broadcast_to(a["L0_attn_bv"], (P, D)),
        "wq1": a["L1_attn_Wq"].T, "wk1": a["L1_attn_Wk"].T,
        "bq1": col(a["L1_attn_bq"]), "bk1": col(a["L1_attn_bk"]),
        "ident": np.eye(P), "tri0": mean_to[0:P, :], "tri1": mean_to[P:SEQ, P:SEQ],
        "tie": np.broadcast_to(tie, (P, TILES * E0)), "sel0": sel0.reshape(P, -1), "sel1": sel1.reshape(P, -1),
    }
    small = np.concatenate([np.asarray(parts[n], np.float32) for n, _ in SMALL], axis=1)

    gu = a["L0_ffn_w_gate_up"]
    shared_down = np.zeros((len(SH_ROWS) * P, D), np.float32)
    shared_down[:SHARED] = a["L0_ffn_shared_w_down"].T
    w0 = np.concatenate([
        gu[:, :, :F0].transpose(1, 0, 2).reshape(D, -1), gu[:, :, F0:].transpose(1, 0, 2).reshape(D, -1),
        a["L0_ffn_w_down"].reshape(PAIRS, P, D).transpose(1, 0, 2).reshape(P, -1),
        a["L0_ffn_shared_w_gate"].T, a["L0_ffn_shared_w_up"].T,
        shared_down.reshape(-1, P, D).transpose(1, 0, 2).reshape(P, -1),
    ], axis=1)
    w1 = a["L1_ffn_W1"].transpose(2, 0, 1).reshape(D, -1)
    w2 = a["L1_ffn_W2"].transpose(0, 2, 1).reshape(E1 * CH1, P, D).transpose(1, 0, 2).reshape(P, -1)

    arrays = {"x": a["L0_attn_hidden_states"], "small": small, "w0": w0, "w1": w1, "w2": w2}
    arrays = {k: np.ascontiguousarray(v) for k, v in arrays.items()}
    nc = bacc.Bacc("TRN2", target_bir_lowering=False, num_devices=1)
    args = [nc.dram_tensor(n, v.shape, mb.dt.from_np(v.dtype), kind="ExternalInput").ap() for n, v in arrays.items()]
    args.append(nc.dram_tensor("out", arrays["x"].shape, F32, kind="ExternalOutput").ap())
    program(nc, *args)
    r = run(nc, [arrays], core_ids=[0])
    return r.results[0]["out"]
```

```python
import math
from contextlib import ExitStack

import concourse.bass as bass
from concourse import mybir

ALU = mybir.AluOpType
ACT = mybir.ActivationFunctionType
F32 = mybir.dt.float32
F32R = mybir.dt.float32r
AX_X = mybir.AxisListType.X

P = 128
D = 128
TILES = 4
GTOK = TILES * P
SEQ = 256
GROUPS = 8
E0, F0 = 16, 64
PAIRS = E0 // 2
SHARED = 352
SH_ROWS = [128, 128, 96]
N0 = PAIRS + len(SH_ROWS)
E1, H1 = 8, 512
CH1 = H1 // P
N1 = E1 * CH1
RING = 4
LO = 32
HI_BY_ACT = (1, 3)
EPS = 1e-5
BIG = 1.0e30
INV = float(D) ** -0.5
C_G, C_H, C_D = 0, E0 * F0, 2 * E0 * F0
C_SG = C_D + PAIRS * D
C_SU, C_SD = C_SG + SHARED, C_SG + 2 * SHARED
W0_COLS = C_SD + len(SH_ROWS) * D
W1_COLS = E1 * H1
EIGHTH = W1_COLS // GROUPS
W0_PARTS = 4
W0_PART = W0_COLS // W0_PARTS

SMALL = [
    ("ident", P), ("gate0", E0 + 1), ("tie", TILES * E0),
    ("wr1", 64), ("wr2", E1), ("b1", N1), ("b2", E1), ("br1", 1), ("gamma", 1), ("beta", 1),
    ("bq", 1), ("bk", 1), ("wq", D), ("wqa", D), ("wk", D), ("wka", D), ("wv", D), ("bq_row", D), ("bqa_row", D),
    ("bka_row", D), ("bv_row", D), ("ones_row", P), ("wq1", D), ("wk1", D), ("bq1", 1), ("bk1", 1), ("tri0", SEQ),
    ("tri1", P),
]
FIRST_SMALL = P + E0 + 1 + TILES * E0
SMALL_AT = {}
SMALL_COLS = 0
for _n, _w in SMALL:
    SMALL_AT[_n] = (SMALL_COLS, _w)
    SMALL_COLS += _w


def program(nc, x_in, small_in, sel_in, w0_in, w1_in, w2_in, out):
    x_dram = x_in.rearrange("a (b p) d -> p (a b) d", p=P)
    out_dram = out.rearrange("a (b p) d -> p (a b) d", p=P)
    with ExitStack() as ctx:
        def sb(name, shape, dt=F32):
            return ctx.enter_context(nc.sbuf_tensor(name, shape, dt))

        def sem(name):
            return ctx.enter_context(nc.semaphore(name))

        X = sb("x_sb", [P, GROUPS * TILES, D])
        small = sb("small_sb", [P, SMALL_COLS])

        def split_weights(name, cols):
            high = sb(name + "_high", [P, cols], F32R)
            with nc.sbuf_tensor(name + "_raw", [P, cols], F32) as raw:
                pass
            return high, sb(name + "_low", [P, cols], F32R), raw

        w0h, w0l, w0raw = split_weights("w0", W0_COLS)
        w1h, w1l, w1raw = split_weights("w1", W1_COLS)
        w2h, w2l, w2raw = split_weights("w2", W1_COLS)
        work = sb("work", [P, 2, RING, GTOK])
        with nc.sbuf_tensor("attn", [P, 2, RING, GTOK], F32) as attn:
            pass
        hi = sb("hi", [P, RING, GTOK], F32R)
        lo = sb("lo", [P, RING, GTOK], F32R)
        with nc.sbuf_tensor("sel_raw", [64, PAIRS + 1 + E1, P], F32) as sel_raw:
            pass
        sel = sb("sel", [64, PAIRS + 1 + E1, P], F32R)
        xn = sb("xn", [P, 2, TILES, D])
        xT = sb("xT", [P, 2, GTOK])
        xh, xl = sb("xh", [P, 2, GTOK], F32R), sb("xl", [P, 2, GTOK], F32R)
        combT = sb("combT", [64, 2, GTOK], F32R)
        comb_bc = sb("comb_bc", [P, 2, GTOK])
        term = sb("term", [P, 2, GTOK])
        yT = sb("yT", [P, GTOK])
        hr = sb("hr", [65, GTOK])
        st = sb("st", [P, 2, TILES, 6])
        mv = sb("mv", [P, 2, TILES, 2])
        ve = sb("ve", [P, 2, TILES])
        rstd = sb("rstd", [P, 2, TILES])
        mhalf = sb("mhalf", [P, TILES])
        euler = sb("euler", [P, TILES * E1])
        gates = sb("gates", [P, 3, 2 * TILES])
        cm = sb("cm", [P, TILES, P], F32R)
        hold = sb("hold", [P, 1])
        rt = sb("rt", [P, 8, TILES * (E0 + 1)])
        mx = sb("mx", [P, 8, TILES])
        rmx = sb("rmx", [P, 8, TILES])
        rsum = sb("rsum", [P, 2, TILES])
        rinv = sb("rinv", [P, 2, TILES])

        bank = [ctx.enter_context(nc.psum_tensor(f"bank{i}", [P, GTOK], F32)) for i in range(8)]
        GATE, UP = bank[0:2], bank[2:4]
        RINGB = [bank[0], bank[1], bank[2], bank[7]]
        YB = [bank[3], bank[4]]
        Y0, CB, TB, RB = bank[4], bank[5], bank[6], bank[6]
        CB2 = [bank[5], bank[7]]

        def cst(name, rows=P):
            a, w = SMALL_AT[name]
            return small[0:rows, a:a + w]

        ident = cst("ident")

        s_small, s_small2, s_sel_raw = sem("s_first_small_loaded"), sem("s_small_loaded"), sem("s_sel_loaded")
        s_x0, s_x1 = sem("s_first_x_loaded"), sem("s_x_loaded")
        s_raw = [sem(f"s_w0_raw{n}_loaded") for n in range(W0_PARTS)]
        s_raw1, s_raw2 = sem("s_w1_loaded"), sem("s_w2_loaded")
        s_w12h, s_w12l = sem("s_w12_high"), sem("s_w12_low")
        s_wh, s_wl = sem("s_weights_high"), sem("s_weights_low")
        s_mhalf, s_sel, s_hr1 = sem("s_minus_half"), sem("s_selectors"), sem("s_hr_ones")
        s_out = sem("s_out")
        s_ve, s_rstd, s_xn = sem("s_var_eps"), sem("s_rstd"), sem("s_xn")
        s_T, s_xh, s_xl = sem("s_xn_transposed"), sem("s_xT_high"), sem("s_xT_low")
        s_ct = sem("s_comb_transposed_copied")
        s_yT, s_xo = sem("s_yT"), sem("s_x_updated_by_ffn")
        s_oT = sem("s_out_transposed")
        r0 = {n: sem("s0_" + n) for n in ("chain", "logits", "d", "exp", "comb", "combT")}
        s_up, s_silu, s_t, s_u, s_uh, s_ul, s_dn = (sem("s0_" + n) for n in ("up", "silu", "gated", "scaled", "high", "low", "down"))
        s_gate, s_cb = sem("s0_gate"), sem("s0_comb_bc")
        r1 = {n: sem("s1_" + n) for n in ("chain", "hid", "gelu", "logits", "d", "exp", "comb", "combT")}
        s1_up, s1_he, s1_hiA, s1_hiD, s1_lo, s1_Y = (sem("s1_" + n) for n in ("up", "gelu_f", "high_act", "high_dve", "low", "down"))
        s1_cbp, s1_cb, s1_term, s1_acc = (sem("s1_" + n) for n in ("comb_bc_psum", "comb_bc", "term", "acc"))
        ROUTE, WIDTH = (r0, r1), (E0 + 1, E1)
        A0N = ("ln", "one", "two", "ve1", "rstd1", "ve2", "rstd2", "xn", "T", "hT", "q", "k", "qt", "v", "qT", "kT", "l1",
               "d1", "vc", "e1", "wq", "pool", "mixed", "l2", "mixt", "d2", "e2", "w2", "pk")
        a0 = {n: sem("a0_" + n) for n in A0N}
        A1N = ("ln", "one", "two", "ve1", "rstd1", "xn", "xnc", "T", "xT", "q", "k", "qT", "kT", "s", "nmax", "e", "a",
               "aT", "aTc", "o")
        a1 = {n: sem("a1_" + n) for n in A1N}

        block = ctx.enter_context(nc.Block())

        def tile_of(g, j):
            return X[:, bass.ds(g * TILES + j, 1), :]

        def group_of(g):
            return X[:, bass.ts(g, TILES), :]

        def t4(ap):
            return ap.rearrange("p (j d) -> p j d", j=TILES)

        def over(col, n):
            return col.unsqueeze(2).broadcast_to([P, TILES, n])

        def down_w(w, k):
            if k < PAIRS:
                return w[:, C_D + k * D:C_D + (k + 1) * D]
            s = k - PAIRS
            return w[0:SH_ROWS[s], C_SD + s * D:C_SD + (s + 1) * D]

        def up_w(w, k, gate):
            if k < PAIRS:
                a = (C_G if gate else C_H) + k * P
                return w[:, a:a + P]
            s = k - PAIRS
            a = (C_SG if gate else C_SU) + s * P
            return w[:, a:a + SH_ROWS[s]]

        def rows(k):
            return P if k < PAIRS else SH_ROWS[k - PAIRS]

        class Chain:

            def __init__(self, eng, s, base, n=0):
                self.eng, self.s, self.base, self.n = eng, s, base, n

            def mark(self, ins):
                self.n += 1
                ins.then_inc(self.s, 1)

            def need(self):
                self.eng.wait_ge(self.s, self.base + self.n)

        def ffn_groups(eng, f, kind, occ, front, back, finish, fronted=False, then=None, to=None):
            def after(m, r, g, p):
                return (kind, m + 1, r + 1, g + 1, 1 - p)

            if not fronted:
                front(8 * f, 8 * occ, 0, 0)
            back(8 * f, 8 * occ, 0, 0, after(8 * f, 8 * occ, 0, 0), None)
            with eng.Fori(0, GROUPS // 2 - 1) as i:
                for p in (1, 0):
                    g = i * 2 + (2 - p)
                    back(g + 8 * f, g + 8 * occ, g, p, after(g + 8 * f, g + 8 * occ, g, p), None)
            last = (8 * f + GROUPS - 1, 8 * occ + GROUPS - 1, GROUPS - 1)
            back(*last, (GROUPS - 1) % 2, then, to)
            finish(*last)

        def attn_groups(eng, step, finish):
            step(0, 0, False, True)
            with eng.Fori(0, GROUPS // 2 - 1) as i:
                for p in (1, 0):
                    step(i * 2 + (2 - p), p, True, True)
            step(GROUPS - 1, (GROUPS - 1) % 2, True, False)
            finish(GROUPS - 1, (GROUPS - 1) % 2)

        THEN_FFN1 = (1, 2 * GROUPS, 0, 0, 0)

        def slot0(p, k):
            q = p * N0 + k
            return q % RING if q < 16 else (q - 16) % 3

        def soon0(p, k):
            return (p * N0 + k) % (2 * N0) in (0, 1, 2, 19, 20, 21)


        @block.sync
        def _(sp):
            sp.dma_start(X[:, 0:TILES, :], x_dram[:, 0:TILES, :]).then_inc(s_x0, 16)
            sp.dma_start(small[:, 0:FIRST_SMALL], small_in[:, 0:FIRST_SMALL]).then_inc(s_small, 16)
            sp.dma_start(sel_raw[:], sel_in).then_inc(s_sel_raw, 16)
            for n in range(W0_PARTS):
                part = slice(n * W0_PART, (n + 1) * W0_PART)
                sp.dma_start(w0raw[:, part], w0_in[:, part]).then_inc(s_raw[n], 16)
            sp.dma_start(X[:, TILES:, :], x_dram[:, TILES:, :]).then_inc(s_x1, 16)
            sp.dma_start(small[:, FIRST_SMALL:], small_in[:, FIRST_SMALL:]).then_inc(s_small2, 16)
            sp.dma_start(w1raw[:], w1_in).then_inc(s_raw1, 16)
            sp.dma_start(w2raw[:], w2_in).then_inc(s_raw2, 16)
            with sp.Fori(0, GROUPS) as g:
                sp.wait_ge(s_xo, g + 3 * GROUPS + 2)
                sp.dma_start(out_dram[:, bass.ts(g, TILES), :], group_of(g)).then_inc(s_out, 16)
            sp.wait_ge(s_out, 16 * GROUPS)

        @block.gpsimd
        def _(pool):
            nc.gpsimd.memset(mhalf[:], -0.5).then_inc(s_mhalf, 1)
            nc.gpsimd.memset(euler[:], math.e).then_inc(s_mhalf, 1)
            pool.wait_ge(s_mhalf, 2)

            def power(s_in, s_done, n, p):
                pool.wait_ge(s_in, n + 1)
                nc.gpsimd.tensor_tensor(rstd[:, p, :], ve[:, p, :], mhalf[:], ALU.pow).then_inc(s_done, 1)

            def route_exp(kind, r):
                s = ROUTE[kind]
                src, dst = ((gates[:, 0], gates[:, 1]), (rt[:, 0, 0:TILES * E1], rt[:, 1, 0:TILES * E1]))[kind]
                pool.wait_ge(s["d"], r + 1)
                nc.gpsimd.tensor_tensor(dst, euler[:, 0:src.shape[1]], src, ALU.pow).then_inc(s["exp"], 1)

            def ffn0(m, r, g, p, nxt, to):
                for k in range(N0):
                    if k == 7 and nxt:
                        route_exp(nxt[0], nxt[2])
                    if k == 0 and nxt:
                        power(s_ve, s_rstd, m + 1, 1 - p)
                    if k == 6 and to == 0:
                        power(a0["ve1"], a0["rstd1"], 0, 0)
                    if k == 10 and to == 0:
                        power(a0["ve2"], a0["rstd2"], 0, 0)
                    M, n = rows(k), slot0(p, k)
                    pool.wait_ge(s_uh, r * N0 + k + 1)
                    nc.gpsimd.tensor_tensor(lo[0:M, n, :], work[0:M, 1, n, :], hi[0:M, n, :].bitcast(F32), ALU.subtract).then_inc(s_ul, 1)

            def ffn1(m, r, g, p, nxt, to):
                for e in range(E1):
                    if e == 4 and nxt:
                        route_exp(1, r + 1)
                    if e == 1 and nxt:
                        power(s_ve, s_rstd, m + 1, 1 - p)
                    if e == 1 and to == 1:
                        power(a1["ve1"], a1["rstd1"], 0, 0)
                    if e:
                        pool.wait_ge(s1_term, r * E1 + e + 1)
                        if e > 1:
                            pool.wait_ge(s1_acc, r * (E1 - 1) + e - 1)
                        nc.gpsimd.tensor_tensor(yT[:], yT[:], term[:, e % 2, :], ALU.add).then_inc(s1_acc, 1)

            def front0(m, r, g, p):
                power(s_ve, s_rstd, m, p)
                route_exp(0, r)

            def front1(m, r, g, p):
                power(s_ve, s_rstd, m, p)
                route_exp(1, r)

            none = lambda *a: None

            def step0(n, p, second, norm):
                if norm:
                    power(a0["ve1"], a0["rstd1"], n + 1, 1 - p)
                    power(a0["ve2"], a0["rstd2"], n + 1, 1 - p)
                else:
                    power(s_ve, s_rstd, GROUPS, 0)
                for k, (wl, raw, wh) in enumerate(((w1l, w1raw, w1h), (w2l, w2raw, w2h))):
                    pool.wait_ge(s_w12h, n * 2 + k + 1)
                    part = bass.ts(n, EIGHTH)
                    nc.gpsimd.tensor_tensor(wl[:, part], raw[:, part], wh[:, part].bitcast(F32),
                                            ALU.subtract).then_inc(s_w12l, 1)

            def step1(n, p, second, norm):
                if norm:
                    power(a1["ve1"], a1["rstd1"], n + 1, 1 - p)
                else:
                    power(s_ve, s_rstd, 3 * GROUPS, 0)

            ffn_groups(pool, 0, 0, 0, front0, ffn0, none, to=0)
            attn_groups(pool, step0, lambda n, p: route_exp(0, GROUPS))
            ffn_groups(pool, 1, 0, 1, front0, ffn0, none, then=THEN_FFN1, fronted=True)
            ffn_groups(pool, 2, 1, 0, front1, ffn1, none, fronted=True, to=1)
            attn_groups(pool, step1, lambda n, p: route_exp(1, GROUPS))
            ffn_groups(pool, 3, 1, 1, front1, ffn1, none, fronted=True)

        @block.scalar
        def _(act):
            A = nc.scalar.activation

            act.wait_ge(s_sel_raw, 16)
            A(sel[:], sel_raw[:], ACT.Copy).then_inc(s_sel, 1)
            for n in range(W0_PARTS):
                part = slice(n * W0_PART, (n + 1) * W0_PART)
                act.wait_ge(s_raw[n], 16)
                A(w0h[:, part], w0raw[:, part], ACT.Copy).then_inc(s_wh, 1)
            act.wait_ge(s_small2, 16)

            def take_xT(m, p):
                act.wait_ge(s_T, m + 1)
                A(xT[:, p, :], TB[:], ACT.Copy)
                A(xh[:, p, :], TB[:], ACT.Copy).then_inc(s_xh, 1)

            def take_comb(s, r, m, p):
                act.wait_ge(s["combT"], r + 1)
                A(combT[:, p, :], RB[0:64, :], ACT.Copy).then_inc(s_ct, 1)

            def hidden(r):
                act.wait_ge(r1["hid"], r + 1)
                A(hr[0:64, :], RB[0:64, :], ACT.Gelu, bias=cst("br1", 64)).then_inc(r1["gelu"], 1)

            def front0(m, r, g, p):
                take_xT(m, p)
                take_comb(r0, r, m, p)

            def ahead0(n, p):
                act.wait_ge(a0["T"], n + 1)
                A(xT[:, p, :], bank[6 + p][:], ACT.Identity, bias=cst("beta"), scale=cst("gamma")).then_inc(a0["hT"], 1)

            def ahead1(n, p):
                act.wait_ge(a1["T"], n + 1)
                A(xT[:, p, :], bank[6 + p][:], ACT.Copy).then_inc(a1["xT"], 1)

            def take_y(r):
                act.wait_ge(s_dn, r * N0)
                A(yT[:], Y0[:], ACT.Copy).then_inc(s_yT, 1)

            def back0(m, r, g, p, nxt, to):
                def high(k):
                    M, n = rows(k), slot0(p, k)
                    act.wait_ge(s_u, r * N0 + k + 1)
                    if soon0(p, k) and not (isinstance(g, int) and g == 0 and k < 3):
                        act.wait_ge(s_dn, r * N0 + k - 2)
                    A(hi[0:M, n, :], work[0:M, 1, n, :], ACT.Copy).then_inc(s_uh, 1)

                kind, mn, rn, gn, pn = nxt or (None,) * 5
                for k in range(N0):
                    M = rows(k)
                    act.wait_ge(s_gate, r * N0 + k + 1)
                    A(work[0:M, 0, slot0(p, k), :], GATE[(p + k) % 2][0:M, :], ACT.Silu).then_inc(s_silu, 1)
                    if k == 1 and not (isinstance(g, int) and g == 0):
                        take_y(r)
                    if k:
                        high(k - 1)
                    if nxt and k == 4:
                        take_xT(mn, pn)
                    if kind == 1 and k == 6:
                        hidden(rn)
                    if nxt and k == 10:
                        take_comb(ROUTE[kind], rn, mn, pn)
                high(N0 - 1)
                if to == 0:
                    ahead0(0, 0)

            def finish0(m, r, g):
                take_y(r + 1)

            def front1(m, r, g, p):
                take_xT(m, p)
                hidden(r)
                take_comb(r1, r, m, p)

            def back1(m, r, g, p, nxt, to):
                for kk in range(N1):
                    e, c = divmod(kk, CH1)
                    act.wait_ge(s1_up, r * N1 + kk + 1)
                    b = small[:, SMALL_AT["b1"][0] + kk:SMALL_AT["b1"][0] + kk + 1]
                    A(work[:, 0, kk % RING, :], RINGB[kk % RING][:], ACT.Gelu, bias=b).then_inc(s1_he, 1)
                    if c in HI_BY_ACT:
                        A(hi[:, kk % RING, :], RINGB[kk % RING][:], ACT.Gelu, bias=b).then_inc(s1_hiA, 1)
                    if c == 1:
                        act.wait_ge(s1_cbp, r * E1 + e + 1)
                        A(comb_bc[:, e % 2, :], CB[:], ACT.Copy).then_inc(s1_cb, 1)
                    if nxt and kk == 11:
                        take_xT(m + 1, 1 - p)
                    if to == 1 and kk == 11:
                        ahead1(0, 0)
                    if nxt and kk == 16:
                        hidden(r + 1)
                    if nxt and kk == 30:
                        take_comb(r1, r + 1, m + 1, 1 - p)

            none = lambda *a: None

            def attn0():
                def softmax_exp(n, d, e, p):
                    act.wait_ge(a0[d], n + 1)
                    for j in range(TILES):
                        cols = slice(j * D, (j + 1) * D)
                        ins = A(work[:, p, 1, cols], bank[p][:, cols], ACT.Exp, bias=mx[:, p, j:j + 1], scale=INV,
                                accum_out=rsum[:, p, j:j + 1])
                    ins.then_inc(a0[e], 1)

                def step(n, p, second, norm):
                    act.wait_ge(a0["q"], n + 1)
                    A(attn[:, 0, p, :], bank[p][:], ACT.Identity, bias=cst("bq")).then_inc(a0["qT"], 1)
                    act.wait_ge(a0["k"], n + 1)
                    A(attn[:, 0, 2 + p, :], bank[2 + p][:], ACT.Identity, bias=cst("bk")).then_inc(a0["kT"], 1)
                    act.wait_ge(a0["v"], n + 1)
                    A(comb_bc[:, p, :], bank[6 + p][:], ACT.Copy).then_inc(a0["vc"], 1)
                    if second:
                        softmax_exp(n - 1, "d2", "e2", 1 - p)
                    for wh, raw in ((w1h, w1raw), (w2h, w2raw)):
                        part = bass.ts(n, EIGHTH)
                        A(wh[:, part], raw[:, part], ACT.Copy).then_inc(s_w12h, 1)
                    if norm:
                        ahead0(n + 1, 1 - p)
                    else:
                        take_xT(GROUPS, 0)
                    softmax_exp(n, "d1", "e1", p)

                def finish(n, p):
                    softmax_exp(n, "d2", "e2", p)
                    take_comb(r0, GROUPS, GROUPS, 0)

                act.wait_ge(s_raw1, 16)
                act.wait_ge(s_raw2, 16)
                attn_groups(act, step, finish)

            def attn1():
                def transposed(n, p):
                    act.wait_ge(a1["aT"], n + 1)
                    A(attn[:, 1, 2 * p, :], bank[2 + p][:], ACT.Copy)
                    A(attn[:, 1, 2 * p + 1, :], bank[6 + p][:], ACT.Copy).then_inc(a1["aTc"], 1)

                def step(n, p, second, norm):
                    act.wait_ge(a1["q"], n + 1)
                    A(attn[:, 0, p, :], bank[p][:], ACT.Identity, bias=cst("bq1")).then_inc(a1["qT"], 1)
                    act.wait_ge(a1["k"], n + 1)
                    A(attn[:, 0, 2 + p, :], bank[2 + p][:], ACT.Identity, bias=cst("bk1")).then_inc(a1["kT"], 1)
                    if second:
                        transposed(n - 1, 1 - p)
                    act.wait_ge(a1["xn"], n + 1)
                    if not (isinstance(n, int) and n < 2):
                        act.wait_ge(a1["o"], n - 1)
                    A(t4(comb_bc[:, p, :]), xn[:, p], ACT.Copy).then_inc(a1["xnc"], 1)
                    act.wait_ge(a1["nmax"], n + 1)
                    for j in range(TILES):
                        cols = slice((j % 2) * SEQ, (j % 2 + 1) * SEQ)
                        ins = A(work[:, p, j // 2, cols], bank[4 * (j // 2) + p][:, cols], ACT.Exp,
                                bias=mx[:, p, j:j + 1], scale=INV, accum_out=rsum[:, p, j:j + 1])
                    ins.then_inc(a1["e"], 1)
                    if norm:
                        ahead1(n + 1, 1 - p)
                    else:
                        take_xT(3 * GROUPS, 0)

                def finish(n, p):
                    hidden(GROUPS)
                    transposed(n, p)
                    take_comb(r1, GROUPS, 3 * GROUPS, 0)

                attn_groups(act, step, finish)

            act.wait_ge(s_hr1, 1)
            ffn_groups(act, 0, 0, 0, front0, back0, finish0, to=0)
            attn0()
            ffn_groups(act, 1, 0, 1, front0, back0, finish0, then=THEN_FFN1, fronted=True)
            ffn_groups(act, 2, 1, 0, front1, back1, none, fronted=True, to=1)
            attn1()
            ffn_groups(act, 3, 1, 1, front1, back1, none, fronted=True)

        @block.tensor
        def _(pe):
            MM = nc.tensor.matmul

            def three(dst, w_hi, w_lo, x_hi, x_lo, start, stop):
                MM(dst, w_hi, x_hi, start=start, stop=False)
                MM(dst, w_hi, x_lo, start=False, stop=False)
                return MM(dst, w_lo, x_hi, start=False, stop=stop)

            def transpose4(dst, src, n=P):
                for j in range(TILES):
                    last = nc.tensor.transpose(dst[0:n, j * P:(j + 1) * P], src(j), ident)
                return last

            def is_first(g):
                return isinstance(g, int) and g == 0

            def front_T(m, p):
                pe.wait_ge(s_xn, m + 1)
                transpose4(TB, lambda j: xn[:, p, j, :]).then_inc(s_T, 1)

            def logits0(m, r, p):
                pe.wait_ge(s_xl, m + 1)
                for j in range(TILES):
                    last = MM(RB[:, j * 32:j * 32 + E0 + 1], xT[:, p, j * P:(j + 1) * P], cst("gate0"),
                              start=True, stop=True)
                last.then_inc(r0["logits"], 1)

            def comb_T(s, r):
                pe.wait_ge(s["comb"], r + 1)
                transpose4(RB, lambda j: cm[:, j, :].bitcast(F32)).then_inc(s["combT"], 1)

            def out_T(s, count):
                pe.wait_ge(s, count)
                transpose4(TB, lambda j: yT[:, j * P:(j + 1) * P]).then_inc(s_oT, 1)

            def ahead(s, n, p):
                pe.wait_ge(s["xn"], n + 1)
                transpose4(bank[6 + p], lambda j: xn[:, p, j, :]).then_inc(s["T"], 1)

            def hidden(m, r, p):
                pe.wait_ge(s_xl, m + 1)
                MM(RB[0:64, :], cst("wr1"), xT[:, p, :], start=True, stop=True).then_inc(r1["hid"], 1)

            def logits1(r):
                pe.wait_ge(r1["gelu"], r + 1)
                for j in range(TILES):
                    last = MM(RB[:, j * 32:j * 32 + E1], hr[0:65, j * P:(j + 1) * P], cst("wr2", 65),
                              start=True, stop=True)
                last.then_inc(r1["logits"], 1)

            def front0(m, r, g, p):
                front_T(m, p)
                logits0(m, r, p)
                comb_T(r0, r)

            def up0(m, r, p, k):
                if k >= N0:
                    return up0(m + 1, r + 1, 1 - p, k - N0)
                M = rows(k)
                if k == 0:
                    pe.wait_ge(s_xl, m + 1)
                if k >= 2 or not is_first(r):
                    pe.wait_ge(s_silu, r * N0 + k - 1)
                three(GATE[(p + k) % 2][0:M, :], up_w(w0h, k, True), up_w(w0l, k, True), xh[:, p, :], xl[:, p, :],
                      True, True).then_inc(s_gate, 1)
                if k >= 2 or not is_first(r):
                    pe.wait_ge(s_t, r * N0 + k - 1)
                three(UP[(p + k) % 2][0:M, :], up_w(w0h, k, False), up_w(w0l, k, False), xh[:, p, :], xl[:, p, :],
                      True, True).then_inc(s_up, 1)

            def spread0(m, r, p, k):
                if k >= N0:
                    return spread0(m + 1, r + 1, 1 - p, k - N0)
                if k > PAIRS:
                    return
                if k == 0:
                    pe.wait_ge(s_ct, m + 1)
                if k >= 2:
                    pe.wait_ge(s_u, r * N0 + k - 1)
                elif not is_first(r):
                    pe.wait_ge(s_u, (r - 1) * N0 + PAIRS if k == 0 else r * N0)
                MM(CB2[(p + k) % 2][:], sel[:, k, :], combT[:, p, :], start=True, stop=True).then_inc(s_cb, 1)

            def down0(r, p, k):
                M, n = rows(k), slot0(p, k)
                if k == 0 and not is_first(r):
                    pe.wait_ge(s_yT, r)
                pe.wait_ge(s_ul, r * N0 + k + 1)
                three(Y0[:], down_w(w0h, k), down_w(w0l, k), hi[0:M, n, :], lo[0:M, n, :],
                      k == 0, k == N0 - 1).then_inc(s_dn, 1)

            def back0(m, r, g, p, nxt, to):
                kind, mn, rn, gn, pn = nxt or (None,) * 5
                last = N0 if kind == 0 else 0
                if is_first(g):
                    up0(m, r, p, 0)
                    up0(m, r, p, 1)
                    spread0(m, r, p, 0)
                for k in range(N0):
                    if k + 1 < N0:
                        spread0(m, r, p, k + 1)
                    if k + 2 < N0 + last:
                        up0(m, r, p, k + 2)
                    if k + 1 == N0 and last:
                        spread0(m, r, p, N0)
                    if k:
                        down0(r, p, k - 1)
                    elif not is_first(g):
                        down0(r - 1, 1 - p, N0 - 1)
                    if k == 1 and not is_first(g):
                        out_T(s_yT, r)
                    if nxt and k == 2:
                        pe.wait_ge(s_xo, m + 1)
                        front_T(mn, pn)
                    if nxt and k == 4:
                        logits0(mn, rn, pn) if kind == 0 else hidden(mn, rn, pn)
                    if kind == 1 and k == 5:
                        logits1(rn)
                    if nxt and k == 9:
                        comb_T(ROUTE[kind], rn)
                if to == 0:
                    pe.wait_ge(s_xo, m + 1)
                    ahead(a0, 0, 0)

            def finish0(m, r, g):
                down0(r, g % 2, N0 - 1)
                if m == GROUPS - 1:
                    pe.wait_ge(a0["hT"], 1)
                out_T(s_yT, r + 1)

            def front1(m, r, g, p):
                front_T(m, p)
                hidden(m, r, p)
                logits1(r)
                comb_T(r1, r)

            def up1(m, r, p, kk):
                if kk >= N1:
                    return up1(m + 1, r + 1, 1 - p, kk - N1)
                if kk == 0:
                    pe.wait_ge(s_xl, m + 1)
                ws = slice(kk * P, (kk + 1) * P)
                three(RINGB[kk % RING][:], w1h[:, ws], w1l[:, ws], xh[:, p, :], xl[:, p, :], True, True).then_inc(s1_up, 1)

            def back1(m, r, g, p, nxt, to):
                def down(kk):
                    e, c = divmod(kk, CH1)
                    first = is_first(r)
                    if c == 0:
                        if e >= 1 or not first:
                            pe.wait_ge(s1_cb, r * E1 + e)
                        if e >= 2 or not first:
                            pe.wait_ge(s1_term, r * E1 + e - 1)
                        MM(CB[:], sel[:, PAIRS + 1 + e, :], combT[:, p, :], start=True, stop=True).then_inc(s1_cbp, 1)
                    ws = slice(kk * P, (kk + 1) * P)
                    pe.wait_ge(s1_lo, r * N1 + kk + 1)
                    last = three(YB[e % 2][:], w2h[:, ws], w2l[:, ws], hi[:, kk % RING, :], lo[:, kk % RING, :],
                                 c == 0, c == CH1 - 1)
                    if c == CH1 - 1:
                        last.then_inc(s1_Y, 1)

                if is_first(g):
                    for kk in range(RING - 1):
                        up1(m, r, p, kk)
                for kk in range(N1):
                    if kk + RING - 1 < N1 or nxt:
                        up1(m, r, p, kk + RING - 1)
                    if kk == 0:
                        pe.wait_ge(s_ct, m + 1)
                    down(kk)
                    if kk == 1 and not is_first(g):
                        out_T(s1_acc, r * (E1 - 1))
                    if nxt and kk == 8:
                        pe.wait_ge(s_xo, m + 1)
                        front_T(m + 1, 1 - p)
                    if to == 1 and kk == 8:
                        pe.wait_ge(s_xo, m + 1)
                        ahead(a1, 0, 0)
                    if nxt and kk == 12:
                        hidden(m + 1, r + 1, 1 - p)
                    if nxt and kk == 15:
                        logits1(r + 1)
                    if nxt and kk == 26:
                        comb_T(r1, r + 1)

            def finish1(m, r, g):
                if m == 3 * GROUPS - 1:
                    pe.wait_ge(a1["xT"], 1)
                out_T(s1_acc, (r + 1) * (E1 - 1))

            def tok_major(dst, src, w, bias=None):
                if bias:
                    row = cst(bias, 1).unsqueeze(1).broadcast_to([1, TILES, D])
                    MM(dst[:], cst("ones_row", 1), row, start=True, stop=False)
                for j in range(TILES):
                    last = MM(dst[:, j * D:(j + 1) * D], src[:, j * P:(j + 1) * P], w, start=not bias,
                              stop=(not bias or j == TILES - 1))
                return last

            def attn0():
                tri0, tri1 = cst("tri0"), cst("tri1")

                def w(p, j):
                    return work[:, p, 2, j * D:(j + 1) * D]

                def pool(n, p):
                    pe.wait_ge(a0["wq"], n + 1)
                    pe.wait_ge(a0["kT"], n + 1)
                    for b in (0, 1):
                        MM(bank[2 + p][:, b * SEQ:(b + 1) * SEQ], w(p, 2 * b), tri0, start=True, stop=False)
                        last = MM(bank[2 + p][:, b * SEQ + P:(b + 1) * SEQ], w(p, 2 * b + 1), tri1, start=False, stop=True)
                    last.then_inc(a0["pool"], 1)

                def mixed_keys(n, p):
                    pe.wait_ge(a0["mixed"], n + 1)
                    mixed = attn[:, 1, p, :]
                    tok_major(bank[p], mixed, cst("wka"), "bka_row").then_inc(a0["l2"], 1)
                    transpose4(bank[4 + p], lambda j: mixed[:, j * P:(j + 1) * P]).then_inc(a0["mixt"], 1)

                def pool_keys(n, p):
                    pe.wait_ge(a0["w2"], n + 1)
                    dst = lambda j: bank[2 + p][:, j * D:(j + 1) * D]
                    for b in (0, 1):
                        MM(dst(2 * b), tri0[:, 0:P], w(p, 2 * b), start=True, stop=True)
                        MM(dst(2 * b + 1), tri0[:, P:SEQ], w(p, 2 * b), start=True, stop=False)
                        last = MM(dst(2 * b + 1), tri1, w(p, 2 * b + 1), start=False, stop=True)
                    last.then_inc(a0["pk"], 1)

                def step(n, p, second, norm):
                    pe.wait_ge(a0["hT"], n + 1)
                    if not (isinstance(n, int) and n < 2):
                        pe.wait_ge(a0["two"], (n - 1) * 4)
                    MM(bank[p][:], cst("wq"), xT[:, p, :], start=True, stop=True).then_inc(a0["q"], 1)
                    MM(bank[2 + p][:], cst("wk"), xT[:, p, :], start=True, stop=True).then_inc(a0["k"], 1)
                    if second:
                        pool(n - 1, 1 - p)
                    tok_major(bank[6 + p], xT[:, p, :], cst("wv"), "bv_row").then_inc(a0["v"], 1)
                    if second:
                        mixed_keys(n - 1, 1 - p)
                    pe.wait_ge(a0["qT"], n + 1)
                    tok_major(bank[p], attn[:, 0, p, :], cst("wqa"), "bqa_row").then_inc(a0["l1"], 1)
                    tok_major(bank[4 + p], xT[:, p, :], cst("wq"), "bq_row").then_inc(a0["qt"], 1)
                    if norm:
                        ahead(a0, n + 1, 1 - p)
                    else:
                        pe.wait_ge(a0["vc"], n)
                        front_T(GROUPS, 0)
                    if second:
                        pool_keys(n - 1, 1 - p)

                def finish(n, p):
                    pool(n, p)
                    logits0(GROUPS, GROUPS, 0)
                    mixed_keys(n, p)
                    pool_keys(n, p)
                    comb_T(r0, GROUPS)
                    pe.wait_ge(a0["two"], 4 * GROUPS)

                pe.wait_ge(s_xo, GROUPS + 1)
                attn_groups(pe, step, finish)

            def attn1():
                def weights_T(n, p):
                    pe.wait_ge(a1["a"], n + 1)
                    for j in range(TILES):
                        for h in (0, 1):
                            at = (j % 2) * SEQ + h * P
                            last = nc.tensor.transpose(bank[2 + 4 * h + p][:, j * P:(j + 1) * P],
                                                       work[:, p, 2 + j // 2, at:at + P], ident)
                    last.then_inc(a1["aT"], 1)

                def apply(n, p):
                    pe.wait_ge(a1["aTc"], n + 1)
                    pe.wait_ge(a1["xnc"], n + 1)
                    v = lambda j: comb_bc[:, p, j * D:(j + 1) * D]
                    for j in range(TILES):
                        b = j // 2
                        dst = bank[p][:, j * D:(j + 1) * D]
                        MM(dst, ident, v(j), start=True, stop=False)
                        for h in (0, 1):
                            last = MM(dst, attn[:, 1, 2 * p + h, j * P:(j + 1) * P], v(2 * b + h),
                                      start=False, stop=(h == 1))
                    last.then_inc(a1["o"], 1)

                def step(n, p, second, norm):
                    pe.wait_ge(a1["xT"], n + 1)
                    if not (isinstance(n, int) and n < 2):
                        pe.wait_ge(a1["two"], n - 1)
                    MM(bank[p][:], cst("wq1"), xT[:, p, :], start=True, stop=True).then_inc(a1["q"], 1)
                    MM(bank[2 + p][:], cst("wk1"), xT[:, p, :], start=True, stop=True).then_inc(a1["k"], 1)
                    if second:
                        weights_T(n - 1, 1 - p)
                    pe.wait_ge(a1["qT"], n + 1)
                    pe.wait_ge(a1["kT"], n + 1)
                    for j in range(TILES):
                        b = j // 2
                        last = MM(bank[4 * b + p][:, (j % 2) * SEQ:(j % 2 + 1) * SEQ], attn[:, 0, p, j * P:(j + 1) * P],
                                  attn[:, 0, 2 + p, b * SEQ:(b + 1) * SEQ], start=True, stop=True)
                    last.then_inc(a1["s"], 1)
                    if second:
                        apply(n - 1, 1 - p)
                    if norm:
                        ahead(a1, n + 1, 1 - p)
                    else:
                        front_T(3 * GROUPS, 0)

                def finish(n, p):
                    hidden(3 * GROUPS, GROUPS, 0)
                    weights_T(n, p)
                    logits1(GROUPS)
                    apply(n, p)
                    comb_T(r1, GROUPS)
                    pe.wait_ge(a1["two"], GROUPS)

                pe.wait_ge(s_xo, 3 * GROUPS + 1)
                attn_groups(pe, step, finish)

            pe.wait_ge(s_small, 16)
            pe.wait_ge(s_sel, 1)
            pe.wait_ge(s_wl, W0_PARTS)
            pe.wait_ge(s_hr1, 1)
            ffn_groups(pe, 0, 0, 0, front0, back0, finish0, to=0)
            pe.wait_ge(s_small2, 16)
            attn0()
            ffn_groups(pe, 1, 0, 1, front0, back0, finish0, then=THEN_FFN1, fronted=True)
            pe.wait_ge(s_w12l, 2 * GROUPS)
            ffn_groups(pe, 2, 1, 0, front1, back1, finish1, fronted=True, to=1)
            attn1()
            ffn_groups(pe, 3, 1, 1, front1, back1, finish1, fronted=True)

        @block.vector
        def _(dve):
            V = nc.vector
            V.memset(hr[64:65, :], 1.0).then_inc(s_hr1, 1)
            V.memset(cm[:].bitcast(F32), 0.0).then_inc(s_xo, 1)
            for n in range(W0_PARTS):
                part = slice(n * W0_PART, (n + 1) * W0_PART)
                dve.wait_ge(s_wh, n + 1)
                V.tensor_tensor(w0l[:, part], w0raw[:, part], w0h[:, part].bitcast(F32), ALU.subtract).then_inc(s_wl, 1)
            dve.wait_ge(s_small, 16)
            dve.wait_ge(s_x0, 16)
            dve.wait_ge(s_xo, 1)

            def variance(ch, src, p):
                for j in range(TILES):
                    last = V.bn_stats(st[:, p, j, :], src(j))
                ch.mark(last)
                yield
                ch.need()
                V.memset(hold[:], 0.0)
                for j in range(TILES):
                    last = V.bn_aggr(mv[:, p, j, :], st[:, p, j, :])
                ch.mark(last)
                yield
                ch.need()

            def plus_eps(p):
                return V.tensor_scalar(ve[:, p, :], mv[:, p, :, 1], EPS, None, ALU.add)

            def normed(src, p):
                for j in range(TILES):
                    last = V.tensor_scalar(xn[:, p, j:j + 1, :], src(j), mv[:, p, j, 0:1], rstd[:, p, j:j + 1],
                                           ALU.subtract, ALU.mult)
                return last

            def stats(ch, m, g, p):
                yield from variance(ch, lambda j: tile_of(g, j), p)
                plus_eps(p).then_inc(s_ve, 1)

            def norm(m, g, p):
                dve.wait_ge(s_rstd, m + 1)
                normed(lambda j: tile_of(g, j), p).then_inc(s_xn, 1)

            def split(m, p):
                dve.wait_ge(s_xh, m + 1)
                V.tensor_tensor(xl[:, p, :], TB[:], xh[:, p, :].bitcast(F32), ALU.subtract).then_inc(s_xl, 1)

            def tab(i, w):
                return rt[:, i, 0:TILES * w].rearrange("p (j e) -> p j e", j=TILES)

            def route_max(ch, s, r, E, w):
                lg = RB[:, 0:TILES * 32].rearrange("p (j e) -> p j e", j=TILES)
                dve.wait_ge(s["logits"], r + 1)
                ch.mark(V.tensor_reduce(rmx[:, 0, :], lg[:, :, 0:E], AX_X, ALU.max))
                if w > E:
                    V.tensor_scalar(gates[:, 0, TILES:], lg[:, :, E], -1.0, None, ALU.mult)
                yield
                ch.need()
                ins = V.tensor_tensor(tab(0, E), lg[:, :, 0:E], over(rmx[:, 0, :], E), ALU.subtract)
                if w > E:
                    ch.mark(ins)
                    yield
                    ch.need()
                else:
                    ins.then_inc(s["d"], 1)
                    yield
                    dve.wait_ge(s["d"], r + 1)

            def route_top2(ch, s, r, E, w):
                d = tab(0, E)
                tie = cst("tie").rearrange("p (j e) -> p j e", j=TILES)[:, :, 0:E]
                ch.mark(V.scalar_tensor_tensor(tab(2, E), d, 0.0, tie, ALU.is_ge, ALU.mult))
                yield
                ch.need()
                ch.mark(V.tensor_reduce(rmx[:, 1, :], tab(2, E), AX_X, ALU.max))
                yield
                ch.need()
                ch.mark(V.tensor_tensor(tab(3, E), tab(2, E), over(rmx[:, 1, :], E), ALU.is_equal))
                yield
                ch.need()
                ch.mark(V.scalar_tensor_tensor(tab(4, E), tab(3, E), -BIG, d, ALU.mult, ALU.add))
                yield
                ch.need()
                if w > E:
                    V.tensor_reduce(gates[:, 0, 0:TILES], tab(4, E), AX_X, ALU.max).then_inc(s["d"], 1)
                    yield
                    dve.wait_ge(s["d"], r + 1)
                else:
                    ch.mark(V.tensor_reduce(gates[:, 0, 0:TILES], tab(4, E), AX_X, ALU.max))
                    yield
                    ch.need()
                ch.mark(V.tensor_tensor(tab(5, E), tab(4, E), over(gates[:, 0, 0:TILES], E), ALU.is_equal))
                yield
                ch.need()
                ch.mark(V.tensor_tensor(tab(5, E), tab(5, E), tie, ALU.mult))
                yield
                ch.need()
                ch.mark(V.tensor_reduce(rmx[:, 3, :], tab(5, E), AX_X, ALU.max))
                yield
                ch.need()
                ch.mark(V.tensor_tensor(tab(6, E), tab(5, E), over(rmx[:, 3, :], E), ALU.is_equal))
                yield
                ch.need()

            def comb_parts(ch, s, src, w):
                ch.mark(V.tensor_scalar(cm[:, :, 0:w], src, 0.5, None, ALU.mult))
                yield
                ch.need()
                V.scalar_tensor_tensor(cm[:, :, LO:LO + w], src, 0.5, cm[:, :, 0:w].bitcast(F32), ALU.mult,
                                       ALU.subtract).then_inc(s["comb"], 1)

            def route0(ch, r):
                yield from route_max(ch, r0, r, E0, E0 + 1)
                yield from route_top2(ch, r0, r, E0, E0 + 1)
                dve.wait_ge(r0["exp"], r + 1)
                first, shared = gates[:, 0, 0:TILES], gates[:, 0, TILES:]
                ch.mark(V.tensor_scalar(gates[:, 2, :], gates[:, 1, :], 1.0, None, ALU.add))
                yield
                ch.need()
                ch.mark(V.reciprocal(gates[:, 0, :], gates[:, 2, :]))
                yield
                ch.need()
                V.tensor_tensor(tab(4, E0), tab(3, E0), over(first, E0), ALU.mult)
                V.tensor_scalar(tab(7, E0 + 1)[:, :, E0], shared, 1.0, None, ALU.mult)
                ch.mark(V.tensor_tensor(rmx[:, 5, :], gates[:, 1, 0:TILES], first, ALU.mult))
                yield
                ch.need()
                ch.mark(V.tensor_tensor(tab(5, E0), tab(6, E0), over(rmx[:, 5, :], E0), ALU.mult))
                yield
                ch.need()
                ch.mark(V.tensor_tensor(tab(7, E0 + 1)[:, :, 0:E0], tab(4, E0), tab(5, E0), ALU.add))
                yield
                ch.need()
                yield from comb_parts(ch, r0, tab(7, E0 + 1), E0 + 1)
                assert ch.n == K0C, ch.n

            def route1(ch, r):
                yield from route_max(ch, r1, r, E1, E1)
                yield from route_top2(ch, r1, r, E1, E1)
                ch.mark(V.tensor_tensor(tab(3, E1), tab(3, E1), tab(6, E1), ALU.add))
                yield
                ch.need()
                dve.wait_ge(r1["exp"], r + 1)
                ex = tab(1, E1)
                V.tensor_reduce(rmx[:, 5, :], ex, AX_X, ALU.add)
                ch.mark(V.tensor_tensor(tab(4, E1), ex, tab(3, E1), ALU.mult))
                yield
                ch.need()
                ch.mark(V.reciprocal(rmx[:, 6, :], rmx[:, 5, :]))
                yield
                ch.need()
                ch.mark(V.tensor_tensor(tab(7, E1), tab(4, E1), over(rmx[:, 6, :], E1), ALU.mult))
                yield
                ch.need()
                yield from comb_parts(ch, r1, tab(7, E1), E1)
                assert ch.n == K1C, ch.n

            def all_of(steps):
                for _ in steps:
                    pass

            def add_out(g, n):
                dve.wait_ge(s_oT, n)
                V.tensor_tensor(group_of(g), group_of(g), t4(TB[:]), ALU.add).then_inc(s_xo, 1)

            def front0(m, r, g, p):
                ch = Chain(dve, r0["chain"], r * K0C)
                all_of(stats(ch, m, g, p))
                norm(m, g, p)
                split(m, p)
                all_of(route0(ch, r))
                if isinstance(m, int) and m == 0:
                    dve.wait_ge(s_x1, 16)

            def layer_norms(n, p):
                ch = Chain(dve, a0["ln"], n * 5)
                yield from variance(ch, lambda j: tile_of(n, j), p)
                plus_eps(p).then_inc(a0["ve1"], 1)
                yield
                dve.wait_ge(a0["rstd1"], n + 1)
                ch.mark(normed(lambda j: tile_of(n, j), p))
                yield
                ch.need()
                yield from variance(ch, lambda j: xn[:, p, j, :], p)
                plus_eps(p).then_inc(a0["ve2"], 1)
                yield
                dve.wait_ge(a0["rstd2"], n + 1)
                normed(lambda j: xn[:, p, j:j + 1, :], p).then_inc(a0["xn"], 1)

            def layer_norm(n, p):
                ch = Chain(dve, a1["ln"], n * 2)
                yield from variance(ch, lambda j: tile_of(n, j), p)
                plus_eps(p).then_inc(a1["ve1"], 1)
                yield
                dve.wait_ge(a1["rstd1"], n + 1)
                normed(lambda j: tile_of(n, j), p).then_inc(a1["xn"], 1)

            def some(steps, n):
                for _ in range(n):
                    next(steps, None)

            def back0(m, r, g, p, nxt, to):
                kind, mn, rn, gn, pn = nxt or (None,) * 5
                if nxt:
                    ch = Chain(dve, ROUTE[kind]["chain"], rn * (K0C, K1C)[kind])
                    ahead = stats(ch, mn, gn, pn)
                    routing = (route0, route1)[kind](ch, rn)
                for k in range(N0):
                    M, n = rows(k), slot0(p, k)
                    S, U = work[0:M, 0, n, :], work[0:M, 1, n, :]
                    dve.wait_ge(s_silu, r * N0 + k + 1)
                    dve.wait_ge(s_up, r * N0 + k + 1)
                    V.tensor_tensor(S, S, UP[(p + k) % 2][0:M, :], ALU.mult).then_inc(s_t, 1)
                    if nxt:
                        if k <= 1:
                            some(ahead, 1)
                        if k >= 6 + kind:
                            some(routing, 2)
                    dve.wait_ge(s_cb, r * (PAIRS + 1) + min(k, PAIRS) + 1)
                    dve.wait_ge(s_t, r * N0 + k + 1)
                    if soon0(p, k) and not (isinstance(g, int) and g == 0 and k < 3):
                        dve.wait_ge(s_ul, r * N0 + k - 2)
                    V.tensor_tensor(U, S, CB2[(p + min(k, PAIRS)) % 2][0:M, :], ALU.mult).then_inc(s_u, 1)
                    if nxt and k == 0:
                        all_of(ahead)
                    if nxt and k == 1:
                        norm(mn, gn, pn)
                    if k == 2 and (not isinstance(g, int) or g > 0):
                        add_out(g - 1, m)
                    if nxt and k == 4:
                        split(mn, pn)
                    if nxt and k >= 5 + kind:
                        some(routing, 3)
                    if nxt and k == 9:
                        all_of(routing)
                    if to == 0 and k == 2:
                        norms = layer_norms(0, 0)
                        dve.wait_ge(s_xo, m + 1)
                    if to == 0 and k >= 3:
                        some(norms, 1)

            def finish(m, r, g):
                add_out(g, m + 1)

            def front1(m, r, g, p):
                ch = Chain(dve, r1["chain"], r * K1C)
                all_of(stats(ch, m, g, p))
                norm(m, g, p)
                split(m, p)
                all_of(route1(ch, r))

            def back1(m, r, g, p, nxt, to):
                NA = len(HI_BY_ACT)
                ND = CH1 - NA
                seen_a = seen_d = 0
                if nxt:
                    ch = Chain(dve, r1["chain"], (r + 1) * K1C)
                    ahead = stats(ch, m + 1, g + 1, 1 - p)
                    routing = route1(ch, r + 1)
                for kk in range(N1):
                    e, c = divmod(kk, CH1)
                    he, h, l = work[:, 0, kk % RING, :], hi[:, kk % RING, :], lo[:, kk % RING, :]
                    dve.wait_ge(s1_he, r * N1 + kk + 1)
                    if c in HI_BY_ACT:
                        seen_a += 1
                        dve.wait_ge(s1_hiA, r * (E1 * NA) + seen_a)
                    else:
                        seen_d += 1
                        V.tensor_scalar(h, he, 1.0, None, ALU.mult).then_inc(s1_hiD, 1)
                        if nxt and 3 <= kk <= 7:
                            next(ahead, None)
                        if nxt and kk >= 19:
                            next(routing, None)
                        dve.wait_ge(s1_hiD, r * (E1 * ND) + seen_d)
                    V.tensor_tensor(l, he, h.bitcast(F32), ALU.subtract).then_inc(s1_lo, 1)
                    if c == 3 and e:
                        weigh(r, e - 1)
                    if kk == 5 and (not isinstance(g, int) or g > 0):
                        add_out(g - 1, m)
                    if to == 1 and kk == 5:
                        norms = layer_norm(0, 0)
                        dve.wait_ge(s_xo, m + 1)
                    if to == 1 and 6 <= kk <= 8:
                        some(norms, 1)
                    if to == 1 and kk == 9:
                        all_of(norms)
                    if nxt and kk == 7:
                        all_of(ahead)
                    if nxt and kk == 9:
                        norm(m + 1, g + 1, 1 - p)
                    if nxt and kk == 13:
                        split(m + 1, 1 - p)
                    if nxt and 19 <= kk < 27:
                        next(routing, None)
                        next(routing, None)
                    if nxt and kk == 27:
                        all_of(routing)
                weigh(r, E1 - 1)

            def weigh(r, e):
                dve.wait_ge(s1_Y, r * E1 + e + 1)
                dve.wait_ge(s1_cb, r * E1 + e + 1)
                if e >= 3:
                    dve.wait_ge(s1_acc, r * (E1 - 1) + e - 2)
                dst = term[:, e % 2, :] if e else yT[:]
                b = SMALL_AT["b2"][0] + e
                V.scalar_tensor_tensor(dst, YB[e % 2][:], small[:, b:b + 1], comb_bc[:, e % 2, :], ALU.add,
                                       ALU.mult).then_inc(s1_term, 1)

            def first_norm(m, r, p):
                first = 0 if m == GROUPS else 1
                ch = Chain(dve, ROUTE[first]["chain"], r * (K0C, K1C)[first])
                yield from stats(ch, m, 0, p)
                yield
                norm(m, 0, p)

            def in_turns(*all_steps):
                left = list(all_steps)
                while left:
                    for steps in list(left):
                        if next(steps, all_steps) is all_steps:
                            left.remove(steps)

            def attn0():
                s = a0

                def maximum(ch, n, p, lsem, dsem):
                    dve.wait_ge(s[lsem], n + 1)
                    ch.mark(V.tensor_reduce(mx[:, 2 + p, :], t4(bank[p][:]), AX_X, ALU.max))
                    yield
                    ch.need()
                    V.tensor_scalar(mx[:, p, :], mx[:, 2 + p, :], -INV, None, ALU.mult).then_inc(s[dsem], 1)

                def weights(ch, n, p, esem, bysem, wsem):
                    dve.wait_ge(s[esem], n + 1)
                    ch.mark(V.reciprocal(rinv[:, p, :], rsum[:, p, :]))
                    yield
                    ch.need()
                    dve.wait_ge(s[bysem], n + 1)
                    for j in range(TILES):
                        cols = slice(j * D, (j + 1) * D)
                        last = V.scalar_tensor_tensor(work[:, p, 2, cols], work[:, p, 1, cols], rinv[:, p, j:j + 1],
                                                      bank[4 + p][:, cols], ALU.mult, ALU.mult)
                    last.then_inc(s[wsem], 1)

                def mix(n, p):
                    dve.wait_ge(s["pool"], n + 1)
                    V.tensor_tensor(attn[:, 1, p, :], bank[2 + p][:], attn[:, 0, 2 + p, :], ALU.mult)\
                        .then_inc(s["mixed"], 1)

                def update(ch, n, p):
                    dve.wait_ge(s["vc"], n + 1)
                    dve.wait_ge(s["pk"], n + 1)
                    ch.mark(V.tensor_tensor(term[:, p, :], bank[2 + p][:], comb_bc[:, p, :], ALU.mult))
                    yield
                    ch.need()
                    ch.mark(V.tensor_tensor(group_of(n), group_of(n), t4(term[:, p, :]), ALU.add))

                def step(n, p, second, norm):
                    one, two = Chain(dve, s["one"], n * 2), Chain(dve, s["two"], (n - 1) * 4)
                    norms = layer_norms(n + 1, 1 - p) if norm else first_norm(GROUPS, GROUPS, 0)
                    if second:
                        mix(n - 1, 1 - p)
                    some(norms, 3)
                    if second:
                        in_turns(maximum(two, n - 1, 1 - p, "l2", "d2"))
                    some(norms, 3)
                    if second:
                        in_turns(weights(two, n - 1, 1 - p, "e2", "mixt", "w2"))
                    all_of(norms)
                    in_turns(maximum(one, n, p, "l1", "d1"))
                    if second:
                        in_turns(update(two, n - 1, 1 - p))
                    in_turns(weights(one, n, p, "e1", "qt", "wq"))
                    if second:
                        two.need()
                    if not norm:
                        split(GROUPS, 0)

                def finish(n, p):
                    two = Chain(dve, s["two"], n * 4)
                    routing = route0(Chain(dve, r0["chain"], GROUPS * K0C, 2), GROUPS)
                    mix(n, p)
                    some(routing, 4)
                    in_turns(maximum(two, n, p, "l2", "d2"))
                    some(routing, 5)
                    in_turns(weights(two, n, p, "e2", "mixt", "w2"))
                    all_of(routing)
                    in_turns(update(two, n, p))
                    two.need()

                attn_groups(dve, step, finish)

            def attn1():
                s = a1

                def maximum(ch, n, p):
                    dve.wait_ge(s["s"], n + 1)
                    for b in (0, 1):
                        last = V.tensor_reduce(mx[:, 2 + p, 2 * b:2 * b + 2],
                                               bank[4 * b + p][:].rearrange("q (j t) -> q j t", j=2), AX_X, ALU.max)
                    ch.mark(last)
                    yield
                    ch.need()
                    V.tensor_scalar(mx[:, p, :], mx[:, 2 + p, :], -INV, None, ALU.mult).then_inc(s["nmax"], 1)

                def weights(ch, n, p):
                    dve.wait_ge(s["e"], n + 1)
                    ch.mark(V.reciprocal(rinv[:, p, :], rsum[:, p, :]))
                    yield
                    ch.need()
                    ch.mark(V.tensor_tensor(mx[:, 4 + p, :], rsum[:, p, :], rinv[:, p, :], ALU.mult))
                    yield
                    ch.need()
                    ch.mark(V.tensor_scalar(mx[:, 6 + p, :], mx[:, 4 + p, :], 1.0, 1.0 / SEQ, ALU.add, ALU.mult))
                    yield
                    ch.need()
                    for j in range(TILES):
                        cols = slice((j % 2) * SEQ, (j % 2 + 1) * SEQ)
                        last = V.tensor_scalar(work[:, p, 2 + j // 2, cols], work[:, p, j // 2, cols],
                                               rinv[:, p, j:j + 1], mx[:, 6 + p, j:j + 1], ALU.mult, ALU.subtract)
                    last.then_inc(s["a"], 1)

                def update(n, p):
                    dve.wait_ge(s["o"], n + 1)
                    V.tensor_tensor(group_of(n), group_of(n), t4(bank[p][:]), ALU.add).then_inc(s["two"], 1)

                def step(n, p, second, norm):
                    one = Chain(dve, s["one"], n * 4)
                    norms = layer_norm(n + 1, 1 - p) if norm else first_norm(3 * GROUPS, GROUPS, 0)
                    some(norms, 3)
                    in_turns(maximum(one, n, p), norms)
                    if second:
                        update(n - 1, 1 - p)
                    in_turns(weights(one, n, p))
                    if not norm:
                        split(3 * GROUPS, 0)

                def finish(n, p):
                    routing = route1(Chain(dve, r1["chain"], GROUPS * K1C, 2), GROUPS)
                    all_of(routing)
                    update(n, p)
                    dve.wait_ge(s["two"], n + 1)

                attn_groups(dve, step, finish)

            ffn_groups(dve, 0, 0, 0, front0, back0, finish, to=0)
            dve.wait_ge(s_xo, 1 + GROUPS)
            attn0()
            ffn_groups(dve, 1, 0, 1, front0, back0, finish, then=THEN_FFN1, fronted=True)
            dve.wait_ge(s_xo, 1 + 2 * GROUPS)
            ffn_groups(dve, 2, 1, 0, front1, back1, finish, fronted=True, to=1)
            dve.wait_ge(s_xo, 1 + 3 * GROUPS)
            attn1()
            ffn_groups(dve, 3, 1, 1, front1, back1, finish, fronted=True)


K0C, K1C = 18, 17


def kernel(**inputs):
    import numpy as np
    import concourse.bacc as bacc
    from concourse import mybir as mb
    from concourse.bass_utils import run_bass_kernel_spmd as run

    a = {k: np.asarray(v) for k, v in inputs.items()}

    def col(v):
        out = np.zeros((P, 1), np.float32)
        out[:v.shape[0], 0] = v
        return out

    def block_of(v, width):
        out = np.zeros((P, width), np.float32)
        out[:v.shape[0], :v.shape[1]] = v
        return out

    tok = np.arange(SEQ)
    mean_to = (tok[:, None] <= tok[None, :]) / (tok[None, :] + 1.0)
    tie = np.tile(np.arange(E0, 0, -1, dtype=np.float32), TILES)
    sel0 = np.zeros((64, PAIRS + 1, P), np.float32)
    sel1 = np.zeros((64, E1, P), np.float32)
    for base in (0, LO):
        for k in range(PAIRS):
            sel0[base + 2 * k, k, 0:F0] = 1
            sel0[base + 2 * k + 1, k, F0:P] = 1
        sel0[base + E0, PAIRS, :] = 1
        for e in range(E1):
            sel1[base + e, e, :] = 1

    wr2 = np.concatenate([a["L1_ffn_Wr2"].T, a["L1_ffn_br2"][None, :]], axis=0)
    parts = {
        "gate0": np.concatenate([a["L0_ffn_gate_w"].T, a["L0_ffn_shared_gate_w"].T], axis=1),
        "wr1": a["L1_ffn_Wr1"].T, "wr2": block_of(wr2, E1),
        "b1": a["L1_ffn_b1"].reshape(N1, P).T, "b2": a["L1_ffn_b2"].T, "br1": col(a["L1_ffn_br1"]),
        "gamma": col(a["L0_attn_gamma"]), "beta": col(a["L0_attn_beta"]),
        "bq": col(a["L0_attn_bq"]), "bk": col(a["L0_attn_bk"]),
        "wq": a["L0_attn_Wq"], "wqa": a["L0_attn_Wqa"], "wk": a["L0_attn_Wk"], "wka": a["L0_attn_Wka"],
        "wv": a["L0_attn_Wv"],
        "bq_row": np.broadcast_to(a["L0_attn_bq"], (P, D)), "bqa_row": np.broadcast_to(a["L0_attn_bqa"], (P, D)),
        "bka_row": np.broadcast_to(a["L0_attn_bka"], (P, D)), "bv_row": np.broadcast_to(a["L0_attn_bv"], (P, D)),
        "wq1": a["L1_attn_Wq"].T, "wk1": a["L1_attn_Wk"].T,
        "bq1": col(a["L1_attn_bq"]), "bk1": col(a["L1_attn_bk"]),
        "ones_row": np.ones((P, P)), "ident": np.eye(P), "tri0": mean_to[0:P, :], "tri1": mean_to[P:SEQ, P:SEQ],
        "tie": np.broadcast_to(tie, (P, TILES * E0)),
    }
    small = np.concatenate([np.asarray(parts[n], np.float32) for n, _ in SMALL], axis=1)

    gu = a["L0_ffn_w_gate_up"]
    shared_down = np.zeros((len(SH_ROWS) * P, D), np.float32)
    shared_down[:SHARED] = a["L0_ffn_shared_w_down"].T
    w0 = np.concatenate([
        gu[:, :, :F0].transpose(1, 0, 2).reshape(D, -1), gu[:, :, F0:].transpose(1, 0, 2).reshape(D, -1),
        a["L0_ffn_w_down"].reshape(PAIRS, P, D).transpose(1, 0, 2).reshape(P, -1),
        a["L0_ffn_shared_w_gate"].T, a["L0_ffn_shared_w_up"].T,
        shared_down.reshape(-1, P, D).transpose(1, 0, 2).reshape(P, -1),
    ], axis=1)
    w1 = a["L1_ffn_W1"].transpose(2, 0, 1).reshape(D, -1)
    w2 = a["L1_ffn_W2"].transpose(0, 2, 1).reshape(E1 * CH1, P, D).transpose(1, 0, 2).reshape(P, -1)

    sel = np.concatenate([sel0, sel1], axis=1)
    arrays = {"x": a["L0_attn_hidden_states"], "small_all": small, "sel_of": sel, "w0_all": w0, "w1_all": w1, "w2_all": w2}
    arrays = {k: np.ascontiguousarray(v) for k, v in arrays.items()}
    nc = bacc.Bacc("TRN2", target_bir_lowering=False, num_devices=1)
    args = [nc.dram_tensor(n, v.shape, mb.dt.from_np(v.dtype), kind="ExternalInput").ap() for n, v in arrays.items()]
    args.append(nc.dram_tensor("out", arrays["x"].shape, F32, kind="ExternalOutput").ap())
    program(nc, *args)
    r = run(nc, [arrays], core_ids=[0])
    return r.results[0]["out"]
```

```python
import math
from contextlib import ExitStack

import concourse.bass as bass
from concourse import mybir

ALU = mybir.AluOpType
ACT = mybir.ActivationFunctionType
F32 = mybir.dt.float32
F32R = mybir.dt.float32r
AX_X = mybir.AxisListType.X

P = 128
D = 128
TILES = 4
GTOK = TILES * P
SEQ = 256
GROUPS = 8
E0, F0 = 16, 64
PAIRS = E0 // 2
SHARED = 352
SH_ROWS = [128, 128, 96]
N0 = PAIRS + len(SH_ROWS)
E1, H1 = 8, 512
CH1 = H1 // P
N1 = E1 * CH1
RING = 4
LO = 32
HI_BY_ACT = (1, 3)
EPS = 1e-5
BIG = 1.0e30
INV = float(D) ** -0.5
C_G, C_H, C_D = 0, E0 * F0, 2 * E0 * F0
C_SG = C_D + PAIRS * D
C_SU, C_SD = C_SG + SHARED, C_SG + 2 * SHARED
W0_COLS = C_SD + len(SH_ROWS) * D
W1_COLS = E1 * H1
EIGHTH = W1_COLS // GROUPS
W0_PARTS = 4
W0_PART = W0_COLS // W0_PARTS

SMALL = [
    ("ident", P), ("gate0", E0 + 1), ("tie", TILES * E0),
    ("wr1", 64), ("wr2", E1), ("b1", N1), ("b2", E1), ("br1", 1), ("gamma", 1), ("beta", 1),
    ("bq", 1), ("bk", 1), ("wq", D), ("wqa", D), ("wk", D), ("wka", D), ("wv", D), ("bqa_row", D),
    ("bka_row", D), ("bv_row", D), ("wq1", D), ("wk1", D), ("bq1", 1), ("bk1", 1), ("tri0", SEQ),
    ("tri1", P),
]
FIRST_SMALL = P + E0 + 1 + TILES * E0
SMALL_AT = {}
SMALL_COLS = 0
for _n, _w in SMALL:
    SMALL_AT[_n] = (SMALL_COLS, _w)
    SMALL_COLS += _w


def program(nc, x_in, small_in, sel_in, w0_in, w1_in, w2_in, out):
    x_dram = x_in.rearrange("a (b p) d -> p (a b) d", p=P)
    out_dram = out.rearrange("a (b p) d -> p (a b) d", p=P)
    with ExitStack() as ctx:
        def sb(name, shape, dt=F32):
            return ctx.enter_context(nc.sbuf_tensor(name, shape, dt))

        def sem(name):
            return ctx.enter_context(nc.semaphore(name))

        X = sb("x_sb", [P, GROUPS * TILES, D])
        small = sb("small_sb", [P, SMALL_COLS])

        def split_weights(name, cols):
            high = sb(name + "_high", [P, cols], F32R)
            with nc.sbuf_tensor(name + "_raw", [P, cols], F32) as raw:
                pass
            return high, sb(name + "_low", [P, cols], F32R), raw

        w0h, w0l, w0raw = split_weights("w0", W0_COLS)
        w1h, w1l, w1raw = split_weights("w1", W1_COLS)
        w2h, w2l, w2raw = split_weights("w2", W1_COLS)
        work = sb("work", [P, 2, RING, GTOK])
        with nc.sbuf_tensor("attn", [P, 2, RING, GTOK], F32) as attn:
            pass
        hi = sb("hi", [P, RING, GTOK], F32R)
        lo = sb("lo", [P, RING, GTOK], F32R)
        with nc.sbuf_tensor("sel_raw", [64, PAIRS + 1 + E1, P], F32) as sel_raw:
            pass
        sel = sb("sel", [64, PAIRS + 1 + E1, P], F32R)
        xn = sb("xn", [P, 2, TILES, D])
        xT = sb("xT", [P, 2, GTOK])
        xh, xl = sb("xh", [P, 2, GTOK], F32R), sb("xl", [P, 2, GTOK], F32R)
        combT = sb("combT", [64, 2, GTOK], F32R)
        comb_bc = sb("comb_bc", [P, 2, GTOK])
        term = sb("term", [P, 2, GTOK])
        yT = sb("yT", [P, GTOK])
        hr = sb("hr", [65, GTOK])
        st = sb("st", [P, 2, TILES, 6])
        mv = sb("mv", [P, 2, TILES, 2])
        ve = sb("ve", [P, 2, TILES])
        rstd = sb("rstd", [P, 2, TILES])
        mhalf = sb("mhalf", [P, TILES])
        brow = sb("brow", [64, 3, D], F32R)
        euler = sb("euler", [P, TILES * E1])
        gates = sb("gates", [P, 3, 2 * TILES])
        cm = sb("cm", [P, TILES, P], F32R)
        hold = sb("hold", [P, 2])
        rt = sb("rt", [P, 8, TILES * (E0 + 1)])
        mx = sb("mx", [P, 8, TILES])
        rmx = sb("rmx", [P, 8, TILES])
        rsum = sb("rsum", [P, 2, TILES])
        rinv = sb("rinv", [P, 2, TILES])

        bank = [ctx.enter_context(nc.psum_tensor(f"bank{i}", [P, GTOK], F32)) for i in range(8)]
        GATE, UP = bank[0:2], bank[2:4]
        RINGB = [bank[0], bank[1], bank[2], bank[7]]
        YB = [bank[3], bank[4]]
        Y0, CB, TB, RB = bank[4], bank[5], bank[6], bank[6]
        CB2 = [bank[5], bank[7]]

        def cst(name, rows=P):
            a, w = SMALL_AT[name]
            return small[0:rows, a:a + w]

        ident = cst("ident")
        B_ROWS = SMALL_AT["bqa_row"][0]

        s_small, s_small2, s_sel_raw = sem("s_first_small_loaded"), sem("s_small_loaded"), sem("s_sel_loaded")
        s_x0, s_x1 = sem("s_first_x_loaded"), sem("s_x_loaded")
        s_raw = [sem(f"s_w0_raw{n}_loaded") for n in range(W0_PARTS)]
        s_raw1, s_raw2 = sem("s_w1_loaded"), sem("s_w2_loaded")
        s_w12h, s_w12l = sem("s_w12_high"), sem("s_w12_low")
        s_wh, s_wl = sem("s_weights_high"), sem("s_weights_low")
        s_mhalf, s_sel, s_hr1 = sem("s_minus_half"), sem("s_selectors"), sem("s_hr_ones")
        s_bhi, s_blo = sem("s_bias_rows_high"), sem("s_bias_rows_low")
        s_out = sem("s_out")
        s_ve, s_rstd, s_xn = sem("s_var_eps"), sem("s_rstd"), sem("s_xn")
        s_T, s_xh, s_xl = sem("s_xn_transposed"), sem("s_xT_high"), sem("s_xT_low")
        s_ct = sem("s_comb_transposed_copied")
        s_yT, s_xo = sem("s_yT"), sem("s_x_updated_by_ffn")
        s_oT = sem("s_out_transposed")
        r0 = {n: sem("s0_" + n) for n in ("chain", "logits", "d", "exp", "comb", "combT")}
        s_up, s_silu, s_t, s_u, s_uh, s_ul, s_dn = (sem("s0_" + n) for n in ("up", "silu", "gated", "scaled", "high", "low", "down"))
        s_gate, s_cb = sem("s0_gate"), sem("s0_comb_bc")
        r1 = {n: sem("s1_" + n) for n in ("chain", "hid", "gelu", "logits", "d", "exp", "comb", "combT")}
        s1_up, s1_he, s1_hiA, s1_hiD, s1_lo, s1_Y = (sem("s1_" + n) for n in ("up", "gelu_f", "high_act", "high_dve", "low", "down"))
        s1_cbp, s1_cb, s1_term, s1_acc = (sem("s1_" + n) for n in ("comb_bc_psum", "comb_bc", "term", "acc"))
        ROUTE, WIDTH = (r0, r1), (E0 + 1, E1)
        A0N = ("ln", "ln_of_1", "one", "two", "ve1", "rstd1", "ve2", "rstd2", "xn", "T", "hT", "q", "k", "qt", "v", "qT", "kT", "l1",
               "d1", "vc", "e1", "wq", "pool", "mixed", "l2", "mixt", "d2", "e2", "w2", "pk")
        a0 = {n: sem("a0_" + n) for n in A0N}
        A1N = ("ln", "ln_of_1", "one", "two", "ve1", "rstd1", "xn", "xnc", "T", "xT", "q", "k", "qT", "kT", "s", "nmax", "e", "a",
               "aT", "aTc", "o")
        a1 = {n: sem("a1_" + n) for n in A1N}

        block = ctx.enter_context(nc.Block())

        def tile_of(g, j):
            return X[:, bass.ds(g * TILES + j, 1), :]

        def group_of(g):
            return X[:, bass.ts(g, TILES), :]

        def t4(ap):
            return ap.rearrange("p (j d) -> p j d", j=TILES)

        def over(col, n):
            return col.unsqueeze(2).broadcast_to([P, TILES, n])

        def down_w(w, k):
            if k < PAIRS:
                return w[:, C_D + k * D:C_D + (k + 1) * D]
            s = k - PAIRS
            return w[0:SH_ROWS[s], C_SD + s * D:C_SD + (s + 1) * D]

        def up_w(w, k, gate):
            if k < PAIRS:
                a = (C_G if gate else C_H) + k * P
                return w[:, a:a + P]
            s = k - PAIRS
            a = (C_SG if gate else C_SU) + s * P
            return w[:, a:a + SH_ROWS[s]]

        def rows(k):
            return P if k < PAIRS else SH_ROWS[k - PAIRS]

        class Chain:

            def __init__(self, eng, s, base, n=0):
                self.eng, self.s, self.base, self.n = eng, s, base, n

            def mark(self, ins):
                self.n += 1
                ins.then_inc(self.s, 1)

            def need(self):
                self.eng.wait_ge(self.s, self.base + self.n)

        def ffn_groups(eng, f, kind, occ, back, finish, then=None, to=None):
            def after(m, r, g, p):
                return (kind, m + 1, r + 1, g + 1, 1 - p)

            back(8 * f, 8 * occ, 0, 0, after(8 * f, 8 * occ, 0, 0), None)
            with eng.Fori(0, GROUPS // 2 - 1) as i:
                for p in (1, 0):
                    g = i * 2 + (2 - p)
                    back(g + 8 * f, g + 8 * occ, g, p, after(g + 8 * f, g + 8 * occ, g, p), None)
            last = (8 * f + GROUPS - 1, 8 * occ + GROUPS - 1, GROUPS - 1)
            back(*last, (GROUPS - 1) % 2, then, to)
            finish(*last)

        def attn_groups(eng, step, finish):
            step(0, 0, False, True)
            with eng.Fori(0, GROUPS // 2 - 2) as i:
                for p in (1, 0):
                    step(i * 2 + (2 - p), p, True, True)
            step(GROUPS - 3, 1, True, True)
            step(GROUPS - 2, 0, True, True)
            step(GROUPS - 1, (GROUPS - 1) % 2, True, False)
            finish(GROUPS - 1, (GROUPS - 1) % 2)

        THEN_FFN1 = (1, 2 * GROUPS, 0, 0, 0)

        def slot0(p, k):
            q = p * N0 + k
            return q % RING if q < 16 else (q - 16) % 3

        def soon0(p, k):
            return (p * N0 + k) % (2 * N0) in (0, 1, 2, 19, 20, 21)


        @block.sync
        def _(sp):
            sp.dma_start(X[:, 0:TILES, :], x_dram[:, 0:TILES, :]).then_inc(s_x0, 16)
            sp.dma_start(small[:, 0:FIRST_SMALL], small_in[:, 0:FIRST_SMALL]).then_inc(s_small, 16)
            for n in range(W0_PARTS):
                part = slice(n * W0_PART, (n + 1) * W0_PART)
                sp.dma_start(w0raw[:, part], w0_in[:, part]).then_inc(s_raw[n], 16)
                if n == 1:
                    sp.dma_start(sel_raw[:], sel_in).then_inc(s_sel_raw, 16)
            sp.dma_start(X[:, TILES:, :], x_dram[:, TILES:, :]).then_inc(s_x1, 16)
            sp.dma_start(small[:, FIRST_SMALL:], small_in[:, FIRST_SMALL:]).then_inc(s_small2, 16)
            sp.dma_start(w1raw[:], w1_in).then_inc(s_raw1, 16)
            sp.dma_start(w2raw[:], w2_in).then_inc(s_raw2, 16)
            with sp.Fori(0, GROUPS) as g:
                sp.wait_ge(s_xo, g + 3 * GROUPS + 2)
                sp.dma_start(out_dram[:, bass.ts(g, TILES), :], group_of(g)).then_inc(s_out, 16)
            sp.wait_ge(s_out, 16 * GROUPS)

        @block.gpsimd
        def _(pool):
            nc.gpsimd.memset(mhalf[:], -0.5).then_inc(s_mhalf, 1)
            nc.gpsimd.memset(euler[:], math.e).then_inc(s_mhalf, 1)
            pool.wait_ge(s_mhalf, 2)

            def power(s_in, s_done, n, p):
                pool.wait_ge(s_in, n + 1)
                nc.gpsimd.tensor_tensor(rstd[:, p, :], ve[:, p, :], mhalf[:], ALU.pow).then_inc(s_done, 1)

            def route_exp(kind, r):
                s = ROUTE[kind]
                src, dst = ((gates[:, 0], gates[:, 1]), (rt[:, 0, 0:TILES * E1], rt[:, 1, 0:TILES * E1]))[kind]
                pool.wait_ge(s["d"], r + 1)
                nc.gpsimd.tensor_tensor(dst, euler[:, 0:src.shape[1]], src, ALU.pow).then_inc(s["exp"], 1)

            def ffn0(m, r, g, p, nxt, to):
                for k in range(N0):
                    if k == 7 and nxt:
                        route_exp(nxt[0], nxt[2])
                    if k == 1 and nxt:
                        power(s_ve, s_rstd, m + 1, 1 - p)
                    if k == 5 and to == 0:
                        power(a0["ve1"], a0["rstd1"], 0, 0)
                        power(a0["ve1"], a0["rstd1"], 1, 1)
                    if k == 10 and to == 0:
                        power(a0["ve2"], a0["rstd2"], 0, 0)
                    M, n = rows(k), slot0(p, k)
                    pool.wait_ge(s_uh, r * N0 + k + 1)
                    nc.gpsimd.tensor_tensor(lo[0:M, n, :], work[0:M, 1, n, :], hi[0:M, n, :].bitcast(F32),
                                            ALU.subtract).then_inc(s_ul, 1)
                if to == 0:
                    power(a0["ve2"], a0["rstd2"], 1, 1)

            def add_term(r, e):
                pool.wait_ge(s1_term, r * E1 + e + 1)
                if e > 1:
                    pool.wait_ge(s1_acc, r * (E1 - 1) + e - 1)
                nc.gpsimd.tensor_tensor(yT[:], yT[:], term[:, e % 2, :], ALU.add).then_inc(s1_acc, 1)

            def ffn1(m, r, g, p, nxt, to):
                if not (isinstance(g, int) and g == 0):
                    add_term(r - 1, E1 - 1)
                for e in range(1, E1 - 1):
                    if e == 3 and nxt:
                        route_exp(1, r + 1)
                    if e == 1 and nxt:
                        power(s_ve, s_rstd, m + 1, 1 - p)
                    if e == 1 and to == 1:
                        power(a1["ve1"], a1["rstd1"], 0, 0)
                        power(a1["ve1"], a1["rstd1"], 1, 1)
                    add_term(r, e)

            def finish1(m, r, g):
                add_term(r, E1 - 1)

            def front0(m, r, g, p):
                power(s_ve, s_rstd, m, p)
                route_exp(0, r)

            none = lambda *a: None

            def step0(n, p, second, norm):
                if norm and second:
                    power(a0["ve2"], a0["rstd2"], n + 1, 1 - p)
                for k, (wl, raw, wh) in enumerate(((w1l, w1raw, w1h), (w2l, w2raw, w2h))):
                    pool.wait_ge(s_w12h, n * 2 + k + 1)
                    part = bass.ts(n, EIGHTH)
                    nc.gpsimd.tensor_tensor(wl[:, part], raw[:, part], wh[:, part].bitcast(F32),
                                            ALU.subtract).then_inc(s_w12l, 1)
                if norm:
                    if isinstance(n, int) and n == GROUPS - 2:
                        power(s_ve, s_rstd, GROUPS, 0)
                    else:
                        power(a0["ve1"], a0["rstd1"], n + 2, p)

            def step1(n, p, second, norm):
                if norm and second:
                    power(a1["ve1"], a1["rstd1"], n + 1, 1 - p)
                elif not norm:
                    power(s_ve, s_rstd, 3 * GROUPS, 0)

            front0(0, 0, 0, 0)
            ffn_groups(pool, 0, 0, 0, ffn0, none, to=0)
            attn_groups(pool, step0, lambda n, p: route_exp(0, GROUPS))
            ffn_groups(pool, 1, 0, 1, ffn0, none, then=THEN_FFN1)
            ffn_groups(pool, 2, 1, 0, ffn1, finish1, to=1)
            attn_groups(pool, step1, lambda n, p: route_exp(1, GROUPS))
            ffn_groups(pool, 3, 1, 1, ffn1, finish1)

        @block.scalar
        def _(act):
            A = nc.scalar.activation

            def w0_high(n):
                part = slice(n * W0_PART, (n + 1) * W0_PART)
                act.wait_ge(s_raw[n], 16)
                A(w0h[:, part], w0raw[:, part], ACT.Copy).then_inc(s_wh, 1)

            def take_xT(m, p):
                act.wait_ge(s_T, m + 1)
                A(xT[:, p, :], TB[:], ACT.Copy)
                A(xh[:, p, :], TB[:], ACT.Copy).then_inc(s_xh, 1)

            def take_comb(s, r, m, p):
                act.wait_ge(s["combT"], r + 1)
                A(combT[:, p, :], RB[0:64, :], ACT.Copy).then_inc(s_ct, 1)

            def hidden(r):
                act.wait_ge(r1["hid"], r + 1)
                A(hr[0:64, :], RB[0:64, :], ACT.Gelu, bias=cst("br1", 64)).then_inc(r1["gelu"], 1)

            def front0(m, r, g, p):
                w0_high(0)
                w0_high(1)
                take_xT(m, p)
                act.wait_ge(s_sel_raw, 16)
                A(sel[:], sel_raw[:], ACT.Copy).then_inc(s_sel, 1)
                w0_high(2)
                w0_high(3)
                take_comb(r0, r, m, p)

            def ahead0(n, p):
                act.wait_ge(a0["T"], n + 1)
                A(xT[:, p, :], bank[6 + p][:], ACT.Identity, bias=cst("beta"), scale=cst("gamma")).then_inc(a0["hT"], 1)

            def ahead1(n, p):
                act.wait_ge(a1["T"], n + 1)
                A(xT[:, p, :], bank[6 + p][:], ACT.Copy).then_inc(a1["xT"], 1)

            def take_y(r):
                act.wait_ge(s_dn, r * N0)
                A(yT[:], Y0[:], ACT.Copy).then_inc(s_yT, 1)

            def back0(m, r, g, p, nxt, to):
                def high(k):
                    M, n = rows(k), slot0(p, k)
                    act.wait_ge(s_u, r * N0 + k + 1)
                    if soon0(p, k) and not (isinstance(g, int) and g == 0 and k < 3):
                        act.wait_ge(s_dn, r * N0 + k - 2)
                    A(hi[0:M, n, :], work[0:M, 1, n, :], ACT.Copy).then_inc(s_uh, 1)

                kind, mn, rn, gn, pn = nxt or (None,) * 5
                for k in range(N0):
                    M = rows(k)
                    act.wait_ge(s_gate, r * N0 + k + 1)
                    A(work[0:M, 0, slot0(p, k), :], GATE[(p + k) % 2][0:M, :], ACT.Silu).then_inc(s_silu, 1)
                    if k:
                        high(k - 1)
                    if k == 1 and not (isinstance(g, int) and g == 0):
                        take_y(r)
                    if nxt and k == 4:
                        take_xT(mn, pn)
                    if kind == 1 and k == 6:
                        hidden(rn)
                    if nxt and k == 10:
                        take_comb(ROUTE[kind], rn, mn, pn)
                high(N0 - 1)
                if to == 0:
                    ahead0(0, 0)

            def finish0(m, r, g):
                take_y(r + 1)

            def back1(m, r, g, p, nxt, to):
                for kk in range(N1):
                    e, c = divmod(kk, CH1)
                    act.wait_ge(s1_up, r * N1 + kk + 1)
                    b = small[:, SMALL_AT["b1"][0] + kk:SMALL_AT["b1"][0] + kk + 1]
                    A(work[:, 0, kk % RING, :], RINGB[kk % RING][:], ACT.Gelu, bias=b).then_inc(s1_he, 1)
                    if c in HI_BY_ACT:
                        A(hi[:, kk % RING, :], RINGB[kk % RING][:], ACT.Gelu, bias=b).then_inc(s1_hiA, 1)
                    if c == 2:
                        act.wait_ge(s1_cbp, r * E1 + e + 1)
                        A(comb_bc[:, e % 2, :], CB[:], ACT.Copy).then_inc(s1_cb, 1)
                    if nxt and kk == 11:
                        take_xT(m + 1, 1 - p)
                    if to == 1 and kk == 11:
                        ahead1(0, 0)
                    if nxt and kk == 16:
                        hidden(r + 1)
                    if nxt and kk == 30:
                        take_comb(r1, r + 1, m + 1, 1 - p)

            none = lambda *a: None

            def attn0():
                def softmax_exp(n, d, e, p):
                    act.wait_ge(a0[d], n + 1)
                    for j in range(TILES):
                        cols = slice(j * D, (j + 1) * D)
                        ins = A(work[:, p, 1, cols], bank[p][:, cols], ACT.Exp, bias=mx[:, p, j:j + 1], scale=INV,
                                accum_out=rsum[:, p, j:j + 1])
                    ins.then_inc(a0[e], 1)

                def step(n, p, second, norm):
                    act.wait_ge(a0["q"], n + 1)
                    A(attn[:, 0, p, :], bank[p][:], ACT.Identity, bias=cst("bq")).then_inc(a0["qT"], 1)
                    act.wait_ge(a0["k"], n + 1)
                    A(attn[:, 0, 2 + p, :], bank[2 + p][:], ACT.Identity, bias=cst("bk")).then_inc(a0["kT"], 1)
                    if not second:
                        ahead0(n + 1, 1 - p)
                    for wh, raw in ((w1h, w1raw), (w2h, w2raw)):
                        part = bass.ts(n, EIGHTH)
                        A(wh[:, part], raw[:, part], ACT.Copy).then_inc(s_w12h, 1)
                    if second:
                        softmax_exp(n - 1, "d2", "e2", 1 - p)
                    softmax_exp(n, "d1", "e1", p)
                    act.wait_ge(a0["v"], n + 1)
                    A(comb_bc[:, p, :], bank[6 + p][:], ACT.Copy).then_inc(a0["vc"], 1)
                    if norm and second:
                        ahead0(n + 1, 1 - p)
                    elif not norm:
                        take_xT(GROUPS, 0)

                def finish(n, p):
                    softmax_exp(n, "d2", "e2", p)
                    take_comb(r0, GROUPS, GROUPS, 0)

                act.wait_ge(s_raw1, 16)
                act.wait_ge(s_raw2, 16)
                attn_groups(act, step, finish)

            def attn1():
                def transposed(n, p):
                    act.wait_ge(a1["aT"], n + 1)
                    A(attn[:, 1, 2 * p, :], bank[2 + p][:], ACT.Copy)
                    A(attn[:, 1, 2 * p + 1, :], bank[6 + p][:], ACT.Copy).then_inc(a1["aTc"], 1)

                def step(n, p, second, norm):
                    act.wait_ge(a1["k"], n + 1)
                    A(attn[:, 0, 2 + p, :], bank[2 + p][:], ACT.Identity, bias=cst("bk1")).then_inc(a1["kT"], 1)
                    act.wait_ge(a1["q"], n + 1)
                    A(attn[:, 0, p, :], bank[p][:], ACT.Identity, bias=cst("bq1")).then_inc(a1["qT"], 1)
                    if second:
                        transposed(n - 1, 1 - p)
                    else:
                        ahead1(n + 1, 1 - p)
                    act.wait_ge(a1["xn"], n + 1)
                    if not (isinstance(n, int) and n < 2):
                        act.wait_ge(a1["o"], n - 1)
                    A(t4(comb_bc[:, p, :]), xn[:, p], ACT.Copy).then_inc(a1["xnc"], 1)
                    act.wait_ge(a1["nmax"], n + 1)
                    for j in range(TILES):
                        cols = slice((j % 2) * SEQ, (j % 2 + 1) * SEQ)
                        ins = A(work[:, p, j // 2, cols], bank[4 * (j // 2) + p][:, cols], ACT.Exp,
                                bias=mx[:, p, j:j + 1], scale=INV, accum_out=rsum[:, p, j:j + 1])
                    ins.then_inc(a1["e"], 1)
                    if norm and second:
                        ahead1(n + 1, 1 - p)
                    elif not norm:
                        take_xT(3 * GROUPS, 0)

                def finish(n, p):
                    transposed(n, p)
                    hidden(GROUPS)
                    take_comb(r1, GROUPS, 3 * GROUPS, 0)

                attn_groups(act, step, finish)

            front0(0, 0, 0, 0)
            act.wait_ge(s_small2, 16)
            A(brow[:].rearrange("p b d -> p (b d)"), small[0:64, B_ROWS:B_ROWS + 3 * D], ACT.Copy).then_inc(s_bhi, 1)
            act.wait_ge(s_hr1, 1)
            ffn_groups(act, 0, 0, 0, back0, finish0, to=0)
            attn0()
            ffn_groups(act, 1, 0, 1, back0, finish0, then=THEN_FFN1)
            ffn_groups(act, 2, 1, 0, back1, none, to=1)
            attn1()
            ffn_groups(act, 3, 1, 1, back1, none)

        @block.tensor
        def _(pe):
            MM = nc.tensor.matmul

            def three(dst, w_hi, w_lo, x_hi, x_lo, start, stop):
                MM(dst, w_hi, x_hi, start=start, stop=False)
                MM(dst, w_hi, x_lo, start=False, stop=False)
                return MM(dst, w_lo, x_hi, start=False, stop=stop)

            def transpose4(dst, src, n=P):
                for j in range(TILES):
                    last = nc.tensor.transpose(dst[0:n, j * P:(j + 1) * P], src(j), ident)
                return last

            def is_first(g):
                return isinstance(g, int) and g == 0

            def front_T(m, p):
                pe.wait_ge(s_xn, m + 1)
                transpose4(TB, lambda j: xn[:, p, j, :]).then_inc(s_T, 1)

            def logits0(m, r, p):
                pe.wait_ge(s_xl, m + 1)
                for j in range(TILES):
                    last = MM(RB[:, j * 32:j * 32 + E0 + 1], xT[:, p, j * P:(j + 1) * P], cst("gate0"),
                              start=True, stop=True)
                last.then_inc(r0["logits"], 1)

            def comb_T(s, r):
                pe.wait_ge(s["comb"], r + 1)
                transpose4(RB, lambda j: cm[:, j, :].bitcast(F32)).then_inc(s["combT"], 1)

            def out_T(s, count):
                pe.wait_ge(s, count)
                transpose4(TB, lambda j: yT[:, j * P:(j + 1) * P]).then_inc(s_oT, 1)

            def ahead(s, n, p):
                pe.wait_ge(s["xn"], n + 1)
                transpose4(bank[6 + p], lambda j: xn[:, p, j, :]).then_inc(s["T"], 1)

            def hidden(m, r, p):
                pe.wait_ge(s_xl, m + 1)
                MM(RB[0:64, :], cst("wr1"), xT[:, p, :], start=True, stop=True).then_inc(r1["hid"], 1)

            def logits1(r):
                pe.wait_ge(r1["gelu"], r + 1)
                for j in range(TILES):
                    last = MM(RB[:, j * 32:j * 32 + E1], hr[0:65, j * P:(j + 1) * P], cst("wr2", 65),
                              start=True, stop=True)
                last.then_inc(r1["logits"], 1)

            def up0(m, r, p, k):
                if k >= N0:
                    return up0(m + 1, r + 1, 1 - p, k - N0)
                M = rows(k)
                if k == 0:
                    pe.wait_ge(s_xl, m + 1)
                if k >= 2 or not is_first(r):
                    pe.wait_ge(s_silu, r * N0 + k - 1)
                three(GATE[(p + k) % 2][0:M, :], up_w(w0h, k, True), up_w(w0l, k, True), xh[:, p, :], xl[:, p, :],
                      True, True).then_inc(s_gate, 1)
                if k >= 2 or not is_first(r):
                    pe.wait_ge(s_t, r * N0 + k - 1)
                three(UP[(p + k) % 2][0:M, :], up_w(w0h, k, False), up_w(w0l, k, False), xh[:, p, :], xl[:, p, :],
                      True, True).then_inc(s_up, 1)

            def spread0(m, r, p, k):
                if k >= N0:
                    return spread0(m + 1, r + 1, 1 - p, k - N0)
                if k > PAIRS:
                    return
                if k == 0:
                    pe.wait_ge(s_ct, m + 1)
                if k >= 2:
                    pe.wait_ge(s_u, r * N0 + k - 1)
                elif not is_first(r):
                    pe.wait_ge(s_u, (r - 1) * N0 + PAIRS if k == 0 else r * N0)
                MM(CB2[(p + k) % 2][:], sel[:, k, :], combT[:, p, :], start=True, stop=True).then_inc(s_cb, 1)

            def down0(r, p, k):
                M, n = rows(k), slot0(p, k)
                if k == 0 and not is_first(r):
                    pe.wait_ge(s_yT, r)
                pe.wait_ge(s_ul, r * N0 + k + 1)
                three(Y0[:], down_w(w0h, k), down_w(w0l, k), hi[0:M, n, :], lo[0:M, n, :],
                      k == 0, k == N0 - 1).then_inc(s_dn, 1)

            def front0(m, r, g, p):
                front_T(m, p)
                logits0(m, r, p)
                pe.wait_ge(s_wl, 2)
                up0(m, r, p, 0)
                up0(m, r, p, 1)
                comb_T(r0, r)
                pe.wait_ge(s_sel, 1)
                spread0(m, r, p, 0)
                pe.wait_ge(s_wl, W0_PARTS)

            def back0(m, r, g, p, nxt, to):
                kind, mn, rn, gn, pn = nxt or (None,) * 5
                last = N0 if kind == 0 else 0
                for k in range(N0):
                    if k + 1 < N0:
                        spread0(m, r, p, k + 1)
                    if k + 2 < N0 + last:
                        up0(m, r, p, k + 2)
                    if k + 1 == N0 and last:
                        spread0(m, r, p, N0)
                    if k:
                        down0(r, p, k - 1)
                    elif not is_first(g):
                        down0(r - 1, 1 - p, N0 - 1)
                    if k == 1 and not is_first(g):
                        out_T(s_yT, r)
                    if nxt and k == 2:
                        pe.wait_ge(s_xo, m + 1)
                        front_T(mn, pn)
                    if nxt and k == 4:
                        logits0(mn, rn, pn) if kind == 0 else hidden(mn, rn, pn)
                    if kind == 1 and k == 5:
                        logits1(rn)
                    if nxt and k == 9:
                        comb_T(ROUTE[kind], rn)
                if to == 0:
                    pe.wait_ge(s_xo, m + 1)
                    ahead(a0, 0, 0)

            def start_a0(n, p):
                pe.wait_ge(a0["hT"], n + 1)
                MM(bank[p][:], cst("wq"), xT[:, p, :], start=True, stop=True).then_inc(a0["q"], 1)

            def keys(n, p):
                MM(bank[2 + p][:], cst("wk"), xT[:, p, :], start=True, stop=True).then_inc(a0["k"], 1)

            def start_a1(n, p):
                pe.wait_ge(a1["xT"], n + 1)
                MM(bank[2 + p][:], cst("wk1"), xT[:, p, :], start=True, stop=True).then_inc(a1["k"], 1)
                if not (isinstance(n, int) and n < 2):
                    pe.wait_ge(a1["two"], n - 1)
                MM(bank[p][:], cst("wq1"), xT[:, p, :], start=True, stop=True).then_inc(a1["q"], 1)

            def finish0(m, r, g):
                down0(r, g % 2, N0 - 1)
                if m == GROUPS - 1:
                    pe.wait_ge(s_small2, 16)
                    pe.wait_ge(s_blo, 1)
                    start_a0(0, 0)
                    keys(0, 0)
                    pe.wait_ge(a0["hT"], 1)
                out_T(s_yT, r + 1)

            def up1(m, r, p, kk):
                if kk >= N1:
                    return up1(m + 1, r + 1, 1 - p, kk - N1)
                if kk == 0:
                    pe.wait_ge(s_xl, m + 1)
                ws = slice(kk * P, (kk + 1) * P)
                three(RINGB[kk % RING][:], w1h[:, ws], w1l[:, ws], xh[:, p, :], xl[:, p, :], True, True).then_inc(s1_up, 1)

            def start1(m, r, p):
                for kk in range(RING - 1):
                    up1(m, r, p, kk)

            def back1(m, r, g, p, nxt, to):
                def down(kk):
                    e, c = divmod(kk, CH1)
                    first = is_first(r)
                    if c == 0:
                        if e >= 1 or not first:
                            pe.wait_ge(s1_cb, r * E1 + e)
                        if e >= 2 or not first:
                            pe.wait_ge(s1_term, r * E1 + e - 1)
                        MM(CB[:], sel[:, PAIRS + 1 + e, :], combT[:, p, :], start=True, stop=True).then_inc(s1_cbp, 1)
                    ws = slice(kk * P, (kk + 1) * P)
                    pe.wait_ge(s1_lo, r * N1 + kk + 1)
                    last = three(YB[e % 2][:], w2h[:, ws], w2l[:, ws], hi[:, kk % RING, :], lo[:, kk % RING, :],
                                 c == 0, c == CH1 - 1)
                    if c == CH1 - 1:
                        last.then_inc(s1_Y, 1)

                if is_first(r):
                    start1(m, r, p)
                for kk in range(N1):
                    if kk + RING - 1 < N1 or nxt:
                        up1(m, r, p, kk + RING - 1)
                    if kk == 0:
                        pe.wait_ge(s_ct, m + 1)
                    down(kk)
                    if kk == 2 and not is_first(g):
                        out_T(s1_acc, r * (E1 - 1))
                    if nxt and kk == 9:
                        pe.wait_ge(s_xo, m + 1)
                        front_T(m + 1, 1 - p)
                    if to == 1 and kk == 8:
                        pe.wait_ge(s_xo, m + 1)
                        ahead(a1, 0, 0)
                    if nxt and kk == 13:
                        hidden(m + 1, r + 1, 1 - p)
                    if nxt and kk == 15:
                        logits1(r + 1)
                    if nxt and kk == 27:
                        comb_T(r1, r + 1)

            def finish1(m, r, g):
                if m == 3 * GROUPS - 1:
                    start_a1(0, 0)
                    pe.wait_ge(a1["xT"], 1)
                out_T(s1_acc, (r + 1) * (E1 - 1))

            def tok_major(dst, src, w, bias=None):
                if bias is not None:
                    row = brow[:, bias, :].unsqueeze(1).broadcast_to([64, TILES, D])
                    MM(dst[:], sel[:, PAIRS + 1, :], row, start=True, stop=False)
                for j in range(TILES):
                    last = MM(dst[:, j * D:(j + 1) * D], src[:, j * P:(j + 1) * P], w, start=(bias is None),
                              stop=(bias is None or j == TILES - 1))
                return last

            def attn0():
                tri0, tri1 = cst("tri0"), cst("tri1")

                def w(p, j):
                    return work[:, p, 2, j * D:(j + 1) * D]

                def pool(n, p):
                    pe.wait_ge(a0["wq"], n + 1)
                    pe.wait_ge(a0["kT"], n + 1)
                    for b in (0, 1):
                        MM(bank[2 + p][:, b * SEQ:(b + 1) * SEQ], w(p, 2 * b), tri0, start=True, stop=False)
                        last = MM(bank[2 + p][:, b * SEQ + P:(b + 1) * SEQ], w(p, 2 * b + 1), tri1, start=False, stop=True)
                    last.then_inc(a0["pool"], 1)

                def mixed_keys(n, p):
                    pe.wait_ge(a0["mixed"], n + 1)
                    mixed = attn[:, 1, p, :]
                    tok_major(bank[p], mixed, cst("wka"), 1).then_inc(a0["l2"], 1)
                    transpose4(bank[4 + p], lambda j: mixed[:, j * P:(j + 1) * P]).then_inc(a0["mixt"], 1)

                def pool_keys(n, p):
                    pe.wait_ge(a0["w2"], n + 1)
                    dst = lambda j: bank[2 + p][:, j * D:(j + 1) * D]
                    for b in (0, 1):
                        MM(dst(2 * b), tri0[:, 0:P], w(p, 2 * b), start=True, stop=True)
                        MM(dst(2 * b + 1), tri0[:, P:SEQ], w(p, 2 * b), start=True, stop=False)
                        last = MM(dst(2 * b + 1), tri1, w(p, 2 * b + 1), start=False, stop=True)
                    last.then_inc(a0["pk"], 1)

                def step(n, p, second, norm):
                    if not is_first(n):
                        start_a0(n, p)
                    if second:
                        pool(n - 1, 1 - p)
                        if not (isinstance(n, int) and n < 2):
                            pe.wait_ge(a0["two"], (n - 1) * 4)
                        keys(n, p)
                    else:
                        ahead(a0, n + 1, 1 - p)
                    pe.wait_ge(a0["qT"], n + 1)
                    transpose4(bank[4 + p], lambda j: attn[:, 0, p, j * P:(j + 1) * P]).then_inc(a0["qt"], 1)
                    if second:
                        mixed_keys(n - 1, 1 - p)
                    tok_major(bank[p], attn[:, 0, p, :], cst("wqa"), 0).then_inc(a0["l1"], 1)
                    if is_first(n):
                        pe.wait_ge(s_xo, GROUPS + 1)
                    tok_major(bank[6 + p], xT[:, p, :], cst("wv"), 2).then_inc(a0["v"], 1)
                    if second:
                        if norm:
                            ahead(a0, n + 1, 1 - p)
                        else:
                            pe.wait_ge(a0["vc"], n)
                            front_T(GROUPS, 0)
                        pool_keys(n - 1, 1 - p)

                def finish(n, p):
                    pool(n, p)
                    logits0(GROUPS, GROUPS, 0)
                    mixed_keys(n, p)
                    pe.wait_ge(a0["two"], 4 * n)
                    up0(GROUPS, GROUPS, 0, 0)
                    pool_keys(n, p)
                    comb_T(r0, GROUPS)
                    pe.wait_ge(a0["two"], 4 * GROUPS)
                    up0(GROUPS, GROUPS, 0, 1)
                    spread0(GROUPS, GROUPS, 0, 0)

                attn_groups(pe, step, finish)

            def attn1():
                def weights_T(n, p):
                    pe.wait_ge(a1["a"], n + 1)
                    for j in range(TILES):
                        for h in (0, 1):
                            at = (j % 2) * SEQ + h * P
                            last = nc.tensor.transpose(bank[2 + 4 * h + p][:, j * P:(j + 1) * P],
                                                       work[:, p, 2 + j // 2, at:at + P], ident)
                    last.then_inc(a1["aT"], 1)

                def apply(n, p):
                    pe.wait_ge(a1["aTc"], n + 1)
                    pe.wait_ge(a1["xnc"], n + 1)
                    v = lambda j: comb_bc[:, p, j * D:(j + 1) * D]
                    for j in range(TILES):
                        b = j // 2
                        dst = bank[p][:, j * D:(j + 1) * D]
                        MM(dst, ident, v(j), start=True, stop=False)
                        for h in (0, 1):
                            last = MM(dst, attn[:, 1, 2 * p + h, j * P:(j + 1) * P], v(2 * b + h),
                                      start=False, stop=(h == 1))
                    last.then_inc(a1["o"], 1)

                def step(n, p, second, norm):
                    if not is_first(n):
                        start_a1(n, p)
                    if second:
                        weights_T(n - 1, 1 - p)
                    else:
                        ahead(a1, n + 1, 1 - p)
                    pe.wait_ge(a1["qT"], n + 1)
                    pe.wait_ge(a1["kT"], n + 1)
                    for j in range(TILES):
                        b = j // 2
                        last = MM(bank[4 * b + p][:, (j % 2) * SEQ:(j % 2 + 1) * SEQ], attn[:, 0, p, j * P:(j + 1) * P],
                                  attn[:, 0, 2 + p, b * SEQ:(b + 1) * SEQ], start=True, stop=True)
                    last.then_inc(a1["s"], 1)
                    if second:
                        apply(n - 1, 1 - p)
                        if norm:
                            ahead(a1, n + 1, 1 - p)
                        else:
                            front_T(3 * GROUPS, 0)

                def finish(n, p):
                    weights_T(n, p)
                    hidden(3 * GROUPS, GROUPS, 0)
                    apply(n, p)
                    logits1(GROUPS)
                    pe.wait_ge(a1["two"], n)
                    up1(3 * GROUPS, GROUPS, 0, 0)
                    pe.wait_ge(a1["two"], GROUPS)
                    up1(3 * GROUPS, GROUPS, 0, 1)
                    up1(3 * GROUPS, GROUPS, 0, 2)
                    comb_T(r1, GROUPS)

                attn_groups(pe, step, finish)

            pe.wait_ge(s_small, 16)
            front0(0, 0, 0, 0)
            pe.wait_ge(s_hr1, 1)
            ffn_groups(pe, 0, 0, 0, back0, finish0, to=0)
            attn0()
            ffn_groups(pe, 1, 0, 1, back0, finish0, then=THEN_FFN1)
            pe.wait_ge(s_w12l, 2 * GROUPS)
            ffn_groups(pe, 2, 1, 0, back1, finish1, to=1)
            attn1()
            ffn_groups(pe, 3, 1, 1, back1, finish1)

        @block.vector
        def _(dve):
            V = nc.vector
            V.memset(hr[64:65, :], 1.0).then_inc(s_hr1, 1)
            V.memset(cm[:].bitcast(F32), 0.0).then_inc(s_xo, 1)

            def w0_low(n):
                part = slice(n * W0_PART, (n + 1) * W0_PART)
                dve.wait_ge(s_wh, n + 1)
                V.tensor_tensor(w0l[:, part], w0raw[:, part], w0h[:, part].bitcast(F32), ALU.subtract).then_inc(s_wl, 1)
            dve.wait_ge(s_small, 16)
            dve.wait_ge(s_x0, 16)
            dve.wait_ge(s_xo, 1)

            def variance(ch, src, p):
                for j in range(TILES):
                    last = V.bn_stats(st[:, p, j, :], src(j))
                ch.mark(last)
                yield
                ch.need()
                V.memset(hold[:, p:p + 1], 0.0)
                for j in range(TILES):
                    last = V.bn_aggr(mv[:, p, j, :], st[:, p, j, :])
                ch.mark(last)
                yield
                ch.need()

            def plus_eps(p):
                return V.tensor_scalar(ve[:, p, :], mv[:, p, :, 1], EPS, None, ALU.add)

            def normed(src, p):
                for j in range(TILES):
                    last = V.tensor_scalar(xn[:, p, j:j + 1, :], src(j), mv[:, p, j, 0:1], rstd[:, p, j:j + 1],
                                           ALU.subtract, ALU.mult)
                return last

            def stats(ch, m, g, p):
                yield from variance(ch, lambda j: tile_of(g, j), p)
                plus_eps(p).then_inc(s_ve, 1)

            def norm_of(m, g, p):
                dve.wait_ge(s_rstd, m + 1)
                normed(lambda j: tile_of(g, j), p).then_inc(s_xn, 1)

            def split(m, p):
                dve.wait_ge(s_xh, m + 1)
                V.tensor_tensor(xl[:, p, :], TB[:], xh[:, p, :].bitcast(F32), ALU.subtract).then_inc(s_xl, 1)

            def tab(i, w):
                return rt[:, i, 0:TILES * w].rearrange("p (j e) -> p j e", j=TILES)

            def route_max(ch, s, r, E, w):
                lg = RB[:, 0:TILES * 32].rearrange("p (j e) -> p j e", j=TILES)
                dve.wait_ge(s["logits"], r + 1)
                ch.mark(V.tensor_reduce(rmx[:, 0, :], lg[:, :, 0:E], AX_X, ALU.max))
                if w > E:
                    V.tensor_scalar(gates[:, 0, TILES:], lg[:, :, E], -1.0, None, ALU.mult)
                yield
                ch.need()
                ins = V.tensor_tensor(tab(0, E), lg[:, :, 0:E], over(rmx[:, 0, :], E), ALU.subtract)
                if w > E:
                    ch.mark(ins)
                    yield
                    ch.need()
                else:
                    ins.then_inc(s["d"], 1)
                    yield
                    dve.wait_ge(s["d"], r + 1)

            def route_top2(ch, s, r, E, w):
                d = tab(0, E)
                tie = cst("tie").rearrange("p (j e) -> p j e", j=TILES)[:, :, 0:E]
                ch.mark(V.scalar_tensor_tensor(tab(2, E), d, 0.0, tie, ALU.is_ge, ALU.mult))
                yield
                ch.need()
                ch.mark(V.tensor_reduce(rmx[:, 1, :], tab(2, E), AX_X, ALU.max))
                yield
                ch.need()
                ch.mark(V.tensor_tensor(tab(3, E), tab(2, E), over(rmx[:, 1, :], E), ALU.is_equal))
                yield
                ch.need()
                ch.mark(V.scalar_tensor_tensor(tab(4, E), tab(3, E), -BIG, d, ALU.mult, ALU.add))
                yield
                ch.need()
                if w > E:
                    V.tensor_reduce(gates[:, 0, 0:TILES], tab(4, E), AX_X, ALU.max).then_inc(s["d"], 1)
                    yield
                    dve.wait_ge(s["d"], r + 1)
                else:
                    ch.mark(V.tensor_reduce(gates[:, 0, 0:TILES], tab(4, E), AX_X, ALU.max))
                    yield
                    ch.need()
                ch.mark(V.tensor_tensor(tab(5, E), tab(4, E), over(gates[:, 0, 0:TILES], E), ALU.is_equal))
                yield
                ch.need()
                ch.mark(V.tensor_tensor(tab(5, E), tab(5, E), tie, ALU.mult))
                yield
                ch.need()
                ch.mark(V.tensor_reduce(rmx[:, 3, :], tab(5, E), AX_X, ALU.max))
                yield
                ch.need()
                ch.mark(V.tensor_tensor(tab(6, E), tab(5, E), over(rmx[:, 3, :], E), ALU.is_equal))
                yield
                ch.need()

            def comb_parts(ch, s, src, w):
                ch.mark(V.tensor_scalar(cm[:, :, 0:w], src, 0.5, None, ALU.mult))
                yield
                ch.need()
                V.scalar_tensor_tensor(cm[:, :, LO:LO + w], src, 0.5, cm[:, :, 0:w].bitcast(F32), ALU.mult,
                                       ALU.subtract).then_inc(s["comb"], 1)

            def route0(ch, r):
                yield from route_max(ch, r0, r, E0, E0 + 1)
                yield from route_top2(ch, r0, r, E0, E0 + 1)
                dve.wait_ge(r0["exp"], r + 1)
                first, shared = gates[:, 0, 0:TILES], gates[:, 0, TILES:]
                ch.mark(V.tensor_scalar(gates[:, 2, :], gates[:, 1, :], 1.0, None, ALU.add))
                yield
                ch.need()
                ch.mark(V.reciprocal(gates[:, 0, :], gates[:, 2, :]))
                yield
                ch.need()
                V.tensor_tensor(tab(4, E0), tab(3, E0), over(first, E0), ALU.mult)
                V.tensor_scalar(tab(7, E0 + 1)[:, :, E0], shared, 1.0, None, ALU.mult)
                ch.mark(V.tensor_tensor(rmx[:, 5, :], gates[:, 1, 0:TILES], first, ALU.mult))
                yield
                ch.need()
                ch.mark(V.tensor_tensor(tab(5, E0), tab(6, E0), over(rmx[:, 5, :], E0), ALU.mult))
                yield
                ch.need()
                ch.mark(V.tensor_tensor(tab(7, E0 + 1)[:, :, 0:E0], tab(4, E0), tab(5, E0), ALU.add))
                yield
                ch.need()
                yield from comb_parts(ch, r0, tab(7, E0 + 1), E0 + 1)
                assert ch.n == K0C, ch.n

            def route1(ch, r):
                yield from route_max(ch, r1, r, E1, E1)
                yield from route_top2(ch, r1, r, E1, E1)
                ch.mark(V.tensor_tensor(tab(3, E1), tab(3, E1), tab(6, E1), ALU.add))
                yield
                ch.need()
                dve.wait_ge(r1["exp"], r + 1)
                ex = tab(1, E1)
                V.tensor_reduce(rmx[:, 5, :], ex, AX_X, ALU.add)
                ch.mark(V.tensor_tensor(tab(4, E1), ex, tab(3, E1), ALU.mult))
                yield
                ch.need()
                ch.mark(V.reciprocal(rmx[:, 6, :], rmx[:, 5, :]))
                yield
                ch.need()
                ch.mark(V.tensor_tensor(tab(7, E1), tab(4, E1), over(rmx[:, 6, :], E1), ALU.mult))
                yield
                ch.need()
                yield from comb_parts(ch, r1, tab(7, E1), E1)
                assert ch.n == K1C, ch.n

            def all_of(steps):
                for _ in steps:
                    pass

            def add_out(g, n):
                dve.wait_ge(s_oT, n)
                V.tensor_tensor(group_of(g), group_of(g), t4(TB[:]), ALU.add).then_inc(s_xo, 1)

            def front0(m, r, g, p):
                ch = Chain(dve, r0["chain"], r * K0C)
                all_of(stats(ch, m, g, p))
                w0_low(0)
                norm_of(m, g, p)
                w0_low(1)
                split(m, p)
                routing = route0(ch, r)
                some(routing, 8)
                w0_low(2)
                all_of(routing)
                w0_low(3)
                dve.wait_ge(s_x1, 16)

            def norm_chain(s, n, count, done=0):
                if isinstance(n, int) and n == 1:
                    return Chain(dve, s["ln_of_1"], 0, done)
                return Chain(dve, s["ln"], 0 if isinstance(n, int) and n == 0 else (n - 1) * count, done)

            def layer_norms(n, p):
                yield from norms_head(n, p)
                yield
                yield from norms_rest(n, p)

            def norms_head(n, p):
                yield from variance(norm_chain(a0, n, 5), lambda j: tile_of(n, j), p)
                plus_eps(p).then_inc(a0["ve1"], 1)

            def norms_rest(n, p):
                ch = norm_chain(a0, n, 5, 2)
                dve.wait_ge(a0["rstd1"], n + 1)
                ch.mark(normed(lambda j: tile_of(n, j), p))
                yield
                ch.need()
                yield from variance(ch, lambda j: xn[:, p, j, :], p)
                plus_eps(p).then_inc(a0["ve2"], 1)
                yield
                dve.wait_ge(a0["rstd2"], n + 1)
                normed(lambda j: xn[:, p, j:j + 1, :], p).then_inc(a0["xn"], 1)

            def layer_norm(n, p):
                ch = norm_chain(a1, n, 2)
                yield from variance(ch, lambda j: tile_of(n, j), p)
                plus_eps(p).then_inc(a1["ve1"], 1)
                yield
                dve.wait_ge(a1["rstd1"], n + 1)
                normed(lambda j: tile_of(n, j), p).then_inc(a1["xn"], 1)

            def some(steps, n):
                for _ in range(n):
                    next(steps, None)

            def back0(m, r, g, p, nxt, to):
                kind, mn, rn, gn, pn = nxt or (None,) * 5
                if nxt:
                    ch = Chain(dve, ROUTE[kind]["chain"], rn * (K0C, K1C)[kind])
                    ahead = stats(ch, mn, gn, pn)
                    routing = (route0, route1)[kind](ch, rn)
                for k in range(N0):
                    M, n = rows(k), slot0(p, k)
                    S, U = work[0:M, 0, n, :], work[0:M, 1, n, :]
                    dve.wait_ge(s_silu, r * N0 + k + 1)
                    dve.wait_ge(s_up, r * N0 + k + 1)
                    V.tensor_tensor(S, S, UP[(p + k) % 2][0:M, :], ALU.mult).then_inc(s_t, 1)
                    if nxt:
                        if k == 0:
                            some(ahead, 1)
                        if k == 2:
                            norm_of(mn, gn, pn)
                        if k >= 6 + kind:
                            some(routing, 2)
                    if to == 0 and 6 <= k < N0 - 1:
                        some(norms, 1)
                    dve.wait_ge(s_cb, r * (PAIRS + 1) + min(k, PAIRS) + 1)
                    dve.wait_ge(s_t, r * N0 + k + 1)
                    if soon0(p, k) and not (isinstance(g, int) and g == 0 and k < 3):
                        dve.wait_ge(s_ul, r * N0 + k - 2)
                    V.tensor_tensor(U, S, CB2[(p + min(k, PAIRS)) % 2][0:M, :], ALU.mult).then_inc(s_u, 1)
                    if nxt and k == 0:
                        all_of(ahead)
                    if k == 2 and (not isinstance(g, int) or g > 0):
                        add_out(g - 1, m)
                    if nxt and k == 4:
                        split(mn, pn)
                    if nxt and k >= 5 + kind:
                        some(routing, 2 if kind == 0 else 3)
                    if nxt and k == 9:
                        all_of(routing)
                    if to == 0 and k == 0:
                        norms = in_turns(layer_norms(0, 0), layer_norms(1, 1))
                        dve.wait_ge(s_xo, m)
                    if to == 0:
                        some(norms, 1 if k < N0 - 1 else 2)

            def finish(m, r, g):
                add_out(g, m + 1)

            def back1(m, r, g, p, nxt, to):
                NA = len(HI_BY_ACT)
                ND = CH1 - NA
                seen_a = seen_d = 0
                if nxt:
                    ch = Chain(dve, r1["chain"], (r + 1) * K1C)
                    ahead = stats(ch, m + 1, g + 1, 1 - p)
                    routing = route1(ch, r + 1)
                for kk in range(N1):
                    e, c = divmod(kk, CH1)
                    he, h, l = work[:, 0, kk % RING, :], hi[:, kk % RING, :], lo[:, kk % RING, :]
                    dve.wait_ge(s1_he, r * N1 + kk + 1)
                    if c in HI_BY_ACT:
                        seen_a += 1
                        dve.wait_ge(s1_hiA, r * (E1 * NA) + seen_a)
                    else:
                        seen_d += 1
                        V.tensor_scalar(h, he, 1.0, None, ALU.mult).then_inc(s1_hiD, 1)
                        if nxt and 3 <= kk <= 7:
                            next(ahead, None)
                        if nxt and kk >= 17:
                            next(routing, None)
                        dve.wait_ge(s1_hiD, r * (E1 * ND) + seen_d)
                    V.tensor_tensor(l, he, h.bitcast(F32), ALU.subtract).then_inc(s1_lo, 1)
                    if c == 3 and e:
                        weigh(r, e - 1)
                    if kk == 1 and (not isinstance(g, int) or g > 0):
                        weigh(r - 1, E1 - 1)
                    if kk == 5 and (not isinstance(g, int) or g > 0):
                        add_out(g - 1, m)
                    if to == 1 and kk == 5:
                        norms = in_turns(layer_norm(0, 0), layer_norm(1, 1))
                        dve.wait_ge(s_xo, m + 1)
                    if to == 1 and 6 <= kk <= 8:
                        some(norms, 2)
                    if to == 1 and kk == 9:
                        all_of(norms)
                    if nxt and kk == 7:
                        all_of(ahead)
                    if nxt and kk == 9:
                        norm_of(m + 1, g + 1, 1 - p)
                    if nxt and kk == 13:
                        split(m + 1, 1 - p)
                    if nxt and 17 <= kk < 27:
                        next(routing, None)
                    if nxt and kk == 27:
                        all_of(routing)

            def finish1(m, r, g):
                weigh(r, E1 - 1)
                finish(m, r, g)

            def weigh(r, e):
                dve.wait_ge(s1_Y, r * E1 + e + 1)
                dve.wait_ge(s1_cb, r * E1 + e + 1)
                if e >= 3:
                    dve.wait_ge(s1_acc, r * (E1 - 1) + e - 2)
                dst = term[:, e % 2, :] if e else yT[:]
                b = SMALL_AT["b2"][0] + e
                V.scalar_tensor_tensor(dst, YB[e % 2][:], small[:, b:b + 1], comb_bc[:, e % 2, :], ALU.add,
                                       ALU.mult).then_inc(s1_term, 1)

            def first_norm(m, r, p):
                first = 0 if m == GROUPS else 1
                ch = Chain(dve, ROUTE[first]["chain"], r * (K0C, K1C)[first])
                yield from stats(ch, m, 0, p)
                yield
                norm_of(m, 0, p)

            def in_turns(*all_steps):
                left = list(all_steps)
                while left:
                    for steps in list(left):
                        if next(steps, all_steps) is all_steps:
                            left.remove(steps)
                        else:
                            yield

            def attn0():
                s = a0

                def maximum(ch, n, p, lsem, dsem):
                    dve.wait_ge(s[lsem], n + 1)
                    ch.mark(V.tensor_reduce(mx[:, 2 + p, :], t4(bank[p][:]), AX_X, ALU.max))
                    yield
                    ch.need()
                    V.tensor_scalar(mx[:, p, :], mx[:, 2 + p, :], -INV, None, ALU.mult).then_inc(s[dsem], 1)

                def weights(ch, n, p, esem, bysem, wsem):
                    dve.wait_ge(s[esem], n + 1)
                    ch.mark(V.reciprocal(rinv[:, p, :], rsum[:, p, :]))
                    yield
                    ch.need()
                    dve.wait_ge(s[bysem], n + 1)
                    for j in range(TILES):
                        cols = slice(j * D, (j + 1) * D)
                        last = V.scalar_tensor_tensor(work[:, p, 2, cols], work[:, p, 1, cols], rinv[:, p, j:j + 1],
                                                      bank[4 + p][:, cols], ALU.mult, ALU.mult)
                    last.then_inc(s[wsem], 1)

                def mix(n, p):
                    dve.wait_ge(s["pool"], n + 1)
                    V.tensor_tensor(attn[:, 1, p, :], bank[2 + p][:], attn[:, 0, 2 + p, :], ALU.mult)\
                        .then_inc(s["mixed"], 1)

                def update(ch, n, p):
                    dve.wait_ge(s["vc"], n + 1)
                    dve.wait_ge(s["pk"], n + 1)
                    ch.mark(V.tensor_tensor(term[:, p, :], bank[2 + p][:], comb_bc[:, p, :], ALU.mult))
                    yield
                    ch.need()
                    ch.mark(V.tensor_tensor(group_of(n), group_of(n), t4(term[:, p, :]), ALU.add))

                def step(n, p, second, norm):
                    one, two = Chain(dve, s["one"], n * 2), Chain(dve, s["two"], (n - 1) * 4)
                    norms = norms_rest(n + 1, 1 - p) if second and norm else iter(())
                    some(norms, 1)
                    if second:
                        mix(n - 1, 1 - p)
                    some(norms, 3)
                    if second:
                        all_of(maximum(two, n - 1, 1 - p, "l2", "d2"))
                    all_of(maximum(one, n, p, "l1", "d1"))
                    all_of(norms)
                    if not norm:
                        norm_of(GROUPS, 0, 0)
                    if second:
                        all_of(weights(two, n - 1, 1 - p, "e2", "mixt", "w2"))
                    all_of(weights(one, n, p, "e1", "qt", "wq"))
                    if norm:
                        first = isinstance(n, int) and n == GROUPS - 2
                        all_of(stats(Chain(dve, r0["chain"], GROUPS * K0C), GROUPS, 0, 0) if first else norms_head(n + 2, p))
                    else:
                        split(GROUPS, 0)
                    if second:
                        all_of(update(two, n - 1, 1 - p))
                        two.need()

                def finish(n, p):
                    two = Chain(dve, s["two"], n * 4)
                    routing = route0(Chain(dve, r0["chain"], GROUPS * K0C, 2), GROUPS)
                    mix(n, p)
                    some(routing, 4)
                    all_of(maximum(two, n, p, "l2", "d2"))
                    some(routing, 5)
                    all_of(weights(two, n, p, "e2", "mixt", "w2"))
                    all_of(routing)
                    all_of(update(two, n, p))
                    two.need()

                attn_groups(dve, step, finish)

            def attn1():
                s = a1

                def maximum(ch, n, p):
                    dve.wait_ge(s["s"], n + 1)
                    for b in (0, 1):
                        last = V.tensor_reduce(mx[:, 2 + p, 2 * b:2 * b + 2],
                                               bank[4 * b + p][:].rearrange("q (j t) -> q j t", j=2), AX_X, ALU.max)
                    ch.mark(last)
                    yield
                    ch.need()
                    V.tensor_scalar(mx[:, p, :], mx[:, 2 + p, :], -INV, None, ALU.mult).then_inc(s["nmax"], 1)

                def weights(ch, n, p):
                    dve.wait_ge(s["e"], n + 1)
                    ch.mark(V.reciprocal(rinv[:, p, :], rsum[:, p, :]))
                    yield
                    ch.need()
                    ch.mark(V.tensor_tensor(mx[:, 4 + p, :], rsum[:, p, :], rinv[:, p, :], ALU.mult))
                    yield
                    ch.need()
                    ch.mark(V.tensor_scalar(mx[:, 6 + p, :], mx[:, 4 + p, :], 1.0, 1.0 / SEQ, ALU.add, ALU.mult))
                    yield
                    ch.need()
                    for j in range(TILES):
                        cols = slice((j % 2) * SEQ, (j % 2 + 1) * SEQ)
                        last = V.tensor_scalar(work[:, p, 2 + j // 2, cols], work[:, p, j // 2, cols],
                                               rinv[:, p, j:j + 1], mx[:, 6 + p, j:j + 1], ALU.mult, ALU.subtract)
                    last.then_inc(s["a"], 1)

                def update(n, p):
                    dve.wait_ge(s["o"], n + 1)
                    V.tensor_tensor(group_of(n), group_of(n), t4(bank[p][:]), ALU.add).then_inc(s["two"], 1)

                def step(n, p, second, norm):
                    one = Chain(dve, s["one"], n * 4)
                    norms = first_norm(3 * GROUPS, GROUPS, 0)
                    if norm:
                        norms = layer_norm(n + 1, 1 - p) if second else iter(())
                    some(norms, 3)
                    all_of(maximum(one, n, p))
                    all_of(norms)
                    if second:
                        update(n - 1, 1 - p)
                    all_of(weights(one, n, p))
                    if not norm:
                        split(3 * GROUPS, 0)

                def finish(n, p):
                    routing = route1(Chain(dve, r1["chain"], GROUPS * K1C, 2), GROUPS)
                    some(routing, 2)
                    update(n, p)
                    all_of(routing)
                    dve.wait_ge(s["two"], n + 1)

                attn_groups(dve, step, finish)

            front0(0, 0, 0, 0)
            dve.wait_ge(s_small2, 16)
            dve.wait_ge(s_bhi, 1)
            low = brow[LO:, :, :].rearrange("p b d -> p (b d)")
            V.tensor_tensor(low, small[LO:64, B_ROWS:B_ROWS + 3 * D], low.bitcast(F32), ALU.subtract).then_inc(s_blo, 1)
            ffn_groups(dve, 0, 0, 0, back0, finish, to=0)
            dve.wait_ge(s_xo, 1 + GROUPS)
            attn0()
            ffn_groups(dve, 1, 0, 1, back0, finish, then=THEN_FFN1)
            dve.wait_ge(s_xo, 1 + 2 * GROUPS)
            ffn_groups(dve, 2, 1, 0, back1, finish1, to=1)
            dve.wait_ge(s_xo, 1 + 3 * GROUPS)
            attn1()
            ffn_groups(dve, 3, 1, 1, back1, finish1)


K0C, K1C = 18, 17


def kernel(**inputs):
    import numpy as np
    import concourse.bacc as bacc
    from concourse import mybir as mb
    from concourse.bass_utils import run_bass_kernel_spmd as run

    a = {k: np.asarray(v) for k, v in inputs.items()}

    def col(v):
        out = np.zeros((P, 1), np.float32)
        out[:v.shape[0], 0] = v
        return out

    def block_of(v, width):
        out = np.zeros((P, width), np.float32)
        out[:v.shape[0], :v.shape[1]] = v
        return out

    tok = np.arange(SEQ)
    mean_to = (tok[:, None] <= tok[None, :]) / (tok[None, :] + 1.0)
    tie = np.tile(np.arange(E0, 0, -1, dtype=np.float32), TILES)
    sel0 = np.zeros((64, PAIRS + 1, P), np.float32)
    sel1 = np.zeros((64, E1, P), np.float32)
    for base in (0, LO):
        for k in range(PAIRS):
            sel0[base + 2 * k, k, 0:F0] = 1
            sel0[base + 2 * k + 1, k, F0:P] = 1
        sel0[base + E0, PAIRS, :] = 1
        for e in range(E1):
            sel1[base + e, e, :] = 1

    wr2 = np.concatenate([a["L1_ffn_Wr2"].T, a["L1_ffn_br2"][None, :]], axis=0)
    parts = {
        "gate0": np.concatenate([a["L0_ffn_gate_w"].T, a["L0_ffn_shared_gate_w"].T], axis=1),
        "wr1": a["L1_ffn_Wr1"].T, "wr2": block_of(wr2, E1),
        "b1": a["L1_ffn_b1"].reshape(N1, P).T, "b2": a["L1_ffn_b2"].T, "br1": col(a["L1_ffn_br1"]),
        "gamma": col(a["L0_attn_gamma"]), "beta": col(a["L0_attn_beta"]),
        "bq": col(a["L0_attn_bq"]), "bk": col(a["L0_attn_bk"]),
        "wq": a["L0_attn_Wq"], "wqa": a["L0_attn_Wqa"], "wk": a["L0_attn_Wk"], "wka": a["L0_attn_Wka"],
        "wv": a["L0_attn_Wv"],
        "bqa_row": np.broadcast_to(a["L0_attn_bqa"], (P, D)),
        "bka_row": np.broadcast_to(a["L0_attn_bka"], (P, D)), "bv_row": np.broadcast_to(a["L0_attn_bv"], (P, D)),
        "wq1": a["L1_attn_Wq"].T, "wk1": a["L1_attn_Wk"].T,
        "bq1": col(a["L1_attn_bq"]), "bk1": col(a["L1_attn_bk"]),
        "ident": np.eye(P), "tri0": mean_to[0:P, :], "tri1": mean_to[P:SEQ, P:SEQ],
        "tie": np.broadcast_to(tie, (P, TILES * E0)),
    }
    small = np.concatenate([np.asarray(parts[n], np.float32) for n, _ in SMALL], axis=1)

    gu = a["L0_ffn_w_gate_up"]
    shared_down = np.zeros((len(SH_ROWS) * P, D), np.float32)
    shared_down[:SHARED] = a["L0_ffn_shared_w_down"].T
    w0 = np.concatenate([
        gu[:, :, :F0].transpose(1, 0, 2).reshape(D, -1), gu[:, :, F0:].transpose(1, 0, 2).reshape(D, -1),
        a["L0_ffn_w_down"].reshape(PAIRS, P, D).transpose(1, 0, 2).reshape(P, -1),
        a["L0_ffn_shared_w_gate"].T, a["L0_ffn_shared_w_up"].T,
        shared_down.reshape(-1, P, D).transpose(1, 0, 2).reshape(P, -1),
    ], axis=1)
    w1 = a["L1_ffn_W1"].transpose(2, 0, 1).reshape(D, -1)
    w2 = a["L1_ffn_W2"].transpose(0, 2, 1).reshape(E1 * CH1, P, D).transpose(1, 0, 2).reshape(P, -1)

    sel = np.concatenate([sel0, sel1], axis=1)
    arrays = {"x": a["L0_attn_hidden_states"], "small_all": small, "sel_of": sel, "w0_all": w0, "w1_all": w1, "w2_all": w2}
    arrays = {k: np.ascontiguousarray(v) for k, v in arrays.items()}
    nc = bacc.Bacc("TRN2", target_bir_lowering=False, num_devices=1)
    args = [nc.dram_tensor(n, v.shape, mb.dt.from_np(v.dtype), kind="ExternalInput").ap() for n, v in arrays.items()]
    args.append(nc.dram_tensor("out", arrays["x"].shape, F32, kind="ExternalOutput").ap())
    program(nc, *args)
    r = run(nc, [arrays], core_ids=[0])
    return r.results[0]["out"]
```
